# Optimizing a Trainium2 kernel written in Bass

```python
import numpy as np
import jax
import jax.numpy as jnp

def _softmax(x, axis=-1):
    return jax.nn.softmax(x, axis=axis)

def _gelu(x):
    return jax.nn.gelu(x, approximate=True)

def _silu(x):
    return jax.nn.silu(x)

def _sigmoid(x):
    return jax.nn.sigmoid(x)

def _layernorm(x, axis=-1, eps=1e-05):
    m = jnp.mean(x, axis=axis, keepdims=True)
    v = jnp.var(x, axis=axis, keepdims=True)
    return (x - m) / jnp.sqrt(v + eps)

def _scatter_add(tgt, idx, src, axis=0):
    return tgt.at[idx].add(src)

def _segment_sum(src, seg, n):
    return jax.ops.segment_sum(src, seg, n)
kernel_name = 'mk_gnn_ffn_d1_gnn_r32_015cac'

def setup_inputs(seed: int=0):
    np.random.seed(seed)
    _w = jnp.asarray

    def _rec_inputs():
        import jax
        import jax.numpy as jnp
        _gk = jax.random.key(seed)
        x = -8.776e-05 + 1 * jax.random.normal(jax.random.fold_in(_gk, 1), (10000, 512), jnp.float32)
        src = jax.random.randint(jax.random.fold_in(_gk, 2), (10000,), 0, 10000, jnp.int32)
        dst = jax.random.randint(jax.random.fold_in(_gk, 3), (10000,), 0, 10000, jnp.int32)
        _o = jnp.argsort(dst, stable=True)
        src = src[_o]
        dst = dst[_o]
        return (x, src, dst)
    x, src, dst = _rec_inputs()

    def _L0_gnn_setup():
        import jax, jax.numpy as jnp
        import numpy as np
        N = 10000
        E = 5000
        H = 4
        C = 256
        D_IN = 512
        D_OUT = 512
        NEG_SLOPE = 0.2

        def gat_conv(x, src, dst, W, a_src, a_dst, bias):
            n = x.shape[0]
            h = (x @ W).reshape(n, H, C)
            al_s = jnp.einsum('nhc,hc->nh', h, a_src)
            al_d = jnp.einsum('nhc,hc->nh', h, a_dst)
            e = jax.nn.leaky_relu(al_s[src] + al_d[dst], NEG_SLOPE)
            emax = jax.ops.segment_max(e, dst, num_segments=n)
            w = jnp.exp(e - emax[dst])
            denom = jax.ops.segment_sum(w, dst, num_segments=n)
            alpha = w / denom[dst]
            out = jax.ops.segment_sum(h[src] * alpha[:, :, None], dst, num_segments=n)
            return out.reshape(n, H * C) + bias
        key = jax.random.key(seed)
        ks = jax.random.split(key, 13)
        s = 0.05
        return {'x': jax.random.normal(ks[0], (N, D_IN), jnp.float32), 'edge_index': jax.random.randint(ks[1], (2, E), 0, N, dtype=jnp.int32), 'W1': jax.random.normal(ks[2], (D_IN, H * C), jnp.float32) * s, 'a_src1': jax.random.normal(ks[3], (H, C), jnp.float32) * s, 'a_dst1': jax.random.normal(ks[4], (H, C), jnp.float32) * s, 'b1': jnp.zeros((H * C,), jnp.float32), 'W2': jax.random.normal(ks[5], (H * C, H * C), jnp.float32) * s, 'a_src2': jax.random.normal(ks[6], (H, C), jnp.float32) * s, 'a_dst2': jax.random.normal(ks[7], (H, C), jnp.float32) * s, 'b2': jnp.zeros((H * C,), jnp.float32), 'Wfc': jax.random.normal(ks[8], (H * C, D_OUT), jnp.float32) * s, 'bfc': jnp.zeros((D_OUT,), jnp.float32)}
    _L0_gnn_all = _L0_gnn_setup()
    _L0_gnn_in = {k: v for k, v in _L0_gnn_all.items() if k in ('W1', 'a_src1', 'a_dst1', 'b1', 'W2', 'a_src2', 'a_dst2', 'b2', 'Wfc', 'bfc')}
    del _L0_gnn_all

    def _L0_ffn_setup():
        import jax, jax.numpy as jnp
        import numpy as np
        K = 2
        key = jax.random.key(seed)
        ks = jax.random.split(key, 6)
        B, T, d, E, dff = (2, 64, 512, 8, 64)
        x = jax.random.normal(ks[0], (B, T, d), dtype=jnp.float32)
        Wg = jax.random.normal(ks[1], (d, E), dtype=jnp.float32) * 0.02
        W1 = jax.random.normal(ks[2], (E, d, dff), dtype=jnp.float32) * 0.02
        b1 = jnp.zeros((E, dff), dtype=jnp.float32)
        W2 = jax.random.normal(ks[3], (E, dff, d), dtype=jnp.float32) * 0.02
        b2 = jnp.zeros((E, d), dtype=jnp.float32)
        return {'x': x, 'Wg': Wg, 'W1': W1, 'b1': b1, 'W2': W2, 'b2': b2}
    _L0_ffn_all = _L0_ffn_setup()
    _L0_ffn_in = {k: v for k, v in _L0_ffn_all.items() if k in ('Wg', 'W1', 'b1', 'W2', 'b2')}
    del _L0_ffn_all
    return {'x': x, 'src': src, 'dst': dst, 'L0_gnn_W1': _L0_gnn_in['W1'], 'L0_gnn_a_src1': _L0_gnn_in['a_src1'], 'L0_gnn_a_dst1': _L0_gnn_in['a_dst1'], 'L0_gnn_b1': _L0_gnn_in['b1'], 'L0_gnn_W2': _L0_gnn_in['W2'], 'L0_gnn_a_src2': _L0_gnn_in['a_src2'], 'L0_gnn_a_dst2': _L0_gnn_in['a_dst2'], 'L0_gnn_b2': _L0_gnn_in['b2'], 'L0_gnn_Wfc': _L0_gnn_in['Wfc'], 'L0_gnn_bfc': _L0_gnn_in['bfc'], 'L0_ffn_Wg': _L0_ffn_in['Wg'], 'L0_ffn_W1': _L0_ffn_in['W1'], 'L0_ffn_b1': _L0_ffn_in['b1'], 'L0_ffn_W2': _L0_ffn_in['W2'], 'L0_ffn_b2': _L0_ffn_in['b2']}

def reference(x, src, dst, L0_gnn_W1, L0_gnn_a_src1, L0_gnn_a_dst1, L0_gnn_b1, L0_gnn_W2, L0_gnn_a_src2, L0_gnn_a_dst2, L0_gnn_b2, L0_gnn_Wfc, L0_gnn_bfc, L0_ffn_Wg, L0_ffn_W1, L0_ffn_b1, L0_ffn_W2, L0_ffn_b2):
    import jax
    import jax.numpy as jnp

    def _L0_gnn_ref(x, edge_index, W1, a_src1, a_dst1, b1, W2, a_src2, a_dst2, b2, Wfc, bfc):
        import jax, jax.numpy as jnp
        import numpy as np
        N = 10000
        E = 5000
        H = 4
        C = 256
        D_IN = 512
        D_OUT = 512
        NEG_SLOPE = 0.2

        def gat_conv(x, src, dst, W, a_src, a_dst, bias):
            n = x.shape[0]
            h = (x @ W).reshape(n, H, C)
            al_s = jnp.einsum('nhc,hc->nh', h, a_src)
            al_d = jnp.einsum('nhc,hc->nh', h, a_dst)
            e = jax.nn.leaky_relu(al_s[src] + al_d[dst], NEG_SLOPE)
            emax = jax.ops.segment_max(e, dst, num_segments=n)
            w = jnp.exp(e - emax[dst])
            denom = jax.ops.segment_sum(w, dst, num_segments=n)
            alpha = w / denom[dst]
            out = jax.ops.segment_sum(h[src] * alpha[:, :, None], dst, num_segments=n)
            return out.reshape(n, H * C) + bias
        loop = jnp.arange(N, dtype=edge_index.dtype)
        src = jnp.concatenate([edge_index[0], loop])
        dst = jnp.concatenate([edge_index[1], loop])
        h = jax.nn.relu(gat_conv(x, src, dst, W1, a_src1, a_dst1, b1))
        h = jax.nn.relu(gat_conv(h, src, dst, W2, a_src2, a_dst2, b2))
        return h @ Wfc + bfc

    def _L0_ffn_ref(x, Wg, W1, b1, W2, b2):
        import jax, jax.numpy as jnp
        import numpy as np
        K = 2
        logits = jnp.einsum('btd,de->bte', x, Wg)
        probs = jax.nn.softmax(logits, axis=-1)
        top_p, _top_i = jax.lax.top_k(probs, K)
        top_p = top_p / jnp.sum(top_p, axis=-1, keepdims=True)
        b2_sum = jnp.sum(b2, axis=0)
        out = jnp.zeros_like(x)
        for i in range(K):
            w_in = x * top_p[..., i:i + 1]
            h = jax.nn.gelu(jnp.einsum('btd,edf->ebtf', w_in, W1) + b1[:, None, None, :], approximate=False)
            out = out + jnp.einsum('ebtf,efd->btd', h, W2) + b2_sum
        return out
    edge_index = jnp.stack([src, dst])
    x = x + _L0_gnn_ref(_layernorm(x, axis=-1), edge_index, L0_gnn_W1, L0_gnn_a_src1, L0_gnn_a_dst1, L0_gnn_b1, L0_gnn_W2, L0_gnn_a_src2, L0_gnn_a_dst2, L0_gnn_b2, L0_gnn_Wfc, L0_gnn_bfc)
    x = x + _L0_ffn_ref(_layernorm(x, axis=-1)[None], L0_ffn_Wg, L0_ffn_W1, L0_ffn_b1, L0_ffn_W2, L0_ffn_b2)[0]
    return x

_drawn_inputs = setup_inputs


def setup_inputs(seed=0):
    import zlib

    import numpy as np

    out = dict(_drawn_inputs(seed))
    spreads = {'L0_gnn_b1': (0.0, 0.1),
     'L0_gnn_b2': (0.0, 0.1),
     'L0_gnn_bfc': (0.0, 0.1),
     'L0_ffn_b1': (0.0, 0.267),
     'L0_ffn_b2': (0.0, 0.1)}
    factors = {'L0_gnn_a_dst2': 2.943, 'L0_ffn_Wg': 8.0}
    for name, (base, spread) in spreads.items():
        noise = np.random.default_rng([zlib.crc32(name.encode()), seed]).standard_normal(out[name].shape)
        drawn = base * np.exp(spread * noise) if base else spread * noise
        out[name] = jnp.asarray(drawn.astype(out[name].dtype))
    for name, factor in factors.items():
        out[name] = (out[name] * factor).astype(out[name].dtype)
    return out
```

```python
from contextlib import ExitStack, contextmanager

import concourse.bass as bass
from concourse import mybir

F32 = mybir.dt.float32
BF16 = mybir.dt.bfloat16
I32 = mybir.dt.int32
U32 = mybir.dt.uint32
ALU = mybir.AluOpType
ACT = mybir.ActivationFunctionType
AX = mybir.AxisListType
ds = bass.ds

P = 128
EPS = 1e-5
SLOPE = 0.2
BIG = 1e30
NODES = 125
HEADS = 4
OVMUL = 16384


class Tile:

    def __init__(self, t, h, u, T=None, TH=None, phase=0):
        self.t, self.h, self.u, self.T, self.TH, self.phase = t, h, u, T, TH, phase


class Count:
    n = 0


def first(tile_half, u):
    return Tile(t=tile_half * 2 + u, h=tile_half, u=u)


def after(s):
    return first(s.h, 1) if s.u == 0 else first(s.h + 1, 0)


def before(s):
    return first(s.h - 1, 1) if s.u == 0 else first(s.h, 0)


def last_but_one(s):
    return isinstance(s.t, int) and s.u == 0 and s.h > 0


def is_zero(t):
    return isinstance(t, int) and t == 0


def wait(eng, sem, value):
    if not isinstance(value, int) or value > 0:
        eng.wait_ge(sem, value)


def gnn_ffn_kernel(nc, x, src, dst, w1, as1, ad1, b1, w2, as2, ad2, b2, wfc, bfc, wg, f1, fb1, f2, fb2, out):
    N, D = x.shape
    E = src.shape[0]
    HC = w1.shape[1]
    C = HC // HEADS
    EX, _, DFF = f1.shape
    FF = EX * DFF
    TILES = N // NODES
    HALF = TILES // 2
    EC = E // NODES
    KD, KH, KF = D // P, HC // P, FF // P
    ROW = HC + 2 * HEADS
    MAIN = 2 * TILES
    SLOTS = MAIN + (E // P + 2)
    ROWS = TILES * P
    DUMMY = 1 << 20
    WC_LOADS = 16 * (EX + 6)
    assert N % NODES == 0 and E % NODES == 0 and TILES % 2 == 0 and SLOTS % 2 == 0

    table1 = nc.dram_tensor("table1", (ROWS, ROW), F32, kind="Internal").ap()
    table2 = nc.dram_tensor("table2", (ROWS, ROW), F32, kind="Internal").ap()
    slots_dram = nc.dram_tensor("slots", (P * SLOTS, 2), I32, kind="Internal").ap()

    ctx = ExitStack()
    with ctx:
        def sb(name, shape, dt=F32, to=ctx):
            return to.enter_context(nc.sbuf_tensor(name, shape, dt))

        def sem(name):
            return ctx.enter_context(nc.semaphore(name))

        bank = [ctx.enter_context(nc.psum_tensor(f"bank{i}", [P, 512], F32)) for i in range(8)]

        w2_sb = sb("w2_sb", [P, KH, HC])
        wfc_sb = sb("wfc_sb", [P, KH, D])
        f1_sb = sb("f1_sb", [P, KD, FF])
        f2_sb = sb("f2_sb", [P, KF, D])
        wg_sb = sb("wg_sb", [P, KD, EX])
        v2_sb = sb("v2_sb", [P, KH, 8])
        b1_bc = sb("b1_bc", [P, HC])
        b2_bc = sb("b2_bc", [P, HC])
        bfc_bc = sb("bfc_bc", [P, D])
        fb1_bc = sb("fb1_bc", [P, FF])
        fb2_sb = sb("fb2_sb", [EX, D])
        ones_ex = sb("ones_ex", [EX, P])
        fb2_twice = sb("fb2_twice", [P, D])
        ident = sb("ident", [P, P])
        iota_node = sb("iota_node", [P, P])
        slot_loc = sb("slot_loc", [P, SLOTS])
        slot_meta = sb("slot_meta", [P, SLOTS, 2], I32)
        ov_start = sb("ov_start", [1, TILES + 8], I32)

        early_space = ExitStack()
        w1_sb = sb("w1_sb", [P, KD, HC], to=early_space)
        v1_sb = sb("v1_sb", [P, KD, 8], to=early_space)
        a_bc = sb("a_bc", [P, 4, HC], to=early_space)
        fold_out = sb("fold_out", [P, C], to=early_space)
        xa = [sb(f"xa{u}", [P, D], to=early_space) for u in range(2)]
        xna = [sb(f"xna{u}", [P, D], to=early_space) for u in range(2)]
        xTa = [sb(f"xTa{u}", [P, KD, P], to=early_space) for u in range(2)]
        stat_a = sb("stat_a", [P, 10], to=early_space)
        rowa = [sb(f"rowa{u}", [P, ROW], to=early_space) for u in range(2)]
        pairs = sb("pairs", [P, EC, 2], I32, to=early_space)
        slot_idx = sb("slot_idx", [P, EC], I32, to=early_space)
        pair_st = sb("pair_st", [P, 4, 2], I32, to=early_space)
        idx_st = sb("idx_st", [P, 4], I32, to=early_space)
        fill = sb("fill", [P, SLOTS, 2], I32, to=early_space)
        place = ExitStack()
        dst_i = sb("dst_i", [P, EC], I32, to=place)
        src_i = sb("src_i", [P, EC], I32, to=place)
        ef = sb("ef", [P, 10, EC], to=place)
        ei = sb("ei", [P, 4, EC], I32, to=place)
        onehot_t = sb("onehot_t", [P, EC, TILES], BF16, to=place)
        same = sb("same", [P, EC, EC], BF16, to=place)
        earlier = sb("earlier", [P, EC, EC], BF16, to=place)
        iota_tile = sb("iota_tile", [P, TILES], to=place)
        tri = sb("tri", [P, P], to=place)
        ones = sb("ones", [P, P], to=place)
        count_pt = sb("count_pt", [P, TILES], to=place)
        scan = sb("scan", [P, 2, TILES], to=place)
        ov_i = sb("ov_i", [P, 2, TILES], I32, to=place)
        lookup = same
        base_t = sb("base_t", [P, 3, TILES], to=place)
        place.close()
        early_space.close()

        G = [sb(f"G{u}", [P, 2, ROW]) for u in range(2)]
        H = [sb(f"H{u}", [P, ROW]) for u in range(2)]
        GO = sb("GO", [P, ROW])
        gidx = [sb(f"gidx{u}", [P, 2], I32) for u in range(2)]
        goidx = sb("goidx", [P, 1], I32)
        OH = sb("OH", [P, 2, P])
        NM = sb("NM", [P, 2, P])
        AM = sb("AM", [P, 2, HEADS, P])
        OHo = sb("OHo", [P, P])
        NMo = sb("NMo", [P, P])
        AMo = sb("AMo", [P, HEADS, P])
        ohTo = sb("ohTo", [P, P])
        So = sb("So", [P, HEADS, P])
        S = sb("S", [P, 2, HEADS, P])
        ohT = sb("ohT", [P, 2, P])
        small_f = sb("small_f", [P, 106])
        mx2 = sb("mx2", [P, 2, HEADS])
        mixed = sb("mixed", [P, HC])
        hT = sb("hT", [P, KH, P])
        rowb = [sb(f"rowb{u}", [P, ROW]) for u in range(2)]
        xc = [sb(f"xc{u}", [P, D]) for u in range(2)]
        x2 = [sb(f"x2_{u}", [P, D]) for u in range(2)]
        xn2 = sb("xn2", [P, D])
        xT2 = sb("xT2", [P, KD, P])
        ffn_v = sb("ffn_v", [P, 2, FF])
        gsum = sb("gsum", [P, FF])
        gT = sb("gT", [P, KF, P])
        outb = [sb(f"outb{u}", [P, D]) for u in range(2)]

        mx, mxo = small_f[:, 0:4], small_f[:, 4:8]
        lsum, rhs8 = small_f[:, 8:12], small_f[:, 12:20]
        selfz, wself = small_f[:, 20:24], small_f[:, 24:28]
        z = small_f[:, 28:36].rearrange("p (c h) -> p c h", c=2)
        w = small_f[:, 36:44].rearrange("p (c h) -> p c h", c=2)
        zo, wo = small_f[:, 44:48], small_f[:, 48:52]
        dsum, rden, wsn = small_f[:, 52:56], small_f[:, 56:60], small_f[:, 60:64]
        stat_c = small_f[:, 96:106]
        m8, nmax, e8, esum = small_f[:, 73:81], small_f[:, 81:82], small_f[:, 82:90], small_f[:, 90:91]
        rsum, s2, p2 = small_f[:, 91:92], small_f[:, 92:93], small_f[:, 94:96]

        small = bank[2]
        ohT_ps = small[:, 0:256].rearrange("p (c e) -> p c e", c=2)
        edge_ps = small[:, 256:272].rearrange("p (c k) -> p c k", c=2)
        den_ps, den_o_ps, edge_o_ps, gate_ps = small[:, 272:276], small[:, 280:284], small[:, 288:296], small[:, 304:312]
        ohT_o_ps = small[:, 384:512]

        w1_in, edges_in, w2_in, wc_in = sem("w1_in"), sem("edges_in"), sem("w2_in"), sem("wc_in")
        consts = sem("consts")
        fold1, fold2 = sem("fold1"), sem("fold2")
        fb2_sum = sem("fb2_sum")
        placing, count_done, pl_base, filled, staged, scattered, meta_in, meta_ready = (
            sem("placing"), sem("count_done"), sem("pl_base"), sem("filled"), sem("staged"),
            [sem(f"scattered{i}") for i in range(4)], sem("meta_in"), sem("meta_ready"))
        placed, ov_ready, c_const = sem("placed"), sem("ov_ready"), sem("c_const")
        xa_in = [sem(f"xa_in{u}") for u in range(2)]
        stored1 = [sem(f"stored1_{u}") for u in range(2)]
        a_stats, xna_ready, xa_turned, xTa_copied, h1_done, h1_lo, h1_hi = (
            sem(n) for n in ("a_stats", "xna_ready", "xa_turned", "xTa_copied", "h1_done", "h1_lo", "h1_hi"))
        self_in = [sem(f"self_in{u}") for u in range(2)]
        gathered = [[sem(f"gathered{u}{c}") for c in range(2)] for u in range(2)]
        cleared = sem("cleared")
        (index_staged, onehot, nomatch, masked, maskedT, onehotT, onehotT_copied, edge_max, node_max, lgt_sum,
         shift_ready, self_logit, self_weight, edge_rhs, edge_logit, edge_weight, scatter_ready, aggregated, den_done,
         den_total, den_inv, self_scale, self_scaled, mix_done, mixedT, relu_done) = (sem(n) for n in (
             "index_staged", "onehot", "nomatch", "masked", "maskedT", "onehotT", "onehotT_copied", "edge_max",
             "node_max", "lgt_sum", "shift_ready", "self_logit", "self_weight", "edge_rhs", "edge_logit",
             "edge_weight", "scatter_ready", "aggregated", "den_done", "den_total", "den_inv", "self_scale",
             "self_scaled", "mix_done", "mixedT", "relu_done"))
        (ov_staged, ov_in, ov1_masked, ov1_dve, ov1_T, ov1_max, ov2_onehot, ov2_T, ov2_copied, ov2_rhs, ov2_logit,
         ov2_weight, ov2_scatter, ov2_agg, ov2_den) = (sem(n) for n in (
             "ov_staged", "ov_in", "ov1_masked", "ov1_dve", "ov1_T", "ov1_max", "ov2_onehot", "ov2_T", "ov2_copied",
             "ov2_rhs", "ov2_logit", "ov2_weight", "ov2_scatter", "ov2_agg", "ov2_den"))
        dense_done, h2_lo, h2_hi = sem("dense_done"), sem("h2_lo"), sem("h2_hi")
        stored2 = [sem(f"stored2_{u}") for u in range(2)]
        xc_in = [sem(f"xc_in{u}") for u in range(2)]
        out_stored = [sem(f"out_stored{u}") for u in range(2)]
        (fc_done, c_x2, c_stats, c_xn, c_xT, c_xTc, gate_done, f1_done, c_top, c_exp, c_prob, ffn_in, gelu_done,
         gsum_done, c_gT, gT_copied, f2_done, out_sum) = (sem(n) for n in (
             "fc_done", "c_x2", "c_stats", "c_xn", "c_xT", "c_xTc", "gate_done", "f1_done", "c_top", "c_exp",
             "c_prob", "ffn_in", "gelu_done", "gsum_done", "c_gT", "gT_copied", "f2_done", "out_sum"))

        def phase_tile(s, phase):
            return Tile(t=s.t, h=s.h, u=s.u, T=s.t + TILES * phase, TH=s.h + HALF * phase, phase=phase)

        def early(eng, value):
            return value if isinstance(value, int) else eng.snap(eng.to_reg(value))

        def alone(eng, sem, value):
            eng.wait_ge(consts, 1)
            eng.wait_ge(sem, value)

        def overflow(eng, s, total):
            a = eng.value_load(ov_start[0:1, ds(s.t, 1)], min_val=0, max_val=SLOTS - MAIN)
            b = eng.value_load(ov_start[0:1, ds(s.t + 1, 1)], min_val=0, max_val=SLOTS - MAIN)
            return a, b, (total if s.phase else 0)

        @contextmanager
        def each(eng, a, b):
            with eng.If(a < b):
                with eng.Fori(a, b) as g:
                    yield g

        def over_tiles(eng, body):
            body(first(0, 0), True)
            body(first(0, 1), True)
            with eng.Fori(1, HALF - 1) as it:
                body(first(it, 0), True)
                body(first(it, 1), True)
            body(first(HALF - 1, 0), True)
            body(first(HALF - 1, 1), False)

        with nc.Block() as block:
            @block.sync
            def _(sp):
                sp.dma_start(dst_i[0:NODES, :], dst.rearrange("(p c) -> p c", c=EC)).then_inc(edges_in, 16)
                sp.dma_start(src_i[0:NODES, :], src.rearrange("(p c) -> p c", c=EC)).then_inc(edges_in, 16)
                sp.wait_ge(consts, 1)
                for u in range(2):
                    sp.dma_start(xa[u][0:NODES, :], x[u * NODES:(u + 1) * NODES, :]).then_inc(xa_in[u], 16)
                sp.dma_start(w1_sb[:, :, :], w1.rearrange("(k p) n -> p k n", p=P)).then_inc(w1_in, 16)
                for i, a in enumerate((as1, ad1, as2, ad2)):
                    sp.dma_start(a_bc[:, i, :], a.rearrange("h c -> (h c)").partition_broadcast(P)).then_inc(w1_in, 16)
                sp.dma_start(w2_sb[:, :, :], w2.rearrange("(k p) n -> p k n", p=P)).then_inc(w2_in, 16)
                for to, of in ((b1_bc, b1), (b2_bc, b2)):
                    sp.dma_start(to[:, :], of.partition_broadcast(P)).then_inc(w2_in, 16)
                sp.dma_start(wfc_sb[:, :, :], wfc.rearrange("(k p) n -> p k n", p=P)).then_inc(wc_in, 16)
                for e in range(EX):
                    sp.dma_start(f1_sb[:, :, e * DFF:(e + 1) * DFF],
                                 f1[e].rearrange("(k p) f -> p k f", p=P)).then_inc(wc_in, 16)
                sp.dma_start(f2_sb[:, :, :],
                             f2.rearrange("e f d -> (e f) d").rearrange("(k p) d -> p k d", p=P)).then_inc(wc_in, 16)
                sp.dma_start(wg_sb[:, :, :], wg.rearrange("(k p) e -> p k e", p=P)).then_inc(wc_in, 16)
                sp.dma_start(fb2_sb[:, :], fb2).then_inc(wc_in, 16)
                sp.dma_start(bfc_bc[:, :], bfc.partition_broadcast(P)).then_inc(wc_in, 16)
                sp.dma_start(fb1_bc[:, :], fb1.rearrange("e f -> (e f)").partition_broadcast(P)).then_inc(wc_in, 16)

                def a_io(s, more):
                    if more is not None:
                        sp.wait_ge(xna_ready, s.t + 1)
                        n = s.t + 2
                        sp.dma_start(xa[s.u][0:NODES, :], x[ds(n * NODES, NODES), :]).then_inc(xa_in[s.u], 16)
                    sp.wait_ge(h1_lo, s.t + 1)
                    sp.wait_ge(h1_hi, 2 * s.t + 2)
                    sp.dma_start(table1[ds(s.t * P, P), :], rowa[s.u][:, :]).then_inc(stored1[s.u], 16)

                with sp.Fori(0, HALF - 1) as it:
                    a_io(first(it, 0), True)
                    a_io(first(it, 1), True)
                a_io(first(HALF - 1, 0), None)
                a_io(first(HALF - 1, 1), None)

                for i in range(4):
                    sp.wait_ge(scattered[i], 16 * (EC // 4))
                sp.dma_start(slot_meta[:, :, :], slots_dram.rearrange("(p c) k -> p c k", p=P)).then_inc(meta_in, 16)
                sp.wait_ge(cleared, 1)
                for u in range(2):
                    sp.wait_ge(stored1[u], 16 * HALF)

                def self_load(s, table):
                    sp.dma_start(H[s.u][:, :], table[ds(s.t * P, P), :]).then_inc(self_in[s.u], 16)

                def b_io(s, more):
                    if more is not None:
                        sp.wait_ge(self_scaled, 4 * (s.t + 1))
                        self_load(Tile(s.t + 2, s.h + 1, s.u), table1)
                    sp.wait_ge(h2_lo, s.t + 1)
                    sp.wait_ge(h2_hi, 2 * s.t + 2)
                    sp.dma_start(table2[ds(s.t * P, P), :], rowb[s.u][:, :]).then_inc(stored2[s.u], 16)

                self_load(first(0, 0), table1)
                self_load(first(0, 1), table1)
                with sp.Fori(0, HALF - 1) as it:
                    b_io(first(it, 0), True)
                    b_io(first(it, 1), True)
                b_io(first(HALF - 1, 0), None)
                b_io(first(HALF - 1, 1), None)

                sp.wait_ge(self_scaled, 4 * TILES)
                for u in range(2):
                    sp.wait_ge(stored2[u], 16 * HALF)

                def x_load(s):
                    sp.dma_start(xc[s.u][0:NODES, :], x[ds(s.t * NODES, NODES), :]).then_inc(xc_in[s.u], 16)

                def c_io(s, more):
                    if more is not None:
                        n = Tile(s.t + 2, s.h + 1, s.u)
                        sp.wait_ge(self_scaled, 4 * (s.t + TILES + 1))
                        self_load(n, table2)
                        sp.wait_ge(c_x2, 2 * s.t + 2)
                        x_load(n)
                    sp.wait_ge(out_sum, 2 * s.t + 2)
                    sp.dma_start(out[ds(s.t * NODES, NODES), :], outb[s.u][0:NODES, :]).then_inc(out_stored[s.u], 16)

                for u in range(2):
                    self_load(first(0, u), table2)
                    x_load(first(0, u))
                with sp.Fori(0, HALF - 1) as it:
                    c_io(first(it, 0), True)
                    c_io(first(it, 1), True)
                c_io(first(HALF - 1, 0), None)
                c_io(first(HALF - 1, 1), None)
                for u in range(2):
                    sp.wait_ge(out_stored[u], 16 * HALF)

            @block.gpsimd
            def _(pool):
                for u in range(2):
                    pool.memset(xa[u][:, :], 0.0)
                pool.memset(ones_ex[:, :], 1.0)
                pool.memset(fill[:, :, 0:1], DUMMY)
                pool.memset(fill[:, :, 1:2], -1).then_inc(consts, 1)
                pool.iota(iota_node[:, :], [[1, P]], base=0, channel_multiplier=0,
                          allow_small_or_imprecise_dtypes=True)
                pool.iota(iota_tile[:, :], [[1, TILES]], base=0, channel_multiplier=0,
                          allow_small_or_imprecise_dtypes=True)
                pool.memset(ident[:, :], 0.0)
                pool.memset(tri[:, :], 1.0)
                pool.memset(earlier[:, :, :], 1.0)
                pool.memset(ones[:, :], 1.0).then_inc(consts, 1)
                pool.wait_ge(consts, 2)
                pool.affine_select(out=ident[:, :], in_=ident[:, :], pattern=[[-1, P]], compare_op=ALU.not_equal,
                                   fill=1.0, base=0, channel_multiplier=1)
                pool.affine_select(out=tri[:, :], in_=tri[:, :], pattern=[[1, P]], compare_op=ALU.is_gt,
                                   fill=0.0, base=0, channel_multiplier=-1)
                pool.affine_select(out=earlier[:, :, :], in_=earlier[:, :, :], pattern=[[1, EC], [-1, EC]],
                                   compare_op=ALU.is_gt, fill=0.0, base=0, channel_multiplier=0).then_inc(consts, 1)
                pool.dma_start(slots_dram.rearrange("(p c) k -> p c k", p=P), fill[:, :, :]).then_inc(filled, 16)

                pool.wait_ge(placed, 2)
                pool.wait_ge(filled, 16)
                def scatter(it):
                    for i in range(4):
                        wait(pool, scattered[i], 16 * it)
                    counted = early(pool, 2 * it + 2)
                    pool.tensor_copy(pair_st[0:NODES, :, :], pairs[0:NODES, ds(4 * it, 4), :]).then_inc(staged, 1)
                    pool.tensor_copy(idx_st[0:NODES, :], slot_idx[0:NODES, ds(4 * it, 4)]).then_inc(staged, 1)
                    alone(pool, staged, counted)
                    for i in range(4):
                        pool.indirect_dma_start(
                            out=slots_dram, out_offset=bass.IndirectOffsetOnAxis(ap=idx_st[0:NODES, i:i + 1], axis=0),
                            in_=pair_st[0:NODES, i, :], in_offset=None).then_inc(scattered[i], 16)

                scatter(0)
                with pool.Fori(1, EC // 4) as it:
                    scatter(it)

                for i in range(4):
                    pool.wait_ge(scattered[i], 16 * (EC // 4))
                pool.wait_ge(fold2, KH * 8)
                pool.wait_ge(h1_done, TILES)
                for u in range(2):
                    pool.wait_ge(stored1[u], 16 * HALF)
                for u in range(2):
                    pool.memset(G[u][:, :, :], 0.0)
                    pool.memset(xc[u][:, :], 0.0)
                pool.memset(GO[:, :], 0.0).then_inc(cleared, 1)
                pool.wait_ge(cleared, 1)
                pool.wait_ge(ov_ready, 1)
                pool.wait_ge(meta_in, 16)
                total = pool.snap(pool.value_load(ov_start[0:1, TILES:TILES + 1], min_val=0, max_val=SLOTS - MAIN))

                pool.sem_inc(ov1_masked, 1)
                pool.sem_inc(ov2_agg, 1)

                def gather(s, table):
                    counted = early(pool, s.T + 1)
                    pool.tensor_copy(gidx[s.u][:, :], slot_meta[:, ds(2 * s.t, 2), 0]).then_inc(index_staged, 1)
                    alone(pool, index_staged, counted)
                    for c in range(2):
                        pool.indirect_dma_start(
                            out=G[s.u][:, c, :], out_offset=None, in_=table,
                            in_offset=bass.IndirectOffsetOnAxis(ap=gidx[s.u][:, c:c + 1], axis=0),
                            bounds_check=ROWS - 1, oob_is_err=False).then_inc(gathered[s.u][c], 16)

                def gather_overflow(s, table):
                    a, b, off = overflow(pool, s, total)

                    def one(g, nth):
                        counted = early(pool, nth + 1)
                        pool.tensor_copy(goidx[:, :], slot_meta[:, ds(g + MAIN, 1), 0]).then_inc(ov_staged, 1)
                        alone(pool, ov_staged, counted)
                        pool.indirect_dma_start(
                            out=GO[:, :], out_offset=None, in_=table,
                            in_offset=bass.IndirectOffsetOnAxis(ap=goidx[:, 0:1], axis=0),
                            bounds_check=ROWS - 1, oob_is_err=False).then_inc(ov_in, 16)

                    with each(pool, a, b) as g:
                        alone(pool, ov2_agg, a + off + 1)
                        pool.wait_ge(ov1_masked, g + off + 1)
                        one(g, a + g + off * 2)
                    with each(pool, a, b) as g:
                        alone(pool, ov1_masked, b + off + 1)
                        pool.wait_ge(ov2_agg, g + off + 1)
                        one(g, b + g + off * 2)

                for phase, table, stored in ((0, table1, stored1), (1, table2, stored2)):
                    for u in range(2):
                        pool.wait_ge(stored[u], 16 * HALF)
                    if phase:
                        pool.wait_ge(aggregated, TILES)
                    for u in range(2):
                        gather(phase_tile(first(0, u), phase), table)

                    def body(s, more):
                        s = phase_tile(s, phase)
                        gather_overflow(s, table)
                        if more:
                            pool.wait_ge(aggregated, s.T + 1)
                            gather(phase_tile(Tile(s.t + 2, s.h + 1, s.u), phase), table)

                    with pool.Fori(0, HALF - 1) as it:
                        body(first(it, 0), True)
                        body(first(it, 1), True)
                    body(first(HALF - 1, 0), False)
                    body(first(HALF - 1, 1), False)

            @block.tensor
            def _(pe):
                pe.wait_ge(consts, 3)
                pe.wait_ge(count_done, 1)
                pe.matmul(bank[7][:, 0:TILES], tri[0:NODES, :], count_pt[0:NODES, :], start=True, stop=True)
                pe.matmul(bank[7][:, 128:128 + TILES], ones[0:NODES, :], count_pt[0:NODES, :],
                          start=True, stop=True).then_inc(pl_base, 1)
                pe.wait_ge(fold1, KD * 8)
                pe.wait_ge(w1_in, 16 * 5)

                def turn(s):
                    pe.wait_ge(xna_ready, s.t + 1)
                    wait(pe, xTa_copied, s.t - 1)
                    for k in range(KD):
                        ins = pe.transpose(bank[s.u][:, k * P:(k + 1) * P], xna[s.u][:, k * P:(k + 1) * P], ident[:, :])
                    ins.then_inc(xa_turned, 1)

                def product(s):
                    pe.wait_ge(xTa_copied, s.t + 1)
                    wait(pe, h1_lo, s.t - 1)
                    wait(pe, h1_hi, 2 * s.t - 2)
                    for k in range(KD):
                        lhs = xTa[s.u][:, k, :]
                        for half in range(2):
                            pe.matmul(bank[2 + 2 * s.u + half][:, :], lhs, w1_sb[:, k, half * 512:(half + 1) * 512],
                                      start=(k == 0), stop=(k == KD - 1))
                        ins = pe.matmul(bank[6 + s.u][:, 256:264], lhs, v1_sb[:, k, :], start=(k == 0),
                                        stop=(k == KD - 1))
                    ins.then_inc(h1_done, 1)

                pe.wait_ge(placed, 1)
                turn(first(0, 0))

                def a_body(s, more):
                    if more:
                        turn(after(s))
                    product(s)

                over_tiles(pe, a_body)

                def turn_masked(s):
                    pe.wait_ge(masked, s.T + 1)
                    wait(pe, relu_done, 2 * s.T)
                    for c in range(2):
                        for h in range(HEADS):
                            ins = pe.transpose(bank[c][:, h * P:(h + 1) * P], AM[:, c, h, :], ident[:, :])
                    ins.then_inc(maskedT, 1)
                    for c in range(2):
                        ins = pe.transpose(ohT_ps[:, c, :], OH[:, c, :], ident[:, :])
                    ins.then_inc(onehotT, 1)
                    a, b, off = overflow(pe, s, total)
                    with each(pe, a, b) as g:
                        pe.wait_ge(ov1_masked, g + off + 2)
                        for h in range(HEADS):
                            ins = pe.transpose(bank[0][:, h * P:(h + 1) * P], AMo[:, h, :], ident[:, :])
                        ins.then_inc(ov1_T, 1)

                def target_values(s):
                    pe.wait_ge(shift_ready, 2 * s.T + 2)
                    pe.wait_ge(onehotT_copied, s.T + 1)
                    for c in range(2):
                        ins = pe.matmul(edge_ps[:, c, :], ohT[:, c, :], rhs8, start=True, stop=True)
                    ins.then_inc(edge_rhs, 1)

                def aggregate(s):
                    pe.wait_ge(scatter_ready, s.T + 1)
                    for c in range(2):
                        for h in range(HEADS):
                            ins = pe.matmul(bank[3 + h // 2][:, (h % 2) * C:(h % 2 + 1) * C], S[:, c, h, :],
                                            G[s.u][:, c, h * C:(h + 1) * C], start=(c == 0 and h % 2 == 0),
                                            stop=True, skip_group_check=True)
                    ins.then_inc(aggregated, 1)
                    for c in range(2):
                        ins = pe.matmul(den_ps, OH[:, c, :], w[:, c, :], start=(c == 0), stop=(c == 1))
                    ins.then_inc(den_done, 1)
                    a, b, off = overflow(pe, s, total)
                    with each(pe, a, b) as g:
                        pe.wait_ge(ov2_onehot, g + off + 1)
                        pe.transpose(ohT_o_ps, OHo[:, :], ident[:, :]).then_inc(ov2_T, 1)
                        pe.wait_ge(ov2_copied, g + off + 1)
                        pe.matmul(edge_o_ps, ohTo[:, :], rhs8, start=True, stop=True).then_inc(ov2_rhs, 1)
                        pe.wait_ge(ov2_scatter, g + off + 1)
                        for h in range(HEADS):
                            pe.matmul(bank[3 + h // 2][:, (h % 2) * C:(h % 2 + 1) * C], So[:, h, :],
                                      GO[:, h * C:(h + 1) * C], start=False, stop=True, skip_group_check=True)
                        pe.matmul(den_o_ps, OHo[:, :], wo, start=True, stop=True).then_inc(ov2_agg, 1)

                def turn_mixed(s):
                    for half in range(2):
                        pe.wait_ge(mix_done, 4 * s.T + 2 + 2 * half)
                        for k in range(4):
                            c = 4 * half + k
                            ins = pe.transpose(bank[half][:, k * P:(k + 1) * P], mixed[:, c * P:(c + 1) * P], ident[:, :])
                        ins.then_inc(mixedT, 1)

                def dense(s, ks):
                    if ks[0] == 0:
                        pe.wait_ge(relu_done, 2 * s.T + 2)
                        wait(pe, h2_lo, s.T)
                        wait(pe, h2_hi, 2 * s.T)
                    for k in ks:
                        for half in range(2):
                            pe.matmul(bank[5 + half][:, :], hT[:, k, :], w2_sb[:, k, half * 512:(half + 1) * 512],
                                      start=(k == 0), stop=(k == KH - 1), skip_group_check=True)
                        ins = pe.matmul(bank[7][:, 0:8], hT[:, k, :], v2_sb[:, k, :], start=(k == 0),
                                        stop=(k == KH - 1), skip_group_check=True)
                    if ks[-1] == KH - 1:
                        ins.then_inc(dense_done, 1)

                def prepare(s):
                    turn_masked(s)
                    target_values(s)
                    aggregate(s)
                    turn_mixed(s)

                pe.wait_ge(h1_lo, TILES)
                pe.wait_ge(h1_hi, 2 * TILES)
                pe.wait_ge(ov_ready, 1)
                pe.wait_ge(w2_in, 16 * 3)
                pe.wait_ge(fold2, KH * 8)
                total = pe.snap(pe.value_load(ov_start[0:1, TILES:TILES + 1], min_val=0, max_val=SLOTS - MAIN))
                prepare(phase_tile(first(0, 0), 0))

                def b_body(s, more):
                    n = phase_tile(after(s), 0)
                    s = phase_tile(s, 0)
                    if more:
                        turn_masked(n)
                    dense(s, range(0, 3))
                    if more:
                        target_values(n)
                    dense(s, range(3, 5))
                    if more:
                        aggregate(n)
                    dense(s, range(5, KH))
                    if more:
                        turn_mixed(n)

                over_tiles(pe, b_body)

                pe.wait_ge(h2_lo, TILES)
                pe.wait_ge(h2_hi, 2 * TILES)
                pe.wait_ge(wc_in, WC_LOADS)
                pe.matmul(bank[7][:, :], ones_ex[:, :], fb2_sb[:, :], start=True, stop=True).then_inc(fb2_sum, 1)
                prepare(phase_tile(first(0, 0), 1))

                def ffn_out(s):
                    pe.wait_ge(gT_copied, s.t + 1)
                    wait(pe, out_sum, 2 * s.t)
                    for k in range(KF):
                        ins = pe.matmul(bank[7][:, :], gT[:, k, :], f2_sb[:, k, :], start=(k == 0), stop=(k == KF - 1))
                    ins.then_inc(f2_done, 1)

                def c_body(s, more):
                    n = phase_tile(after(s), 1)
                    s = phase_tile(s, 1)
                    if more:
                        turn_masked(n)
                    pe.wait_ge(relu_done, 2 * s.T + 2)
                    wait(pe, gT_copied, s.t)
                    for k in range(KH):
                        ins = pe.matmul(bank[5][:, :], hT[:, k, :], wfc_sb[:, k, :], start=(k == 0), stop=(k == KH - 1))
                    ins.then_inc(fc_done, 1)
                    if more:
                        target_values(n)
                    if not is_zero(s.t):
                        ffn_out(before(s))
                    pe.wait_ge(c_xn, s.t + 1)
                    for k in range(KD):
                        ins = pe.transpose(bank[5][:, k * P:(k + 1) * P], xn2[:, k * P:(k + 1) * P], ident[:, :])
                    ins.then_inc(c_xT, 1)
                    if more:
                        pe.wait_ge(edge_logit, 4 * n.T + 3)
                    pe.wait_ge(c_xTc, s.t + 1)
                    for k in range(KD):
                        ins = pe.matmul(gate_ps, xT2[:, k, :], wg_sb[:, k, :], start=(k == 0), stop=(k == KD - 1))
                    ins.then_inc(gate_done, 1)
                    for k in range(KD):
                        ins = pe.matmul(bank[6][:, :], xT2[:, k, :], f1_sb[:, k, :], start=(k == 0), stop=(k == KD - 1))
                    ins.then_inc(f1_done, 1)
                    if more:
                        pe.wait_ge(c_top, 2 * s.t + 1)
                        aggregate(n)
                    pe.wait_ge(gsum_done, s.t + 1)
                    for k in range(KF):
                        ins = pe.transpose(bank[5][:, k * P:(k + 1) * P], gsum[:, k * P:(k + 1) * P], ident[:, :])
                    ins.then_inc(c_gT, 1)
                    if more:
                        turn_mixed(n)

                over_tiles(pe, c_body)
                ffn_out(first(HALF - 1, 1))

            @block.vector
            def _(v):
                pl = Count()

                def step(ins):
                    ins.then_inc(placing, 1)
                    pl.n += 1

                def settle():
                    v.wait_ge(placing, pl.n)

                e = lambda i: ef[0:NODES, i, :]
                n_ = NODES
                v.wait_ge(consts, 3)
                v.wait_ge(edges_in, 32)
                step(v.tensor_copy(e(0), dst_i[0:n_, :]))
                step(v.tensor_copy(e(1), src_i[0:n_, :]))
                settle()

                def split(node, tile, rest, tmp_i):
                    step(v.tensor_scalar(tmp_i, node, 1.0 / NODES, None, ALU.mult))
                    settle()
                    step(v.tensor_copy(tile, tmp_i))
                    settle()
                    step(v.scalar_tensor_tensor(rest, tile, -float(NODES), node, ALU.mult, ALU.add))
                    settle()
                    step(v.tensor_scalar(e(9), rest, 0.0, None, ALU.is_lt))
                    step(v.tensor_scalar(e(8), rest, float(NODES), None, ALU.is_ge))
                    settle()
                    step(v.tensor_tensor(tile, tile, e(9), ALU.subtract))
                    settle()
                    step(v.tensor_tensor(tile, tile, e(8), ALU.add))
                    settle()
                    step(v.scalar_tensor_tensor(rest, tile, -float(NODES), node, ALU.mult, ALU.add))
                    settle()

                split(e(0), e(2), e(3), ei[0:n_, 0, :])
                split(e(1), e(4), e(5), ei[0:n_, 1, :])
                step(v.scalar_tensor_tensor(pairs[0:n_, :, 0], e(4), float(P), e(5), ALU.mult, ALU.add))
                step(v.tensor_copy(pairs[0:n_, :, 1], e(3)))
                full = [n_, EC, TILES]
                step(v.tensor_tensor(onehot_t[0:n_, :, :], e(2).unsqueeze(2).to_broadcast(full),
                                     iota_tile[0:n_, :].unsqueeze(1).to_broadcast(full), ALU.is_equal))
                settle()
                v.tensor_reduce(count_pt[0:n_, :], onehot_t[0:n_, :, :].rearrange("p c t -> p t c"), AX.X,
                                ALU.add).then_inc(count_done, 1)
                full = [n_, EC, EC]
                step(v.tensor_tensor(same[0:n_, :, :], e(2).unsqueeze(2).to_broadcast(full),
                                     e(2).unsqueeze(1).to_broadcast(full), ALU.is_equal))
                settle()
                step(v.tensor_tensor(same[0:n_, :, :], same[0:n_, :, :], earlier[0:n_, :, :], ALU.mult))
                settle()
                step(v.tensor_reduce(e(6), same[0:n_, :, :], AX.X, ALU.add))
                v.wait_ge(pl_base, 1)
                step(v.tensor_scalar(base_t[:, 0, :], bank[7][:, 128:128 + TILES], -float(P + 1), 0.0, ALU.add, ALU.max))
                settle()
                step(v.tensor_copy(ov_i[:, 0, :], base_t[:, 0, :]))
                settle()
                step(v.tensor_scalar(ov_i[:, 1, :], ov_i[:, 0, :], 7, None, ALU.arith_shift_right))
                settle()
                step(v.tensor_copy(base_t[:, 1, :], ov_i[:, 1, :]))
                settle()
                step(v.tensor_copy(scan[:, 0, :], base_t[:, 1, :]))
                settle()
                cur, d = 0, 1
                while d < TILES:
                    step(v.tensor_copy(scan[:, 1 - cur, 0:d], scan[:, cur, 0:d]))
                    step(v.tensor_tensor(scan[:, 1 - cur, d:TILES], scan[:, cur, d:TILES],
                                         scan[:, cur, 0:TILES - d], ALU.add))
                    settle()
                    cur, d = 1 - cur, 2 * d
                step(v.memset(ov_start[0:1, :], 0))
                settle()
                v.tensor_copy(ov_start[0:1, 1:TILES + 1], scan[0:1, cur, :]).then_inc(ov_ready, 1)
                step(v.tensor_tensor(base_t[:, 2, :], scan[:, cur, :], base_t[:, 1, :], ALU.subtract))
                for to, what in ((7, bank[7][0:n_, 0:TILES]), (8, base_t[0:n_, 2, :])):
                    settle()
                    full = [n_, EC, TILES]
                    step(v.tensor_copy(base_t[0:n_, 0, :], what))
                    settle()
                    hi_i, lo_f, hi_f = ov_i[0:n_, 0, :], base_t[0:n_, 0, :], base_t[0:n_, 1, :]
                    step(v.tensor_copy(hi_i, lo_f))
                    settle()
                    step(v.tensor_scalar(ov_i[0:n_, 1, :], hi_i, 7, None, ALU.arith_shift_right))
                    settle()
                    step(v.tensor_copy(hi_f, ov_i[0:n_, 1, :]))
                    settle()
                    step(v.scalar_tensor_tensor(lo_f, hi_f, -128.0, lo_f, ALU.mult, ALU.add))
                    settle()
                    for part, dest in ((lo_f, e(to)), (hi_f, e(9))):
                        step(v.tensor_tensor(lookup[0:n_, :, :], onehot_t[0:n_, :, :],
                                             part.unsqueeze(1).to_broadcast(full), ALU.mult))
                        settle()
                        step(v.tensor_reduce(dest, lookup[0:n_, :, :], AX.X, ALU.add))
                        settle()
                    step(v.scalar_tensor_tensor(e(to), e(9), 128.0, e(to), ALU.mult, ALU.add))
                    settle()
                step(v.tensor_tensor(e(6), e(6), e(7), ALU.add))
                settle()
                step(v.tensor_copy(ei[0:n_, 0, :], e(6)))
                settle()
                step(v.tensor_scalar(ei[0:n_, 1, :], ei[0:n_, 0, :], 7, None, ALU.arith_shift_right))
                step(v.tensor_scalar(ei[0:n_, 2, :], ei[0:n_, 0, :], P - 1, None, ALU.bitwise_and))
                settle()
                step(v.tensor_copy(e(0), ei[0:n_, 1, :]))
                step(v.tensor_copy(e(1), ei[0:n_, 2, :]))
                settle()
                step(v.scalar_tensor_tensor(e(7), e(2), -2.0, e(8), ALU.mult, ALU.add))
                step(v.tensor_scalar(e(5), e(0), 2.0, None, ALU.is_ge))
                step(v.scalar_tensor_tensor(e(4), e(2), 2.0, e(0), ALU.mult, ALU.add))
                settle()
                step(v.tensor_scalar(e(7), e(7), float(MAIN - 2), None, ALU.add))
                settle()
                step(v.tensor_tensor(e(7), e(7), e(5), ALU.mult))
                settle()
                step(v.tensor_tensor(e(4), e(4), e(7), ALU.add))
                settle()
                v.scalar_tensor_tensor(slot_idx[0:n_, :], e(1), float(SLOTS), e(4), ALU.mult,
                                       ALU.add).then_inc(placed, 1)
                v.wait_ge(placed, 1)
                v.tensor_copy(e(0), e(1)).then_inc(placed, 1)

                def fold(w_sb, k_all, v_sb, which, done):
                    for k in range(k_all):
                        for j in range(2):
                            for h in range(HEADS):
                                i = (k * 2 + j) * HEADS + h
                                wait(v, done, i)
                                v.tensor_tensor_reduce(
                                    fold_out[:, :], w_sb[:, k, h * C:(h + 1) * C],
                                    a_bc[:, which + j, h * C:(h + 1) * C], 1.0, 0.0, ALU.mult, ALU.add,
                                    v_sb[:, k, j * HEADS + h:j * HEADS + h + 1]).then_inc(done, 1)

                v.wait_ge(w1_in, 16 * 5)
                fold(w1_sb, KD, v1_sb, 0, fold1)
                v.wait_ge(w2_in, 16 * 3)
                v.wait_ge(fold1, KD * 8)
                fold(w2_sb, KH, v2_sb, 2, fold2)

                def inverse_root(stat, sem_, n):
                    a, y, t = stat[:, 7:8], stat[:, 8:9], stat[:, 9:10]
                    ops = [lambda: v.tensor_scalar(a, a, EPS, None, ALU.add),
                           lambda: v.tensor_scalar(t.bitcast(I32), a.bitcast(I32), 1, None, ALU.arith_shift_right),
                           lambda: v.tensor_scalar(y.bitcast(I32), t.bitcast(I32), -1.0, float(0x5f3759df),
                                                   ALU.mult, ALU.add)]
                    ops += [lambda: v.scalar_tensor_tensor(t, y, a, y, ALU.mult, ALU.mult),
                            lambda: v.tensor_scalar(t, t, -0.5, 1.5, ALU.mult, ALU.add),
                            lambda: v.tensor_tensor(y, y, t, ALU.mult)] * 3
                    for i, op in enumerate(ops):
                        op().then_inc(sem_, 1)
                        v.wait_ge(sem_, n + i + 1)

                def normalise(xt, xn, stat, sem_, n, done):
                    counted = early(v, n + 1)
                    v.bn_stats(stat[:, 0:6], xt).then_inc(sem_, 1)
                    alone(v, sem_, counted)
                    v.bn_aggr(stat[:, 6:8], stat[:, 0:6]).then_inc(sem_, 1)
                    v.wait_ge(sem_, n + 2)
                    inverse_root(stat, sem_, n + 2)
                    v.tensor_scalar(xn, xt, stat[:, 6:7], stat[:, 8:9], ALU.subtract, ALU.mult).then_inc(done, 1)

                def a_norm(s):
                    v.wait_ge(xa_in[s.u], 16 * s.h + 16)
                    wait(v, xa_turned, s.t - 1)
                    wait(v, xna_ready, s.t)
                    normalise(xa[s.u][:, :], xna[s.u][:, :], stat_a, a_stats, 14 * s.t, xna_ready)

                def a_evict(s):
                    v.wait_ge(h1_done, s.t + 1)
                    wait(v, stored1[s.u], 16 * s.h)
                    v.tensor_copy(rowa[s.u][:, 512:HC], bank[3 + 2 * s.u][:, :]).then_inc(h1_hi, 1)
                    v.tensor_copy(rowa[s.u][:, HC:ROW], bank[6 + s.u][:, 256:264]).then_inc(h1_hi, 1)

                a_norm(first(0, 0))

                def a_body(s, more):
                    if more:
                        a_norm(after(s))
                    a_evict(s)

                over_tiles(v, a_body)
                v.wait_ge(meta_in, 16)
                v.tensor_copy(slot_loc[:, :], slot_meta[:, :, 1]).then_inc(meta_ready, 1)
                v.wait_ge(meta_ready, 1)
                total = v.snap(v.value_load(ov_start[0:1, TILES:TILES + 1], min_val=0, max_val=SLOTS - MAIN))

                def al_src(row):
                    return row[:, HC:HC + HEADS]

                def al_dst(row):
                    return row[:, HC + HEADS:ROW]

                def mask(s):
                    for c in range(2):
                        v.wait_ge(gathered[s.u][c], 16 * s.TH + 16)
                    full = [P, 2, P]
                    v.tensor_tensor(OH[:, :, :], iota_node[:, :].unsqueeze(1).to_broadcast(full),
                                    slot_loc[:, ds(2 * s.t, 2)].unsqueeze(2).to_broadcast(full),
                                    ALU.is_equal).then_inc(onehot, 1)
                    v.wait_ge(onehot, s.T + 1)
                    v.tensor_scalar(NM[:, :, :], OH[:, :, :], BIG, -BIG, ALU.mult, ALU.add).then_inc(nomatch, 1)
                    v.wait_ge(nomatch, s.T + 1)
                    full = [P, 2, HEADS, P]
                    v.tensor_tensor(AM[:, :, :, :], NM[:, :, :].unsqueeze(2).to_broadcast(full),
                                    G[s.u][:, :, HC:HC + HEADS].unsqueeze(3).to_broadcast(full),
                                    ALU.add).then_inc(masked, 1)

                def maximum(s):
                    a, b, off = overflow(v, s, total)
                    v.wait_ge(maskedT, s.T + 1)
                    for c in range(2):
                        v.tensor_reduce(mx2[:, c, :],
                                        bank[c][:, :].rearrange("p (h e) -> p h e", h=HEADS), AX.X,
                                        ALU.max).then_inc(edge_max, 1)
                    v.wait_ge(edge_max, 3 * s.T + 2)
                    counted = early(v, 3 * s.T + 3)
                    v.tensor_tensor(mx, mx2[:, 0, :], mx2[:, 1, :], ALU.max).then_inc(edge_max, 1)
                    alone(v, edge_max, counted)
                    with each(v, a, b) as g:
                        v.wait_ge(ov_in, (a + g + off * 2 + 1) * 16)
                        mask_overflow(g, off, 1)
                        v.wait_ge(ov1_T, g + off + 1)
                        v.tensor_reduce(mxo, bank[0][:, :].rearrange("p (h e) -> p h e", h=HEADS), AX.X,
                                        ALU.max).then_inc(ov1_max, 1)
                        v.wait_ge(ov1_max, (g + off) * 2 + 1)
                        v.tensor_tensor(mx, mx, mxo, ALU.max).then_inc(ov1_max, 1)
                        v.wait_ge(ov1_max, (g + off) * 2 + 2)
                    v.wait_ge(self_in[s.u], 16 * s.TH + 16)
                    als, ald = al_src(H[s.u]), al_dst(H[s.u])
                    v.tensor_tensor(mx, mx, als, ALU.max).then_inc(node_max, 1)
                    v.wait_ge(node_max, s.T + 1)
                    v.tensor_tensor(lsum, mx, ald, ALU.add).then_inc(lgt_sum, 1)
                    v.wait_ge(lgt_sum, s.T + 1)
                    v.tensor_copy(rhs8[:, 0:4], ald).then_inc(shift_ready, 1)
                    v.scalar_tensor_tensor(rhs8[:, 4:8], lsum, SLOPE, lsum, ALU.mult, ALU.max).then_inc(shift_ready, 1)
                    v.tensor_tensor(selfz, als, ald, ALU.add).then_inc(self_logit, 1)
                    v.wait_ge(self_logit, 3 * s.T + 1)
                    v.scalar_tensor_tensor(selfz, selfz, SLOPE, selfz, ALU.mult, ALU.max).then_inc(self_logit, 1)
                    v.wait_ge(self_logit, 3 * s.T + 2)
                    v.wait_ge(shift_ready, 2 * s.T + 2)
                    v.tensor_tensor(selfz, selfz, rhs8[:, 4:8], ALU.subtract).then_inc(self_logit, 1)

                def mask_overflow(g, off, which):
                    n = (g + off) * 3
                    v.tensor_tensor(OHo[:, :], iota_node[:, :],
                                    slot_loc[:, ds(g + MAIN, 1)].to_broadcast([P, P]),
                                    ALU.is_equal).then_inc(ov1_dve if which == 1 else ov2_onehot, 1)
                    if which == 1:
                        v.wait_ge(ov1_dve, (g + off) * 2 + 1)
                        v.tensor_scalar(NMo[:, :], OHo[:, :], BIG, -BIG, ALU.mult, ALU.add).then_inc(ov1_dve, 1)
                        v.wait_ge(ov1_dve, (g + off) * 2 + 2)
                        full = [P, HEADS, P]
                        v.tensor_tensor(AMo[:, :, :], NMo[:, :].unsqueeze(1).to_broadcast(full),
                                        al_src(GO).unsqueeze(2).to_broadcast(full), ALU.add).then_inc(ov1_masked, 1)

                def logits(zt, als, per_target, sem_, n):
                    v.tensor_tensor(zt, als, per_target[0], ALU.add).then_inc(sem_, 1)
                    v.wait_ge(sem_, n + 1)
                    v.scalar_tensor_tensor(zt, zt, SLOPE, zt, ALU.mult, ALU.max).then_inc(sem_, 1)
                    v.wait_ge(sem_, n + 2)
                    v.tensor_tensor(zt, zt, per_target[1], ALU.subtract).then_inc(sem_, 1)
                    v.wait_ge(sem_, n + 3)
                    v.tensor_scalar(zt, zt, 0.0, None, ALU.min).then_inc(sem_, 1)

                def scatter(s):
                    v.wait_ge(edge_rhs, s.T + 1)
                    logits(z, G[s.u][:, :, HC:HC + HEADS], (edge_ps[:, :, 0:4], edge_ps[:, :, 4:8]), edge_logit, 4 * s.T)
                    v.wait_ge(edge_weight, s.T + 1)
                    full = [P, 2, HEADS, P]
                    v.tensor_tensor(S[:, :, :, :], OH[:, :, :].unsqueeze(2).to_broadcast(full),
                                    w.unsqueeze(3).to_broadcast(full), ALU.mult).then_inc(scatter_ready, 1)

                def mix(s, bias):
                    a, b, off = overflow(v, s, total)
                    counted = early(v, s.T + 1)
                    v.wait_ge(den_done, s.T + 1)
                    v.wait_ge(self_weight, s.T + 1)
                    v.tensor_tensor(dsum, den_ps, wself, ALU.add).then_inc(den_total, 1)
                    alone(v, den_total, counted)
                    with each(v, a, b) as g:
                        v.wait_ge(ov_in, (b + g + off * 2 + 1) * 16)
                        mask_overflow(g, off, 2)
                        v.wait_ge(ov2_T, g + off + 1)
                        v.tensor_copy(ohTo[:, :], ohT_o_ps).then_inc(ov2_copied, 1)
                        v.wait_ge(ov2_rhs, g + off + 1)
                        logits(zo, al_src(GO), (edge_o_ps[:, 0:4], edge_o_ps[:, 4:8]), ov2_logit, (g + off) * 4)
                        v.wait_ge(ov2_weight, g + off + 1)
                        full = [P, HEADS, P]
                        v.tensor_tensor(So[:, :, :], OHo[:, :].unsqueeze(1).to_broadcast(full),
                                        wo.unsqueeze(2).to_broadcast(full), ALU.mult).then_inc(ov2_scatter, 1)
                        v.wait_ge(ov2_agg, g + off + 2)
                        v.tensor_tensor(dsum, dsum, den_o_ps, ALU.add).then_inc(ov2_den, 1)
                        v.wait_ge(ov2_den, g + off + 1)
                    v.reciprocal(rden, dsum).then_inc(den_inv, 1)
                    v.wait_ge(den_inv, s.T + 1)
                    v.tensor_tensor(wsn, wself, rden, ALU.mult).then_inc(self_scale, 1)
                    v.wait_ge(self_scale, s.T + 1)
                    for h in range(HEADS):
                        cols = slice(h * C, (h + 1) * C)
                        v.scalar_tensor_tensor(mixed[:, cols], H[s.u][:, cols], wsn[:, h:h + 1], bias[:, cols],
                                               ALU.mult, ALU.add).then_inc(self_scaled, 1)
                    v.wait_ge(aggregated, s.T + 1)
                    for h in range(HEADS):
                        cols = slice(h * C, (h + 1) * C)
                        v.wait_ge(self_scaled, 4 * s.T + h + 1)
                        v.scalar_tensor_tensor(mixed[:, cols], bank[3 + h // 2][:, (h % 2) * C:(h % 2 + 1) * C],
                                               rden[:, h:h + 1], mixed[:, cols], ALU.mult, ALU.add).then_inc(mix_done, 1)

                def prepare(s, bias):
                    mask(s)
                    maximum(s)
                    scatter(s)
                    mix(s, bias)

                prepare(phase_tile(first(0, 0), 0), b1_bc)
                mask(phase_tile(first(0, 1), 0))

                def b_body(s, more):
                    n = phase_tile(after(s), 0)
                    if more:
                        maximum(n)
                        scatter(n)
                        mix(n, b1_bc)
                    v.wait_ge(dense_done, s.t + 1)
                    wait(v, stored2[s.u], 16 * s.h)
                    v.tensor_copy(rowb[s.u][:, 512:HC], bank[6][:, :]).then_inc(h2_hi, 1)
                    v.tensor_copy(rowb[s.u][:, HC:ROW], bank[7][:, 0:8]).then_inc(h2_hi, 1)
                    if more and not last_but_one(s):
                        mask(phase_tile(after(after(s)), 0))

                over_tiles(v, b_body)

                v.wait_ge(fb2_sum, 1)
                v.tensor_scalar(fb2_twice[:, :], bank[7][:, :], 2.0, None, ALU.mult).then_inc(c_const, 1)
                v.wait_ge(c_const, 1)
                prepare(phase_tile(first(0, 0), 1), b2_bc)
                mask(phase_tile(first(0, 1), 1))

                def finish_tile(s):
                    v.wait_ge(f2_done, s.t + 1)
                    wait(v, out_stored[s.u], 16 * s.h)
                    v.tensor_tensor(outb[s.u][:, :], bank[7][:, :], x2[s.u][:, :], ALU.add).then_inc(out_sum, 1)
                    v.wait_ge(out_sum, 2 * s.t + 1)
                    v.tensor_tensor(outb[s.u][:, :], outb[s.u][:, :], fb2_twice[:, :], ALU.add).then_inc(out_sum, 1)

                def c_body(s, more):
                    n = phase_tile(after(s), 1)
                    if more:
                        maximum(n)
                    v.wait_ge(fc_done, s.t + 1)
                    v.wait_ge(xc_in[s.u], 16 * s.h + 16)
                    v.tensor_tensor(x2[s.u][:, :], bank[5][:, :], bfc_bc[:, :], ALU.add).then_inc(c_x2, 1)
                    v.wait_ge(c_x2, 2 * s.t + 1)
                    v.tensor_tensor(x2[s.u][:, :], x2[s.u][:, :], xc[s.u][:, :], ALU.add).then_inc(c_x2, 1)
                    v.wait_ge(c_x2, 2 * s.t + 2)
                    normalise(x2[s.u][:, :], xn2[:, :], stat_c, c_stats, 14 * s.t, c_xn)
                    if more:
                        scatter(n)
                    if not is_zero(s.t):
                        finish_tile(before(s))
                    alone(v, gate_done, s.t + 1)
                    v.max(m8, gate_ps).then_inc(c_top, 1)
                    v.wait_ge(c_top, 2 * s.t + 1)
                    v.tensor_scalar(nmax, m8[:, 0:1], -1.0, None, ALU.mult).then_inc(c_top, 1)
                    v.wait_ge(c_exp, s.t + 1)
                    v.reciprocal(rsum, esum).then_inc(c_prob, 1)
                    v.wait_ge(c_prob, 5 * s.t + 1)
                    v.tensor_scalar(e8, e8, rsum, None, ALU.mult).then_inc(c_prob, 1)
                    v.wait_ge(c_prob, 5 * s.t + 2)
                    v.tensor_tensor(s2, e8[:, 0:1], e8[:, 1:2], ALU.add).then_inc(c_prob, 1)
                    v.wait_ge(c_prob, 5 * s.t + 3)
                    v.reciprocal(s2, s2).then_inc(c_prob, 1)
                    v.wait_ge(c_prob, 5 * s.t + 4)
                    v.tensor_scalar(p2, e8[:, 0:2], s2, None, ALU.mult).then_inc(c_prob, 1)
                    v.wait_ge(c_prob, 5 * s.t + 5)
                    v.wait_ge(f1_done, s.t + 1)
                    for i in range(2):
                        v.scalar_tensor_tensor(ffn_v[:, i, :], bank[6][:, :], p2[:, i:i + 1], fb1_bc[:, :],
                                               ALU.mult, ALU.add).then_inc(ffn_in, 1)
                    v.wait_ge(gelu_done, s.t + 1)
                    v.tensor_tensor(gsum[:, :], ffn_v[:, 0, :], ffn_v[:, 1, :], ALU.add).then_inc(gsum_done, 1)
                    if more:
                        mix(n, b2_bc)
                    if more and not last_but_one(s):
                        mask(phase_tile(after(after(s)), 1))

                over_tiles(v, c_body)
                finish_tile(first(HALF - 1, 1))

            @block.scalar
            def _(act):
                def a_body(s, more):
                    if more:
                        turned(after(s))
                    act.wait_ge(h1_done, s.t + 1)
                    wait(act, stored1[s.u], 16 * s.h)
                    act.copy(rowa[s.u][:, 0:512], bank[2 + 2 * s.u][:, :]).then_inc(h1_lo, 1)

                def turned(s):
                    act.wait_ge(xa_turned, s.t + 1)
                    wait(act, h1_done, s.t - 1)
                    act.copy(xTa[s.u][:, :, :].rearrange("p k n -> p (k n)"), bank[s.u][:, :]).then_inc(xTa_copied, 1)

                turned(first(0, 0))
                over_tiles(act, a_body)
                act.wait_ge(ov_ready, 1)
                act.wait_ge(cleared, 1)
                total = act.snap(act.value_load(ov_start[0:1, TILES:TILES + 1], min_val=0, max_val=SLOTS - MAIN))

                def spread(s):
                    act.wait_ge(onehotT, s.T + 1)
                    act.copy(ohT[:, :, :].rearrange("p c e -> p (c e)"), small[:, 0:256]).then_inc(onehotT_copied, 1)
                    act.wait_ge(self_logit, 3 * s.T + 3)
                    act.activation(wself, selfz, ACT.Exp).then_inc(self_weight, 1)

                def weigh(s):
                    act.wait_ge(edge_logit, 4 * s.T + 4)
                    act.activation(w, z, ACT.Exp).then_inc(edge_weight, 1)
                    a, b, off = overflow(act, s, total)
                    with each(act, a, b) as g:
                        act.wait_ge(ov2_logit, (g + off) * 4 + 4)
                        act.activation(wo, zo, ACT.Exp).then_inc(ov2_weight, 1)

                def relu(s):
                    for half in range(2):
                        act.wait_ge(mixedT, 2 * s.T + 1 + half)
                        act.activation(hT[:, 4 * half:4 * half + 4, :].rearrange("p k n -> p (k n)"),
                                       bank[half][:, :], ACT.Relu).then_inc(relu_done, 1)

                def prepare(s):
                    spread(s)
                    weigh(s)
                    relu(s)

                prepare(phase_tile(first(0, 0), 0))

                def b_body(s, more):
                    n = phase_tile(after(s), 0)
                    if more:
                        spread(n)
                        weigh(n)
                    act.wait_ge(dense_done, s.t + 1)
                    wait(act, stored2[s.u], 16 * s.h)
                    act.copy(rowb[s.u][:, 0:512], bank[5][:, :]).then_inc(h2_lo, 1)
                    if more:
                        relu(n)

                over_tiles(act, b_body)
                prepare(phase_tile(first(0, 0), 1))

                def c_body(s, more):
                    n = phase_tile(after(s), 1)
                    if more:
                        spread(n)
                    act.wait_ge(c_xT, s.t + 1)
                    act.copy(xT2[:, :, :].rearrange("p k n -> p (k n)"), bank[5][:, :]).then_inc(c_xTc, 1)
                    if more:
                        weigh(n)
                    act.wait_ge(c_top, 2 * s.t + 2)
                    act.activation(e8, m8, ACT.Exp, bias=nmax, accum_out=esum).then_inc(c_exp, 1)
                    act.wait_ge(ffn_in, 2 * s.t + 2)
                    flat = ffn_v[:, :, :].rearrange("p i f -> p (i f)")
                    act.activation(flat, flat, ACT.Gelu).then_inc(gelu_done, 1)
                    act.wait_ge(c_gT, s.t + 1)
                    act.copy(gT[:, :, :].rearrange("p k n -> p (k n)"), bank[5][:, :]).then_inc(gT_copied, 1)
                    if more:
                        relu(n)

                over_tiles(act, c_body)


_INS = ['x', 'src', 'dst', 'L0_gnn_W1', 'L0_gnn_a_src1', 'L0_gnn_a_dst1', 'L0_gnn_b1', 'L0_gnn_W2', 'L0_gnn_a_src2',
        'L0_gnn_a_dst2', 'L0_gnn_b2', 'L0_gnn_Wfc', 'L0_gnn_bfc', 'L0_ffn_Wg', 'L0_ffn_W1', 'L0_ffn_b1', 'L0_ffn_W2',
        'L0_ffn_b2']


def kernel(**inputs):
    import numpy as np
    import concourse.bacc as bacc
    from concourse.bass_utils import run_bass_kernel_spmd

    nc = bacc.Bacc("TRN2", target_bir_lowering=False, num_devices=1)
    arrays, args = {}, []
    for name in _INS:
        a = np.ascontiguousarray(inputs[name])
        arrays[f"in_{name}"] = a
        args.append(nc.dram_tensor(f"in_{name}", a.shape, mybir.dt.from_np(a.dtype), kind="ExternalInput").ap())
    args.append(nc.dram_tensor("out", arrays["in_x"].shape, F32, kind="ExternalOutput").ap())
    gnn_ffn_kernel(nc, *args)
    r = run_bass_kernel_spmd(nc, [arrays], core_ids=[0])
    return r.results[0]["out"]
```

```python
from contextlib import ExitStack, contextmanager

import concourse.bass as bass
from concourse import mybir

F32 = mybir.dt.float32
F32R = mybir.dt.float32r
BF16 = mybir.dt.bfloat16
I32 = mybir.dt.int32
U32 = mybir.dt.uint32
ALU = mybir.AluOpType
ACT = mybir.ActivationFunctionType
AX = mybir.AxisListType
ds = bass.ds

P = 128
EPS = 1e-5
SLOPE = 0.2
BIG = 1e30
NODES = 125
HEADS = 4
OVMUL = 16384


class Tile:

    def __init__(self, t, h, u, T=None, TH=None, phase=0):
        self.t, self.h, self.u, self.T, self.TH, self.phase = t, h, u, T, TH, phase


class Count:
    n = 0


class Space:

    def __init__(self, nc, start):
        self.nc, self.end = nc, (start + 31) // 32 * 32

    def take(self, name, shape, dt=F32):
        tensor = self.nc.alloc_sbuf_tensor_at(name, shape, dt, offset=self.end)
        size = 2 if dt == BF16 else 4
        for n in shape[1:]:
            size *= n
        self.end += (size + 31) // 32 * 32
        return tensor

    def pair(self, name, shape):
        return [self.take(f"{name}_{part}", shape, F32R) for part in ("hi", "lo")]


def first(tile_half, u):
    return Tile(t=tile_half * 2 + u, h=tile_half, u=u)


def after(s):
    return first(s.h, 1) if s.u == 0 else first(s.h + 1, 0)


def before(s):
    return first(s.h - 1, 1) if s.u == 0 else first(s.h, 0)


def last_but_one(s):
    return isinstance(s.t, int) and s.u == 0 and s.h > 0


def is_zero(t):
    return isinstance(t, int) and t == 0


def wait(eng, sem, value):
    if not isinstance(value, int) or value > 0:
        eng.wait_ge(sem, value)


def gnn_ffn_kernel(nc, x, src, dst, w1, as1, ad1, b1, w2, as2, ad2, b2, wfc, bfc, wg, f1, fb1, f2, fb2, out):
    N, D = x.shape
    E = src.shape[0]
    HC = w1.shape[1]
    C = HC // HEADS
    EX, _, DFF = f1.shape
    FF = EX * DFF
    TILES = N // NODES
    HALF = TILES // 2
    EC = E // NODES
    KD, KH, KF = D // P, HC // P, FF // P
    ROW = HC + 2 * HEADS
    MAIN = 2 * TILES
    SLOTS = MAIN + (E // P + 2)
    ROWS = TILES * P
    DUMMY = 1 << 20
    FG = FF + EX
    W3, F2W = ROW // 3, FG // 2
    WC_LOADS = 16 * (EX + 3)
    assert N % NODES == 0 and E % NODES == 0 and TILES % 2 == 0 and SLOTS % 2 == 0

    table1 = nc.dram_tensor("table1", (ROWS, ROW), F32, kind="Internal").ap()
    table2 = nc.dram_tensor("table2", (ROWS, ROW), F32, kind="Internal").ap()
    slots_dram = nc.dram_tensor("slots", (P * SLOTS, 2), I32, kind="Internal").ap()

    ctx = ExitStack()
    with ctx:
        def sem(name):
            return ctx.enter_context(nc.semaphore(name))

        bank = [ctx.enter_context(nc.psum_tensor(f"bank{i}", [P, 512], F32)) for i in range(8)]

        base = Space(nc, nc.sbuf_base)
        b1_bc = base.take("b1_bc", [P, HC])
        b2_bc = base.take("b2_bc", [P, HC])
        bfc_bc = base.take("bfc_bc", [P, D])
        fb1_bc = base.take("fb1_bc", [P, FF])
        fb2_sb = base.take("fb2_sb", [EX, D])
        ones_ex = base.take("ones_ex", [EX, P])
        fb2_twice = base.take("fb2_twice", [P, D])
        ident = base.take("ident", [P, P])
        iota_node = base.take("iota_node", [P, P])
        slot_loc = base.take("slot_loc", [P, SLOTS])
        slot_meta = base.take("slot_meta", [P, SLOTS, 2], I32)
        ov_start = base.take("ov_start", [1, TILES + 8], I32)

        weights_b = Space(nc, base.end)
        w2_hi = weights_b.take("w2_hi", [P, KH, ROW], F32R)
        w2_raw = Space(nc, weights_b.end).take("w2_raw", [P, KH, ROW])
        w2_lo = weights_b.take("w2_lo", [P, KH, ROW], F32R)
        weights_c = Space(nc, base.end)
        wfc_hi, wfc_lo = weights_c.pair("wfc", [P, KH, D])
        f1_hi, f1_lo = weights_c.pair("f1", [P, KD, FG])
        f2_hi, f2_lo = weights_c.pair("f2", [P, KF, D])
        assert weights_c.end <= weights_b.end

        place = Space(nc, base.end)
        onehot_t = place.take("onehot_t", [P, EC, TILES], BF16)
        same = place.take("same", [P, EC, EC], BF16)
        lookup = same
        assert place.end <= base.end + KH * ROW * 4

        phase_a = Space(nc, weights_b.end)
        w1_hi = phase_a.take("w1_hi", [P, KD, ROW], F32R)
        w1_raw = Space(nc, phase_a.end).take("w1_raw", [P, KD, ROW])
        w1_lo = phase_a.take("w1_lo", [P, KD, ROW], F32R)
        a_bc = phase_a.take("a_bc", [P, 4, HC])
        fold_out = phase_a.take("fold_out", [P, C])
        xa = [phase_a.take(f"xa{u}", [P, D]) for u in range(2)]
        xna = [phase_a.take(f"xna{u}", [P, D]) for u in range(2)]
        xTa = [phase_a.pair(f"xTa{u}", [P, KD, P]) for u in range(2)]
        stat_a = phase_a.take("stat_a", [P, 10])
        rowa = [phase_a.take(f"rowa{u}", [P, ROW]) for u in range(2)]
        pairs = phase_a.take("pairs", [P, EC, 2], I32)
        slot_idx = phase_a.take("slot_idx", [P, EC], I32)
        pair_st = phase_a.take("pair_st", [P, 4, 2], I32)
        idx_st = phase_a.take("idx_st", [P, 4], I32)
        fill = phase_a.take("fill", [P, SLOTS, 2], I32)
        dst_i = phase_a.take("dst_i", [P, EC], I32)
        src_i = phase_a.take("src_i", [P, EC], I32)
        ef = phase_a.take("ef", [P, 10, EC])
        ei = phase_a.take("ei", [P, 4, EC], I32)
        earlier = phase_a.take("earlier", [P, EC, EC], BF16)
        iota_tile = phase_a.take("iota_tile", [P, TILES])
        tri = phase_a.take("tri", [P, P])
        ones = phase_a.take("ones", [P, P])
        count_pt = phase_a.take("count_pt", [P, TILES])
        scan = phase_a.take("scan", [P, 2, TILES])
        ov_i = phase_a.take("ov_i", [P, 2, TILES], I32)
        base_t = phase_a.take("base_t", [P, 3, TILES])

        raw_c = Space(nc, weights_b.end)
        wfc_raw = raw_c.take("wfc_raw", [P, KH, D])
        f1_raw = raw_c.take("f1_raw", [P, KD, FG])
        f2_raw = raw_c.take("f2_raw", [P, KF, D])
        phase_c = Space(nc, weights_b.end)
        xc = [phase_c.take(f"xc{u}", [P, D]) for u in range(2)]
        x2 = [phase_c.take(f"x2_{u}", [P, D]) for u in range(2)]
        xn2 = phase_c.take("xn2", [P, D])
        xT2 = phase_c.pair("xT2", [P, KD, P])
        ffn_v = phase_c.take("ffn_v", [P, 2, FF])
        gsum = phase_c.take("gsum", [P, FF])
        gT = phase_c.pair("gT", [P, KF, P])
        outb = [phase_c.take(f"outb{u}", [P, D]) for u in range(2)]

        agg = Space(nc, max(raw_c.end, phase_c.end))
        G = [agg.take(f"G{u}", [P, 2, ROW]) for u in range(2)]
        H = [agg.take(f"H{u}", [P, ROW]) for u in range(2)]
        GS = agg.pair("GS", [P, 2, HC])
        GO = agg.take("GO", [P, ROW])
        gidx = [agg.take(f"gidx{u}", [P, 2], I32) for u in range(2)]
        goidx = agg.take("goidx", [P, 1], I32)
        OH = [agg.take(f"OH{u}", [P, 2, P], F32R) for u in range(2)]
        NM = agg.take("NM", [P, 2, P])
        AM = agg.take("AM", [P, 2, HEADS, P])
        OHo = agg.take("OHo", [P, P], F32R)
        NMo = agg.take("NMo", [P, P])
        AMo = agg.take("AMo", [P, HEADS, P])
        ohTo = agg.take("ohTo", [P, P])
        ohT = agg.take("ohT", [P, 2, P])
        small_f = agg.take("small_f", [P, 106])
        mx2 = agg.take("mx2", [P, 2, HEADS])
        mixed = agg.take("mixed", [P, HC])
        hT = agg.pair("hT", [P, KH, P])
        rowb = [agg.take(f"rowb{u}", [P, ROW]) for u in range(2)]

        mx, mxo = small_f[:, 0:4], small_f[:, 4:8]
        lsum, rhs8 = small_f[:, 8:12], small_f[:, 12:20]
        selfz, wself = small_f[:, 20:24], small_f[:, 24:28]
        z = small_f[:, 28:36].rearrange("p (c h) -> p c h", c=2)
        w = small_f[:, 36:44].rearrange("p (c h) -> p c h", c=2)
        zo, wo = small_f[:, 44:48], small_f[:, 48:52]
        dsum, rden, wsn = small_f[:, 52:56], small_f[:, 56:60], small_f[:, 60:64]
        stat_c = small_f[:, 96:106]
        m8, nmax, e8, esum = small_f[:, 73:81], small_f[:, 81:82], small_f[:, 82:90], small_f[:, 90:91]
        rsum, s2, p2 = small_f[:, 91:92], small_f[:, 92:93], small_f[:, 94:96]

        small = bank[2]
        ohT_ps = small[:, 0:256].rearrange("p (c e) -> p c e", c=2)
        edge_ps = small[:, 256:272].rearrange("p (c k) -> p c k", c=2)
        den_ps, den_o_ps, edge_o_ps = small[:, 272:276], small[:, 280:284], small[:, 288:296]
        ohT_o_ps = small[:, 384:512]
        gate_ps = bank[7][:, F2W - EX:F2W]

        w1_in, edges_in, w2_in, wc_in = sem("w1_in"), sem("edges_in"), sem("w2_in"), sem("wc_in")
        bias_in = sem("bias_in")
        consts = sem("consts")
        fold1, fold2 = sem("fold1"), sem("fold2")
        w1_hi_done, w1_lo_done, w2_hi_done, w2_lo_done = (sem(n) for n in (
            "w1_hi_done", "w1_lo_done", "w2_hi_done", "w2_lo_done"))
        wc_hi_done, wc_lo_done, xc_cleared = sem("wc_hi_done"), sem("wc_lo_done"), sem("xc_cleared")
        fb2_sum = sem("fb2_sum")
        placing, count_done, pl_base, filled, staged, scattered, meta_in, meta_ready = (
            sem("placing"), sem("count_done"), sem("pl_base"), sem("filled"), sem("staged"),
            [sem(f"scattered{i}") for i in range(4)], sem("meta_in"), sem("meta_ready"))
        placed, ov_ready, c_const = sem("placed"), sem("ov_ready"), sem("c_const")
        xa_in = [sem(f"xa_in{u}") for u in range(2)]
        stored1 = [sem(f"stored1_{u}") for u in range(2)]
        a_stats, xna_ready, xa_turned, xTa_hi, xTa_lo, h1_done, h1_act, h1_dve = (
            sem(n) for n in ("a_stats", "xna_ready", "xa_turned", "xTa_hi", "xTa_lo", "h1_done", "h1_act", "h1_dve"))
        self_in = [sem(f"self_in{u}") for u in range(2)]
        gathered = [[sem(f"gathered{u}{c}") for c in range(2)] for u in range(2)]
        cleared = sem("cleared")
        (index_staged, onehot, nomatch, masked, maskedT, onehotT, onehotT_copied, edge_max, node_max, lgt_sum,
         shift_ready, self_logit, self_weight, edge_rhs, edge_logit, edge_weight, scaled_hi, scaled_lo, aggregated, den_done,
         den_total, den_inv, self_scale, self_scaled, mix_done, mixedT, relu_hi, relu_lo) = (sem(n) for n in (
             "index_staged", "onehot", "nomatch", "masked", "maskedT", "onehotT", "onehotT_copied", "edge_max",
             "node_max", "lgt_sum", "shift_ready", "self_logit", "self_weight", "edge_rhs", "edge_logit",
             "edge_weight", "scaled_hi", "scaled_lo", "aggregated", "den_done", "den_total", "den_inv", "self_scale",
             "self_scaled", "mix_done", "mixedT", "relu_hi", "relu_lo"))
        (ov_staged, ov_in, ov1_masked, ov1_dve, ov1_T, ov1_max, ov2_onehot, ov2_T, ov2_copied, ov2_rhs, ov2_logit,
         ov2_weight, ov2_hi, ov2_lo, ov2_agg, ov2_den) = (sem(n) for n in (
             "ov_staged", "ov_in", "ov1_masked", "ov1_dve", "ov1_T", "ov1_max", "ov2_onehot", "ov2_T", "ov2_copied",
             "ov2_rhs", "ov2_logit", "ov2_weight", "ov2_hi", "ov2_lo", "ov2_agg", "ov2_den"))
        dense_done, h2_act, h2_dve = sem("dense_done"), sem("h2_act"), sem("h2_dve")
        stored2 = [sem(f"stored2_{u}") for u in range(2)]
        xc_in = [sem(f"xc_in{u}") for u in range(2)]
        out_stored = [sem(f"out_stored{u}") for u in range(2)]
        (x_biased, fc_done, c_x2, x2_biased, c_stats, c_xn, c_xT, xT2_hi, xT2_lo, f1_done, c_top, c_exp, c_prob,
         ffn_in, gelu_done, gsum_done, c_gT, gT_hi, gT_lo, f2_done, out_sum) = (sem(n) for n in (
             "x_biased", "fc_done", "c_x2", "x2_biased", "c_stats", "c_xn", "c_xT", "xT2_hi", "xT2_lo", "f1_done",
             "c_top", "c_exp", "c_prob", "ffn_in", "gelu_done", "gsum_done", "c_gT", "gT_hi", "gT_lo", "f2_done",
             "out_sum"))

        def phase_tile(s, phase):
            return Tile(t=s.t, h=s.h, u=s.u, T=s.t + TILES * phase, TH=s.h + HALF * phase, phase=phase)

        def early(eng, value):
            return value if isinstance(value, int) else eng.snap(eng.to_reg(value))

        def alone(eng, sem, value):
            eng.wait_ge(consts, 1)
            eng.wait_ge(sem, value)

        def overflow(eng, s, total):
            a = eng.value_load(ov_start[0:1, ds(s.t, 1)], min_val=0, max_val=SLOTS - MAIN)
            b = eng.value_load(ov_start[0:1, ds(s.t + 1, 1)], min_val=0, max_val=SLOTS - MAIN)
            return a, b, (total if s.phase else 0)

        @contextmanager
        def each(eng, a, b):
            with eng.If(a < b):
                with eng.Fori(a, b) as g:
                    yield g

        def over_tiles(eng, body):
            body(first(0, 0), True)
            body(first(0, 1), True)
            with eng.Fori(1, HALF - 1) as it:
                body(first(it, 0), True)
                body(first(it, 1), True)
            body(first(HALF - 1, 0), True)
            body(first(HALF - 1, 1), False)

        with nc.Block() as block:
            @block.sync
            def _(sp):
                sp.dma_start(dst_i[0:NODES, :], dst.rearrange("(p c) -> p c", c=EC)).then_inc(edges_in, 16)
                sp.dma_start(src_i[0:NODES, :], src.rearrange("(p c) -> p c", c=EC)).then_inc(edges_in, 16)
                sp.wait_ge(consts, 1)
                for u in range(2):
                    sp.dma_start(xa[u][0:NODES, :], x[u * NODES:(u + 1) * NODES, :]).then_inc(xa_in[u], 16)
                sp.dma_start(w1_raw[:, :, 0:HC], w1.rearrange("(k p) n -> p k n", p=P)).then_inc(w1_in, 16)
                for i, a in enumerate((as1, ad1, as2, ad2)):
                    sp.dma_start(a_bc[:, i, :], a.rearrange("h c -> (h c)").partition_broadcast(P)).then_inc(w1_in, 16)
                sp.dma_start(w2_raw[:, :, 0:HC], w2.rearrange("(k p) n -> p k n", p=P)).then_inc(w2_in, 16)
                for to, of in ((b1_bc, b1), (b2_bc, b2)):
                    sp.dma_start(to[:, :], of.partition_broadcast(P)).then_inc(w2_in, 16)
                sp.dma_start(fb2_sb[:, :], fb2).then_inc(bias_in, 16)
                sp.dma_start(bfc_bc[:, :], bfc.partition_broadcast(P)).then_inc(bias_in, 16)
                sp.dma_start(fb1_bc[:, :], fb1.rearrange("e f -> (e f)").partition_broadcast(P)).then_inc(bias_in, 16)

                def a_io(s, more):
                    if more is not None:
                        sp.wait_ge(xna_ready, s.t + 1)
                        n = s.t + 2
                        sp.dma_start(xa[s.u][0:NODES, :], x[ds(n * NODES, NODES), :]).then_inc(xa_in[s.u], 16)
                    sp.wait_ge(h1_act, 2 * s.t + 2)
                    sp.wait_ge(h1_dve, s.t + 1)
                    sp.dma_start(table1[ds(s.t * P, P), :], rowa[s.u][:, :]).then_inc(stored1[s.u], 16)

                with sp.Fori(0, HALF - 1) as it:
                    a_io(first(it, 0), True)
                    a_io(first(it, 1), True)
                a_io(first(HALF - 1, 0), None)
                a_io(first(HALF - 1, 1), None)

                for i in range(4):
                    sp.wait_ge(scattered[i], 16 * (EC // 4))
                sp.dma_start(slot_meta[:, :, :], slots_dram.rearrange("(p c) k -> p c k", p=P)).then_inc(meta_in, 16)
                sp.wait_ge(cleared, 1)
                for u in range(2):
                    sp.wait_ge(stored1[u], 16 * HALF)

                sp.dma_start(wfc_raw[:, :, :], wfc.rearrange("(k p) n -> p k n", p=P)).then_inc(wc_in, 16)
                for e in range(EX):
                    sp.dma_start(f1_raw[:, :, e * DFF:(e + 1) * DFF],
                                 f1[e].rearrange("(k p) f -> p k f", p=P)).then_inc(wc_in, 16)
                sp.dma_start(f1_raw[:, :, FF:FG], wg.rearrange("(k p) e -> p k e", p=P)).then_inc(wc_in, 16)
                sp.dma_start(f2_raw[:, :, :],
                             f2.rearrange("e f d -> (e f) d").rearrange("(k p) d -> p k d", p=P)).then_inc(wc_in, 16)

                def self_load(s, table):
                    sp.dma_start(H[s.u][:, :], table[ds(s.t * P, P), :]).then_inc(self_in[s.u], 16)

                def b_io(s, more):
                    if more is not None:
                        sp.wait_ge(self_scaled, 4 * (s.t + 1))
                        self_load(Tile(s.t + 2, s.h + 1, s.u), table1)
                    sp.wait_ge(h2_act, 2 * s.t + 2)
                    sp.wait_ge(h2_dve, s.t + 1)
                    sp.dma_start(table2[ds(s.t * P, P), :], rowb[s.u][:, :]).then_inc(stored2[s.u], 16)

                self_load(first(0, 0), table1)
                self_load(first(0, 1), table1)
                with sp.Fori(0, HALF - 1) as it:
                    b_io(first(it, 0), True)
                    b_io(first(it, 1), True)
                b_io(first(HALF - 1, 0), None)
                b_io(first(HALF - 1, 1), None)

                sp.wait_ge(self_scaled, 4 * TILES)
                for u in range(2):
                    sp.wait_ge(stored2[u], 16 * HALF)

                def x_load(s):
                    sp.dma_start(xc[s.u][0:NODES, :], x[ds(s.t * NODES, NODES), :]).then_inc(xc_in[s.u], 16)

                def c_io(s, more):
                    if more is not None:
                        n = Tile(s.t + 2, s.h + 1, s.u)
                        sp.wait_ge(self_scaled, 4 * (s.t + TILES + 1))
                        self_load(n, table2)
                        sp.wait_ge(c_x2, s.t + 1)
                        x_load(n)
                    sp.wait_ge(out_sum, s.t + 1)
                    sp.dma_start(out[ds(s.t * NODES, NODES), :], outb[s.u][0:NODES, :]).then_inc(out_stored[s.u], 16)

                for u in range(2):
                    self_load(first(0, u), table2)
                sp.wait_ge(xc_cleared, 1)
                for u in range(2):
                    x_load(first(0, u))
                with sp.Fori(0, HALF - 1) as it:
                    c_io(first(it, 0), True)
                    c_io(first(it, 1), True)
                c_io(first(HALF - 1, 0), None)
                c_io(first(HALF - 1, 1), None)
                for u in range(2):
                    sp.wait_ge(out_stored[u], 16 * HALF)

            @block.gpsimd
            def _(pool):
                for u in range(2):
                    pool.memset(xa[u][:, :], 0.0)
                pool.memset(ones_ex[:, :], 1.0)
                pool.memset(fill[:, :, 0:1], DUMMY)
                pool.memset(fill[:, :, 1:2], -1).then_inc(consts, 1)
                pool.iota(iota_node[:, :], [[1, P]], base=0, channel_multiplier=0,
                          allow_small_or_imprecise_dtypes=True)
                pool.iota(iota_tile[:, :], [[1, TILES]], base=0, channel_multiplier=0,
                          allow_small_or_imprecise_dtypes=True)
                pool.memset(ident[:, :], 0.0)
                pool.memset(tri[:, :], 1.0)
                pool.memset(earlier[:, :, :], 1.0)
                pool.memset(ones[:, :], 1.0).then_inc(consts, 1)
                pool.wait_ge(consts, 2)
                pool.affine_select(out=ident[:, :], in_=ident[:, :], pattern=[[-1, P]], compare_op=ALU.not_equal,
                                   fill=1.0, base=0, channel_multiplier=1)
                pool.affine_select(out=tri[:, :], in_=tri[:, :], pattern=[[1, P]], compare_op=ALU.is_gt,
                                   fill=0.0, base=0, channel_multiplier=-1)
                pool.affine_select(out=earlier[:, :, :], in_=earlier[:, :, :], pattern=[[1, EC], [-1, EC]],
                                   compare_op=ALU.is_gt, fill=0.0, base=0, channel_multiplier=0).then_inc(consts, 1)
                pool.dma_start(slots_dram.rearrange("(p c) k -> p c k", p=P), fill[:, :, :]).then_inc(filled, 16)

                pool.wait_ge(placed, 2)
                pool.wait_ge(filled, 16)
                def scatter(it):
                    for i in range(4):
                        wait(pool, scattered[i], 16 * it)
                    counted = early(pool, 2 * it + 2)
                    pool.tensor_copy(pair_st[0:NODES, :, :], pairs[0:NODES, ds(4 * it, 4), :]).then_inc(staged, 1)
                    pool.tensor_copy(idx_st[0:NODES, :], slot_idx[0:NODES, ds(4 * it, 4)]).then_inc(staged, 1)
                    alone(pool, staged, counted)
                    for i in range(4):
                        pool.indirect_dma_start(
                            out=slots_dram, out_offset=bass.IndirectOffsetOnAxis(ap=idx_st[0:NODES, i:i + 1], axis=0),
                            in_=pair_st[0:NODES, i, :], in_offset=None).then_inc(scattered[i], 16)

                scatter(0)
                with pool.Fori(1, EC // 4) as it:
                    scatter(it)

                pool.wait_ge(fold2, KH * 8)
                for k in range(KH):
                    pool.tensor_copy(w2_hi[:, k, :], w2_raw[:, k, :]).then_inc(w2_hi_done, 1)
                pool.wait_ge(w2_hi_done, KH)
                pool.tensor_tensor(w2_lo[:, :, :], w2_raw[:, :, :], w2_hi[:, :, :].bitcast(F32),
                                   ALU.subtract).then_inc(w2_lo_done, 1)

                for i in range(4):
                    pool.wait_ge(scattered[i], 16 * (EC // 4))
                pool.wait_ge(w2_lo_done, 1)
                pool.wait_ge(h1_done, TILES)
                for u in range(2):
                    pool.wait_ge(stored1[u], 16 * HALF)
                for u in range(2):
                    pool.memset(G[u][:, :, :], 0.0)
                pool.memset(GO[:, :], 0.0).then_inc(cleared, 1)
                pool.wait_ge(cleared, 1)
                pool.wait_ge(ov_ready, 1)
                pool.wait_ge(meta_in, 16)
                total = pool.snap(pool.value_load(ov_start[0:1, TILES:TILES + 1], min_val=0, max_val=SLOTS - MAIN))

                pool.sem_inc(ov1_masked, 1)
                pool.sem_inc(ov2_agg, 1)

                def gather(s, table):
                    counted = early(pool, s.T + 1)
                    pool.tensor_copy(gidx[s.u][:, :], slot_meta[:, ds(2 * s.t, 2), 0]).then_inc(index_staged, 1)
                    alone(pool, index_staged, counted)
                    for c in range(2):
                        pool.indirect_dma_start(
                            out=G[s.u][:, c, :], out_offset=None, in_=table,
                            in_offset=bass.IndirectOffsetOnAxis(ap=gidx[s.u][:, c:c + 1], axis=0),
                            bounds_check=ROWS - 1, oob_is_err=False).then_inc(gathered[s.u][c], 16)

                def gather_overflow(s, table):
                    a, b, off = overflow(pool, s, total)

                    def one(g, nth):
                        counted = early(pool, nth + 1)
                        pool.tensor_copy(goidx[:, :], slot_meta[:, ds(g + MAIN, 1), 0]).then_inc(ov_staged, 1)
                        alone(pool, ov_staged, counted)
                        pool.indirect_dma_start(
                            out=GO[:, :], out_offset=None, in_=table,
                            in_offset=bass.IndirectOffsetOnAxis(ap=goidx[:, 0:1], axis=0),
                            bounds_check=ROWS - 1, oob_is_err=False).then_inc(ov_in, 16)

                    with each(pool, a, b) as g:
                        alone(pool, ov2_agg, a + off + 1)
                        pool.wait_ge(ov1_masked, g + off + 1)
                        one(g, a + g + off * 2)
                    with each(pool, a, b) as g:
                        alone(pool, ov1_masked, b + off + 1)
                        pool.wait_ge(ov2_agg, g + off + 1)
                        one(g, b + g + off * 2)

                def mask(s):
                    for c in range(2):
                        pool.wait_ge(gathered[s.u][c], 16 * s.TH + 16)
                    wait(pool, maskedT, s.T)
                    pool.wait_ge(nomatch, s.T + 1)
                    full = [P, 2, HEADS, P]
                    pool.tensor_tensor(AM[:, :, :, :], NM[:, :, :].unsqueeze(2).to_broadcast(full),
                                       G[s.u][:, :, HC:HC + HEADS].unsqueeze(3).to_broadcast(full),
                                       ALU.add).then_inc(masked, 1)

                def bias_x(s):
                    pool.wait_ge(xc_in[s.u], 16 * s.h + 16)
                    pool.tensor_tensor(xc[s.u][:, :], xc[s.u][:, :], bfc_bc[:, :], ALU.add).then_inc(x_biased, 1)

                def bias_x2(s):
                    pool.wait_ge(c_xn, s.t + 1)
                    pool.tensor_tensor(x2[s.u][:, :], x2[s.u][:, :], fb2_twice[:, :], ALU.add).then_inc(x2_biased, 1)

                def aggregation(table, stored, phase):
                    for u in range(2):
                        pool.wait_ge(stored[u], 16 * HALF)
                    for u in range(2):
                        gather(phase_tile(first(0, u), phase), table)
                    if phase:
                        pool.wait_ge(wc_lo_done, 3)
                        pool.memset(xc[0][:, :], 0.0)
                        pool.memset(xc[1][:, :], 0.0).then_inc(xc_cleared, 1)
                        pool.wait_ge(c_const, 1)

                    def body(s, more):
                        t = s
                        s = phase_tile(s, phase)
                        mask(s)
                        gather_overflow(s, table)
                        if more and not last_but_one(t):
                            pool.wait_ge(scaled_lo, 8 * s.T + 8)
                            gather(phase_tile(Tile(s.t + 2, s.h + 1, s.u), phase), table)
                        if phase:
                            if not is_zero(t.t):
                                bias_x2(before(t))
                            bias_x(t)

                    over_tiles(pool, body)
                    if phase:
                        bias_x2(first(HALF - 1, 1))

                aggregation(table1, stored1, 0)
                aggregation(table2, stored2, 1)

            @block.tensor
            def _(pe):
                pe.wait_ge(consts, 3)
                pe.wait_ge(count_done, 1)
                pe.matmul(bank[7][:, 0:TILES], tri[0:NODES, :], count_pt[0:NODES, :], start=True, stop=True)
                pe.matmul(bank[7][:, 128:128 + TILES], ones[0:NODES, :], count_pt[0:NODES, :],
                          start=True, stop=True).then_inc(pl_base, 1)
                pe.wait_ge(w1_hi_done, 1)
                pe.wait_ge(w1_lo_done, 1)

                def three(out, lhs, rhs, k, last, cols):
                    (l_hi, l_lo), (r_hi, r_lo) = lhs, rhs
                    for i, (l, r) in enumerate(((l_hi, r_hi), (l_hi, r_lo), (l_lo, r_hi))):
                        for o, (a, b) in zip(out, cols):
                            ins = pe.matmul(o, l[:, k, :], r[:, k, a:b], start=(k == 0 and i == 0),
                                            stop=(k == last and i == 2), skip_group_check=True)
                    return ins

                thirds = [(i * W3, (i + 1) * W3) for i in range(3)]

                def turn(s):
                    pe.wait_ge(xna_ready, s.t + 1)
                    wait(pe, xTa_hi, s.t - 1)
                    wait(pe, xTa_lo, s.t - 1)
                    for k in range(KD):
                        ins = pe.transpose(bank[s.u][:, k * P:(k + 1) * P], xna[s.u][:, k * P:(k + 1) * P], ident[:, :])
                    ins.then_inc(xa_turned, 1)

                def product(s):
                    pe.wait_ge(xTa_hi, s.t + 1)
                    pe.wait_ge(xTa_lo, s.t + 1)
                    wait(pe, h1_act, 2 * s.t - 2)
                    wait(pe, h1_dve, s.t - 1)
                    for k in range(KD):
                        ins = three([bank[2 + 3 * s.u + i][:, 0:W3] for i in range(3)], xTa[s.u], (w1_hi, w1_lo), k,
                                    KD - 1, thirds)
                    ins.then_inc(h1_done, 1)

                pe.wait_ge(placed, 1)
                turn(first(0, 0))

                def a_body(s, more):
                    if more:
                        turn(after(s))
                    product(s)

                over_tiles(pe, a_body)

                def turn_masked(s):
                    pe.wait_ge(masked, s.T + 1)
                    for c in range(2):
                        for h in range(HEADS):
                            ins = pe.transpose(bank[c][:, h * P:(h + 1) * P], AM[:, c, h, :], ident[:, :])
                    ins.then_inc(maskedT, 1)
                    for c in range(2):
                        ins = pe.transpose(ohT_ps[:, c, :], OH[s.u][:, c, :].bitcast(F32), ident[:, :])
                    ins.then_inc(onehotT, 1)
                    a, b, off = overflow(pe, s, total)
                    with each(pe, a, b) as g:
                        pe.wait_ge(ov1_masked, g + off + 2)
                        for h in range(HEADS):
                            ins = pe.transpose(bank[0][:, h * P:(h + 1) * P], AMo[:, h, :], ident[:, :])
                        ins.then_inc(ov1_T, 1)

                def target_values(s):
                    pe.wait_ge(shift_ready, 2 * s.T + 2)
                    pe.wait_ge(onehotT_copied, s.T + 1)
                    for c in range(2):
                        ins = pe.matmul(edge_ps[:, c, :], ohT[:, c, :], rhs8, start=True, stop=True)
                    ins.then_inc(edge_rhs, 1)

                def aggregate(s):
                    pe.wait_ge(edge_weight, s.T + 1)
                    for c in range(2):
                        ins = pe.matmul(den_ps, OH[s.u][:, c, :].bitcast(F32), w[:, c, :], start=(c == 0), stop=(c == 1))
                    ins.then_inc(den_done, 1)
                    for c in range(2):
                        pe.wait_ge(scaled_lo, 8 * s.T + 4 * c + 4)
                        for i, part in enumerate(GS):
                            for half in range(2):
                                ins = pe.matmul(bank[3 + half][:, :], OH[s.u][:, c, :], part[:, c, half * 512:half * 512 + 512],
                                                start=(c == 0 and i == 0), stop=True, skip_group_check=True)
                    ins.then_inc(aggregated, 1)
                    a, b, off = overflow(pe, s, total)
                    with each(pe, a, b) as g:
                        pe.wait_ge(ov2_onehot, g + off + 1)
                        pe.transpose(ohT_o_ps, OHo[:, :].bitcast(F32), ident[:, :]).then_inc(ov2_T, 1)
                        pe.wait_ge(ov2_copied, g + off + 1)
                        pe.matmul(edge_o_ps, ohTo[:, :], rhs8, start=True, stop=True).then_inc(ov2_rhs, 1)
                        pe.wait_ge(ov2_lo, (g + off) * 4 + 4)
                        for part in GS:
                            for half in range(2):
                                pe.matmul(bank[3 + half][:, :], OHo[:, :], part[:, 0, half * 512:half * 512 + 512],
                                          start=False, stop=True, skip_group_check=True)
                        pe.matmul(den_o_ps, OHo[:, :].bitcast(F32), wo, start=True, stop=True).then_inc(ov2_agg, 1)

                def turn_mixed(s):
                    for half in range(2):
                        pe.wait_ge(mix_done, 4 * s.T + 2 + 2 * half)
                        for k in range(4):
                            c = 4 * half + k
                            ins = pe.transpose(bank[3 + half][:, k * P:(k + 1) * P], mixed[:, c * P:(c + 1) * P], ident[:, :])
                        ins.then_inc(mixedT, 1)

                def dense(s, ks):
                    if ks[0] == 0:
                        wait(pe, h2_act, 2 * s.T)
                        wait(pe, h2_dve, s.T)
                    for k in ks:
                        if k % 4 == 0:
                            pe.wait_ge(relu_hi, 2 * s.T + 1 + k // 4)
                            pe.wait_ge(relu_lo, 2 * s.T + 1 + k // 4)
                        ins = three([bank[5 + i][:, 0:W3] for i in range(3)], hT, (w2_hi, w2_lo), k, KH - 1, thirds)
                    if ks[-1] == KH - 1:
                        ins.then_inc(dense_done, 1)

                def prepare(s):
                    turn_masked(s)
                    target_values(s)
                    aggregate(s)
                    turn_mixed(s)

                pe.wait_ge(h1_act, 2 * TILES)
                pe.wait_ge(h1_dve, TILES)
                pe.wait_ge(ov_ready, 1)
                pe.wait_ge(w2_hi_done, KH)
                pe.wait_ge(w2_lo_done, 1)
                total = pe.snap(pe.value_load(ov_start[0:1, TILES:TILES + 1], min_val=0, max_val=SLOTS - MAIN))
                prepare(phase_tile(first(0, 0), 0))

                def b_body(s, more):
                    n = phase_tile(after(s), 0)
                    s = phase_tile(s, 0)
                    if more:
                        turn_masked(n)
                    dense(s, range(0, 3))
                    if more:
                        target_values(n)
                    dense(s, range(3, 6))
                    if more:
                        aggregate(n)
                    dense(s, range(6, KH))
                    if more:
                        turn_mixed(n)

                over_tiles(pe, b_body)

                pe.wait_ge(h2_act, 2 * TILES)
                pe.wait_ge(h2_dve, TILES)
                pe.wait_ge(bias_in, 16 * 3)
                pe.matmul(bank[7][:, :], ones_ex[:, :], fb2_sb[:, :], start=True, stop=True).then_inc(fb2_sum, 1)
                prepare(phase_tile(first(0, 0), 1))
                pe.wait_ge(wc_hi_done, 3)
                pe.wait_ge(wc_lo_done, 3)
                pe.wait_ge(c_const, 1)

                def connect(s, ks):
                    for k in ks:
                        if k % 4 == 0:
                            pe.wait_ge(relu_hi, 2 * s.T + 1 + k // 4)
                            pe.wait_ge(relu_lo, 2 * s.T + 1 + k // 4)
                        ins = three([bank[5][:, :]], hT, (wfc_hi, wfc_lo), k, KH - 1, [(0, D)])
                    if ks[-1] == KH - 1:
                        ins.then_inc(fc_done, 1)

                def turn_gelu(s):
                    pe.wait_ge(gsum_done, s.t + 1)
                    for k in range(KF):
                        ins = pe.transpose(bank[7][:, k * P:(k + 1) * P], gsum[:, k * P:(k + 1) * P], ident[:, :])
                    ins.then_inc(c_gT, 1)

                def ffn_out(s):
                    pe.wait_ge(gT_hi, s.t + 1)
                    pe.wait_ge(gT_lo, s.t + 1)
                    for k in range(KF):
                        ins = three([bank[6][:, :]], gT, (f2_hi, f2_lo), k, KF - 1, [(0, D)])
                    ins.then_inc(f2_done, 1)

                def c_body(s, more):
                    n = phase_tile(after(s), 1)
                    s = phase_tile(s, 1)
                    if more:
                        turn_masked(n)
                    connect(s, range(0, 4))
                    if more:
                        target_values(n)
                    if not is_zero(s.t):
                        turn_gelu(before(s))
                    connect(s, range(4, KH))
                    if not is_zero(s.t):
                        ffn_out(before(s))
                    if more:
                        aggregate(n)
                    pe.wait_ge(c_xn, s.t + 1)
                    for k in range(KD):
                        ins = pe.transpose(bank[5][:, k * P:(k + 1) * P], xn2[:, k * P:(k + 1) * P], ident[:, :])
                    ins.then_inc(c_xT, 1)
                    if more:
                        turn_mixed(n)
                    pe.wait_ge(xT2_hi, s.t + 1)
                    pe.wait_ge(xT2_lo, s.t + 1)
                    wait(pe, out_sum, s.t)
                    for k in range(KD):
                        ins = three([bank[6][:, 0:F2W], bank[7][:, 0:F2W]], xT2, (f1_hi, f1_lo), k, KD - 1,
                                    [(0, F2W), (F2W, FG)])
                    ins.then_inc(f1_done, 1)

                over_tiles(pe, c_body)
                turn_gelu(first(HALF - 1, 1))
                ffn_out(first(HALF - 1, 1))

            @block.vector
            def _(v):
                pl = Count()

                def step(ins):
                    ins.then_inc(placing, 1)
                    pl.n += 1

                def settle():
                    v.wait_ge(placing, pl.n)

                e = lambda i: ef[0:NODES, i, :]
                n_ = NODES
                v.wait_ge(consts, 3)
                v.wait_ge(edges_in, 32)
                step(v.tensor_copy(e(0), dst_i[0:n_, :]))
                step(v.tensor_copy(e(1), src_i[0:n_, :]))
                settle()

                def split(node, tile, rest, tmp_i):
                    step(v.tensor_scalar(tmp_i, node, 1.0 / NODES, None, ALU.mult))
                    settle()
                    step(v.tensor_copy(tile, tmp_i))
                    settle()
                    step(v.scalar_tensor_tensor(rest, tile, -float(NODES), node, ALU.mult, ALU.add))
                    settle()
                    step(v.tensor_scalar(e(9), rest, 0.0, None, ALU.is_lt))
                    step(v.tensor_scalar(e(8), rest, float(NODES), None, ALU.is_ge))
                    settle()
                    step(v.tensor_tensor(tile, tile, e(9), ALU.subtract))
                    settle()
                    step(v.tensor_tensor(tile, tile, e(8), ALU.add))
                    settle()
                    step(v.scalar_tensor_tensor(rest, tile, -float(NODES), node, ALU.mult, ALU.add))
                    settle()

                split(e(0), e(2), e(3), ei[0:n_, 0, :])
                split(e(1), e(4), e(5), ei[0:n_, 1, :])
                step(v.scalar_tensor_tensor(pairs[0:n_, :, 0], e(4), float(P), e(5), ALU.mult, ALU.add))
                step(v.tensor_copy(pairs[0:n_, :, 1], e(3)))
                full = [n_, EC, TILES]
                step(v.tensor_tensor(onehot_t[0:n_, :, :], e(2).unsqueeze(2).to_broadcast(full),
                                     iota_tile[0:n_, :].unsqueeze(1).to_broadcast(full), ALU.is_equal))
                settle()
                v.tensor_reduce(count_pt[0:n_, :], onehot_t[0:n_, :, :].rearrange("p c t -> p t c"), AX.X,
                                ALU.add).then_inc(count_done, 1)
                full = [n_, EC, EC]
                step(v.tensor_tensor(same[0:n_, :, :], e(2).unsqueeze(2).to_broadcast(full),
                                     e(2).unsqueeze(1).to_broadcast(full), ALU.is_equal))
                settle()
                step(v.tensor_tensor(same[0:n_, :, :], same[0:n_, :, :], earlier[0:n_, :, :], ALU.mult))
                settle()
                step(v.tensor_reduce(e(6), same[0:n_, :, :], AX.X, ALU.add))
                v.wait_ge(pl_base, 1)
                step(v.tensor_scalar(base_t[:, 0, :], bank[7][:, 128:128 + TILES], -float(P + 1), 0.0, ALU.add, ALU.max))
                settle()
                step(v.tensor_copy(ov_i[:, 0, :], base_t[:, 0, :]))
                settle()
                step(v.tensor_scalar(ov_i[:, 1, :], ov_i[:, 0, :], 7, None, ALU.arith_shift_right))
                settle()
                step(v.tensor_copy(base_t[:, 1, :], ov_i[:, 1, :]))
                settle()
                step(v.tensor_copy(scan[:, 0, :], base_t[:, 1, :]))
                settle()
                cur, d = 0, 1
                while d < TILES:
                    step(v.tensor_copy(scan[:, 1 - cur, 0:d], scan[:, cur, 0:d]))
                    step(v.tensor_tensor(scan[:, 1 - cur, d:TILES], scan[:, cur, d:TILES],
                                         scan[:, cur, 0:TILES - d], ALU.add))
                    settle()
                    cur, d = 1 - cur, 2 * d
                step(v.memset(ov_start[0:1, :], 0))
                settle()
                v.tensor_copy(ov_start[0:1, 1:TILES + 1], scan[0:1, cur, :]).then_inc(ov_ready, 1)
                step(v.tensor_tensor(base_t[:, 2, :], scan[:, cur, :], base_t[:, 1, :], ALU.subtract))
                for to, what in ((7, bank[7][0:n_, 0:TILES]), (8, base_t[0:n_, 2, :])):
                    settle()
                    full = [n_, EC, TILES]
                    step(v.tensor_copy(base_t[0:n_, 0, :], what))
                    settle()
                    hi_i, lo_f, hi_f = ov_i[0:n_, 0, :], base_t[0:n_, 0, :], base_t[0:n_, 1, :]
                    step(v.tensor_copy(hi_i, lo_f))
                    settle()
                    step(v.tensor_scalar(ov_i[0:n_, 1, :], hi_i, 7, None, ALU.arith_shift_right))
                    settle()
                    step(v.tensor_copy(hi_f, ov_i[0:n_, 1, :]))
                    settle()
                    step(v.scalar_tensor_tensor(lo_f, hi_f, -128.0, lo_f, ALU.mult, ALU.add))
                    settle()
                    for part, dest in ((lo_f, e(to)), (hi_f, e(9))):
                        step(v.tensor_tensor(lookup[0:n_, :, :], onehot_t[0:n_, :, :],
                                             part.unsqueeze(1).to_broadcast(full), ALU.mult))
                        settle()
                        step(v.tensor_reduce(dest, lookup[0:n_, :, :], AX.X, ALU.add))
                        settle()
                    step(v.scalar_tensor_tensor(e(to), e(9), 128.0, e(to), ALU.mult, ALU.add))
                    settle()
                step(v.tensor_tensor(e(6), e(6), e(7), ALU.add))
                settle()
                step(v.tensor_copy(ei[0:n_, 0, :], e(6)))
                settle()
                step(v.tensor_scalar(ei[0:n_, 1, :], ei[0:n_, 0, :], 7, None, ALU.arith_shift_right))
                step(v.tensor_scalar(ei[0:n_, 2, :], ei[0:n_, 0, :], P - 1, None, ALU.bitwise_and))
                settle()
                step(v.tensor_copy(e(0), ei[0:n_, 1, :]))
                step(v.tensor_copy(e(1), ei[0:n_, 2, :]))
                settle()
                step(v.scalar_tensor_tensor(e(7), e(2), -2.0, e(8), ALU.mult, ALU.add))
                step(v.tensor_scalar(e(5), e(0), 2.0, None, ALU.is_ge))
                step(v.scalar_tensor_tensor(e(4), e(2), 2.0, e(0), ALU.mult, ALU.add))
                settle()
                step(v.tensor_scalar(e(7), e(7), float(MAIN - 2), None, ALU.add))
                settle()
                step(v.tensor_tensor(e(7), e(7), e(5), ALU.mult))
                settle()
                step(v.tensor_tensor(e(4), e(4), e(7), ALU.add))
                settle()
                v.scalar_tensor_tensor(slot_idx[0:n_, :], e(1), float(SLOTS), e(4), ALU.mult,
                                       ALU.add).then_inc(placed, 1)
                v.wait_ge(placed, 1)
                v.tensor_copy(e(0), e(1)).then_inc(placed, 1)

                def fold(w_sb, k_all, which, done):
                    for k in range(k_all):
                        for j in range(2):
                            for h in range(HEADS):
                                i = (k * 2 + j) * HEADS + h
                                wait(v, done, i)
                                v.tensor_tensor_reduce(
                                    fold_out[:, :], w_sb[:, k, h * C:(h + 1) * C],
                                    a_bc[:, which + j, h * C:(h + 1) * C], 1.0, 0.0, ALU.mult, ALU.add,
                                    w_sb[:, k, HC + j * HEADS + h:HC + j * HEADS + h + 1]).then_inc(done, 1)

                v.wait_ge(w1_in, 16 * 5)
                fold(w1_raw, KD, 0, fold1)
                v.wait_ge(w2_in, 16 * 3)
                v.wait_ge(fold1, KD * 8)
                fold(w2_raw, KH, 2, fold2)
                v.wait_ge(w1_hi_done, 1)
                v.tensor_tensor(w1_lo[:, :, :], w1_raw[:, :, :], w1_hi[:, :, :].bitcast(F32),
                                ALU.subtract).then_inc(w1_lo_done, 1)

                def inverse_root(stat, sem_, n):
                    a, y, t = stat[:, 7:8], stat[:, 8:9], stat[:, 9:10]
                    ops = [lambda: v.tensor_scalar(a, a, EPS, None, ALU.add),
                           lambda: v.tensor_scalar(t.bitcast(I32), a.bitcast(I32), 1, None, ALU.arith_shift_right),
                           lambda: v.tensor_scalar(y.bitcast(I32), t.bitcast(I32), -1.0, float(0x5f3759df),
                                                   ALU.mult, ALU.add)]
                    ops += [lambda: v.scalar_tensor_tensor(t, y, a, y, ALU.mult, ALU.mult),
                            lambda: v.tensor_scalar(t, t, -0.5, 1.5, ALU.mult, ALU.add),
                            lambda: v.tensor_tensor(y, y, t, ALU.mult)] * 3
                    for i, op in enumerate(ops):
                        op().then_inc(sem_, 1)
                        v.wait_ge(sem_, n + i + 1)

                def normalise(xt, xn, stat, sem_, n, done):
                    counted = early(v, n + 1)
                    v.bn_stats(stat[:, 0:6], xt).then_inc(sem_, 1)
                    alone(v, sem_, counted)
                    v.bn_aggr(stat[:, 6:8], stat[:, 0:6]).then_inc(sem_, 1)
                    v.wait_ge(sem_, n + 2)
                    inverse_root(stat, sem_, n + 2)
                    v.tensor_scalar(xn, xt, stat[:, 6:7], stat[:, 8:9], ALU.subtract, ALU.mult).then_inc(done, 1)

                def a_norm(s):
                    v.wait_ge(xa_in[s.u], 16 * s.h + 16)
                    wait(v, xa_turned, s.t - 1)
                    wait(v, xna_ready, s.t)
                    normalise(xa[s.u][:, :], xna[s.u][:, :], stat_a, a_stats, 14 * s.t, xna_ready)

                def low_part(out, turned, high):
                    return v.tensor_tensor(out.rearrange("p k n -> p (k n)"), turned,
                                           high.rearrange("p k n -> p (k n)").bitcast(F32), ALU.subtract)

                def a_low(s):
                    v.wait_ge(xTa_hi, s.t + 1)
                    wait(v, h1_done, s.t - 1)
                    low_part(xTa[s.u][1][:, :, :], bank[s.u][:, :], xTa[s.u][0][:, :, :]).then_inc(xTa_lo, 1)

                def a_evict(s):
                    v.wait_ge(h1_done, s.t + 1)
                    wait(v, stored1[s.u], 16 * s.h)
                    v.tensor_copy(rowa[s.u][:, 2 * W3:ROW], bank[4 + 3 * s.u][:, 0:W3]).then_inc(h1_dve, 1)

                a_norm(first(0, 0))
                a_norm(first(0, 1))
                a_low(first(0, 0))

                def a_body(s, more):
                    if more and not last_but_one(s):
                        a_norm(after(after(s)))
                    if more:
                        a_low(after(s))
                    a_evict(s)

                over_tiles(v, a_body)
                v.wait_ge(meta_in, 16)
                v.tensor_copy(slot_loc[:, :], slot_meta[:, :, 1]).then_inc(meta_ready, 1)
                v.wait_ge(meta_ready, 1)
                total = v.snap(v.value_load(ov_start[0:1, TILES:TILES + 1], min_val=0, max_val=SLOTS - MAIN))

                def al_src(row):
                    return row[:, HC:HC + HEADS]

                def al_dst(row):
                    return row[:, HC + HEADS:ROW]

                def match(s):
                    wait(v, aggregated, s.T - 1)
                    full = [P, 2, P]
                    v.tensor_tensor(OH[s.u][:, :, :], iota_node[:, :].unsqueeze(1).to_broadcast(full),
                                    slot_loc[:, ds(2 * s.t, 2)].unsqueeze(2).to_broadcast(full),
                                    ALU.is_equal).then_inc(onehot, 1)
                    v.wait_ge(onehot, s.T + 1)
                    wait(v, masked, s.T)
                    v.tensor_scalar(NM[:, :, :], OH[s.u][:, :, :].bitcast(F32), BIG, -BIG, ALU.mult,
                                    ALU.add).then_inc(nomatch, 1)

                def maximum(s):
                    a, b, off = overflow(v, s, total)
                    v.wait_ge(maskedT, s.T + 1)
                    for c in range(2):
                        v.tensor_reduce(mx2[:, c, :],
                                        bank[c][:, :].rearrange("p (h e) -> p h e", h=HEADS), AX.X,
                                        ALU.max).then_inc(edge_max, 1)
                    v.wait_ge(edge_max, 3 * s.T + 2)
                    counted = early(v, 3 * s.T + 3)
                    v.tensor_tensor(mx, mx2[:, 0, :], mx2[:, 1, :], ALU.max).then_inc(edge_max, 1)
                    alone(v, edge_max, counted)
                    with each(v, a, b) as g:
                        v.wait_ge(ov_in, (a + g + off * 2 + 1) * 16)
                        mask_overflow(g, off, 1)
                        v.wait_ge(ov1_T, g + off + 1)
                        v.tensor_reduce(mxo, bank[0][:, :].rearrange("p (h e) -> p h e", h=HEADS), AX.X,
                                        ALU.max).then_inc(ov1_max, 1)
                        v.wait_ge(ov1_max, (g + off) * 2 + 1)
                        v.tensor_tensor(mx, mx, mxo, ALU.max).then_inc(ov1_max, 1)
                        v.wait_ge(ov1_max, (g + off) * 2 + 2)
                    v.wait_ge(self_in[s.u], 16 * s.TH + 16)
                    als, ald = al_src(H[s.u]), al_dst(H[s.u])
                    v.tensor_tensor(mx, mx, als, ALU.max).then_inc(node_max, 1)
                    v.wait_ge(node_max, s.T + 1)
                    v.tensor_tensor(lsum, mx, ald, ALU.add).then_inc(lgt_sum, 1)
                    v.wait_ge(lgt_sum, s.T + 1)
                    v.tensor_copy(rhs8[:, 0:4], ald).then_inc(shift_ready, 1)
                    v.scalar_tensor_tensor(rhs8[:, 4:8], lsum, SLOPE, lsum, ALU.mult, ALU.max).then_inc(shift_ready, 1)
                    v.tensor_tensor(selfz, als, ald, ALU.add).then_inc(self_logit, 1)
                    v.wait_ge(self_logit, 3 * s.T + 1)
                    v.scalar_tensor_tensor(selfz, selfz, SLOPE, selfz, ALU.mult, ALU.max).then_inc(self_logit, 1)
                    v.wait_ge(self_logit, 3 * s.T + 2)
                    v.wait_ge(shift_ready, 2 * s.T + 2)
                    v.tensor_tensor(selfz, selfz, rhs8[:, 4:8], ALU.subtract).then_inc(self_logit, 1)

                def mask_overflow(g, off, which):
                    v.tensor_tensor(OHo[:, :], iota_node[:, :],
                                    slot_loc[:, ds(g + MAIN, 1)].to_broadcast([P, P]),
                                    ALU.is_equal).then_inc(ov1_dve if which == 1 else ov2_onehot, 1)
                    if which == 1:
                        v.wait_ge(ov1_dve, (g + off) * 2 + 1)
                        v.tensor_scalar(NMo[:, :], OHo[:, :].bitcast(F32), BIG, -BIG, ALU.mult, ALU.add).then_inc(ov1_dve, 1)
                        v.wait_ge(ov1_dve, (g + off) * 2 + 2)
                        full = [P, HEADS, P]
                        v.tensor_tensor(AMo[:, :, :], NMo[:, :].unsqueeze(1).to_broadcast(full),
                                        al_src(GO).unsqueeze(2).to_broadcast(full), ALU.add).then_inc(ov1_masked, 1)

                def logits(zt, als, per_target, sem_, n):
                    v.tensor_tensor(zt, als, per_target[0], ALU.add).then_inc(sem_, 1)
                    v.wait_ge(sem_, n + 1)
                    v.scalar_tensor_tensor(zt, zt, SLOPE, zt, ALU.mult, ALU.max).then_inc(sem_, 1)
                    v.wait_ge(sem_, n + 2)
                    v.tensor_tensor(zt, zt, per_target[1], ALU.subtract).then_inc(sem_, 1)
                    v.wait_ge(sem_, n + 3)
                    v.tensor_scalar(zt, zt, 0.0, None, ALU.min).then_inc(sem_, 1)

                def edge_logits(s):
                    v.wait_ge(edge_rhs, s.T + 1)
                    logits(z, G[s.u][:, :, HC:HC + HEADS], (edge_ps[:, :, 0:4], edge_ps[:, :, 4:8]), edge_logit, 4 * s.T)

                def scale_low(s):
                    v.wait_ge(edge_weight, s.T + 1)
                    wait(v, aggregated, s.T)
                    for c in range(2):
                        for h in range(HEADS):
                            cols = slice(h * C, (h + 1) * C)
                            v.wait_ge(scaled_hi, 8 * s.T + 4 * c + h + 1)
                            v.scalar_tensor_tensor(GS[1][:, c, cols], G[s.u][:, c, cols], w[:, c, h:h + 1],
                                                   GS[0][:, c, cols].bitcast(F32), ALU.mult,
                                                   ALU.subtract).then_inc(scaled_lo, 1)

                def mix(s, bias):
                    a, b, off = overflow(v, s, total)
                    counted = early(v, s.T + 1)
                    v.wait_ge(den_done, s.T + 1)
                    v.wait_ge(self_weight, s.T + 1)
                    v.tensor_tensor(dsum, den_ps, wself, ALU.add).then_inc(den_total, 1)
                    alone(v, den_total, counted)
                    with each(v, a, b) as g:
                        v.wait_ge(ov_in, (b + g + off * 2 + 1) * 16)
                        mask_overflow(g, off, 2)
                        v.wait_ge(ov2_T, g + off + 1)
                        v.tensor_copy(ohTo[:, :], ohT_o_ps).then_inc(ov2_copied, 1)
                        v.wait_ge(ov2_rhs, g + off + 1)
                        logits(zo, al_src(GO), (edge_o_ps[:, 0:4], edge_o_ps[:, 4:8]), ov2_logit, (g + off) * 4)
                        v.wait_ge(ov2_weight, g + off + 1)
                        v.wait_ge(aggregated, s.T + 1)
                        for h in range(HEADS):
                            cols = slice(h * C, (h + 1) * C)
                            v.wait_ge(ov2_hi, (g + off) * 4 + h + 1)
                            v.scalar_tensor_tensor(GS[1][:, 0, cols], GO[:, cols], wo[:, h:h + 1],
                                                   GS[0][:, 0, cols].bitcast(F32), ALU.mult,
                                                   ALU.subtract).then_inc(ov2_lo, 1)
                        v.wait_ge(ov2_agg, g + off + 2)
                        v.tensor_tensor(dsum, dsum, den_o_ps, ALU.add).then_inc(ov2_den, 1)
                        v.wait_ge(ov2_den, g + off + 1)
                    v.reciprocal(rden, dsum).then_inc(den_inv, 1)
                    v.wait_ge(den_inv, s.T + 1)
                    v.tensor_tensor(wsn, wself, rden, ALU.mult).then_inc(self_scale, 1)
                    v.wait_ge(self_scale, s.T + 1)
                    for h in range(HEADS):
                        cols = slice(h * C, (h + 1) * C)
                        v.scalar_tensor_tensor(mixed[:, cols], H[s.u][:, cols], wsn[:, h:h + 1], bias[:, cols],
                                               ALU.mult, ALU.add).then_inc(self_scaled, 1)
                    v.wait_ge(aggregated, s.T + 1)
                    for h in range(HEADS):
                        cols = slice(h * C, (h + 1) * C)
                        v.wait_ge(self_scaled, 4 * s.T + h + 1)
                        v.scalar_tensor_tensor(mixed[:, cols], bank[3 + h // 2][:, (h % 2) * C:(h % 2 + 1) * C],
                                               rden[:, h:h + 1], mixed[:, cols], ALU.mult, ALU.add).then_inc(mix_done, 1)

                def relu_low(s):
                    for half in range(2):
                        v.wait_ge(relu_hi, 2 * s.T + 1 + half)
                        ks = slice(4 * half, 4 * half + 4)
                        v.scalar_tensor_tensor(hT[1][:, ks, :].rearrange("p k n -> p (k n)"), bank[3 + half][:, :], 0.0,
                                               hT[0][:, ks, :].rearrange("p k n -> p (k n)").bitcast(F32), ALU.max,
                                               ALU.subtract).then_inc(relu_lo, 1)

                def prepare(s, bias):
                    match(s)
                    maximum(s)
                    edge_logits(s)
                    match(phase_tile(first(0, 1), s.phase))
                    scale_low(s)
                    mix(s, bias)
                    relu_low(s)

                prepare(phase_tile(first(0, 0), 0), b1_bc)

                def b_body(s, more):
                    n = phase_tile(after(s), 0)
                    if more:
                        maximum(n)
                        edge_logits(n)
                        if not last_but_one(s):
                            match(phase_tile(after(after(s)), 0))
                        scale_low(n)
                        mix(n, b1_bc)
                    v.wait_ge(dense_done, s.t + 1)
                    wait(v, stored2[s.u], 16 * s.h)
                    v.tensor_copy(rowb[s.u][:, 2 * W3:ROW], bank[7][:, 0:W3]).then_inc(h2_dve, 1)
                    if more:
                        relu_low(n)

                over_tiles(v, b_body)

                for i, (lo, raw, hi) in enumerate(((wfc_lo, wfc_raw, wfc_hi), (f1_lo, f1_raw, f1_hi),
                                                   (f2_lo, f2_raw, f2_hi))):
                    v.wait_ge(wc_hi_done, i + 1)
                    v.tensor_tensor(lo[:, :, :], raw[:, :, :], hi[:, :, :].bitcast(F32),
                                    ALU.subtract).then_inc(wc_lo_done, 1)
                v.wait_ge(fb2_sum, 1)
                v.tensor_scalar(fb2_twice[:, :], bank[7][:, :], 2.0, None, ALU.mult).then_inc(c_const, 1)
                v.wait_ge(c_const, 1)
                prepare(phase_tile(first(0, 0), 1), b2_bc)

                def gelu_sum(s):
                    v.wait_ge(gelu_done, s.t + 1)
                    v.tensor_tensor(gsum[:, :], ffn_v[:, 0, :], ffn_v[:, 1, :], ALU.add).then_inc(gsum_done, 1)

                def gelu_low(s):
                    v.wait_ge(gT_hi, s.t + 1)
                    low_part(gT[1][:, :, :], bank[7][:, :], gT[0][:, :, :]).then_inc(gT_lo, 1)

                def finish_tile(s):
                    v.wait_ge(f2_done, s.t + 1)
                    v.wait_ge(x2_biased, s.t + 1)
                    wait(v, out_stored[s.u], 16 * s.h)
                    v.tensor_tensor(outb[s.u][:, :], bank[6][:, :], x2[s.u][:, :], ALU.add).then_inc(out_sum, 1)

                def c_body(s, more):
                    n = phase_tile(after(s), 1)
                    if more:
                        maximum(n)
                    if not is_zero(s.t):
                        gelu_sum(before(s))
                    if more:
                        edge_logits(n)
                        if not last_but_one(s):
                            match(phase_tile(after(after(s)), 1))
                        scale_low(n)
                    if not is_zero(s.t):
                        gelu_low(before(s))
                    v.wait_ge(fc_done, s.t + 1)
                    v.wait_ge(x_biased, s.t + 1)
                    v.tensor_tensor(x2[s.u][:, :], bank[5][:, :], xc[s.u][:, :], ALU.add).then_inc(c_x2, 1)
                    v.wait_ge(c_x2, s.t + 1)
                    normalise(x2[s.u][:, :], xn2[:, :], stat_c, c_stats, 14 * s.t, c_xn)
                    if not is_zero(s.t):
                        finish_tile(before(s))
                    if more:
                        mix(n, b2_bc)
                    v.wait_ge(xT2_hi, s.t + 1)
                    low_part(xT2[1][:, :, :], bank[5][:, :], xT2[0][:, :, :]).then_inc(xT2_lo, 1)
                    if more:
                        relu_low(n)
                    alone(v, f1_done, s.t + 1)
                    v.max(m8, gate_ps).then_inc(c_top, 1)
                    v.wait_ge(c_top, 2 * s.t + 1)
                    v.tensor_scalar(nmax, m8[:, 0:1], -1.0, None, ALU.mult).then_inc(c_top, 1)
                    v.wait_ge(c_exp, s.t + 1)
                    v.reciprocal(rsum, esum).then_inc(c_prob, 1)
                    v.wait_ge(c_prob, 5 * s.t + 1)
                    v.tensor_scalar(e8, e8, rsum, None, ALU.mult).then_inc(c_prob, 1)
                    v.wait_ge(c_prob, 5 * s.t + 2)
                    v.tensor_tensor(s2, e8[:, 0:1], e8[:, 1:2], ALU.add).then_inc(c_prob, 1)
                    v.wait_ge(c_prob, 5 * s.t + 3)
                    v.reciprocal(s2, s2).then_inc(c_prob, 1)
                    v.wait_ge(c_prob, 5 * s.t + 4)
                    v.tensor_scalar(p2, e8[:, 0:2], s2, None, ALU.mult).then_inc(c_prob, 1)
                    v.wait_ge(c_prob, 5 * s.t + 5)
                    for i in range(2):
                        for b, a, z_ in ((6, 0, F2W), (7, F2W, FF)):
                            v.scalar_tensor_tensor(ffn_v[:, i, a:z_], bank[b][:, 0:z_ - a], p2[:, i:i + 1],
                                                   fb1_bc[:, a:z_], ALU.mult, ALU.add).then_inc(ffn_in, 1)

                over_tiles(v, c_body)
                gelu_sum(first(HALF - 1, 1))
                gelu_low(first(HALF - 1, 1))
                finish_tile(first(HALF - 1, 1))

            @block.scalar
            def _(act):
                def high_part(out, turned):
                    return act.copy(out.rearrange("p k n -> p (k n)"), turned)

                def turned(s):
                    act.wait_ge(xa_turned, s.t + 1)
                    wait(act, h1_done, s.t - 1)
                    high_part(xTa[s.u][0][:, :, :], bank[s.u][:, :]).then_inc(xTa_hi, 1)

                def a_body(s, more):
                    if more:
                        turned(after(s))
                    act.wait_ge(h1_done, s.t + 1)
                    wait(act, stored1[s.u], 16 * s.h)
                    for i in range(2):
                        act.copy(rowa[s.u][:, i * W3:(i + 1) * W3],
                                 bank[2 + 3 * s.u + i][:, 0:W3]).then_inc(h1_act, 1)

                act.wait_ge(fold1, KD * 8)
                act.copy(w1_hi[:, :, :].rearrange("p k n -> p (k n)"),
                         w1_raw[:, :, :].rearrange("p k n -> p (k n)")).then_inc(w1_hi_done, 1)
                turned(first(0, 0))
                over_tiles(act, a_body)
                act.wait_ge(ov_ready, 1)
                act.wait_ge(cleared, 1)
                total = act.snap(act.value_load(ov_start[0:1, TILES:TILES + 1], min_val=0, max_val=SLOTS - MAIN))

                def spread(s):
                    act.wait_ge(onehotT, s.T + 1)
                    act.copy(ohT[:, :, :].rearrange("p c e -> p (c e)"), small[:, 0:256]).then_inc(onehotT_copied, 1)
                    act.wait_ge(self_logit, 3 * s.T + 3)
                    act.activation(wself, selfz, ACT.Exp).then_inc(self_weight, 1)

                def weigh(s):
                    act.wait_ge(edge_logit, 4 * s.T + 4)
                    act.activation(w, z, ACT.Exp).then_inc(edge_weight, 1)

                def scale_high(s):
                    act.wait_ge(edge_weight, s.T + 1)
                    wait(act, aggregated, s.T)
                    for c in range(2):
                        for h in range(HEADS):
                            cols = slice(h * C, (h + 1) * C)
                            act.activation(GS[0][:, c, cols], G[s.u][:, c, cols], ACT.Identity,
                                           scale=w[:, c, h:h + 1]).then_inc(scaled_hi, 1)

                def weigh_overflow(s):
                    a, b, off = overflow(act, s, total)
                    with each(act, a, b) as g:
                        act.wait_ge(ov2_logit, (g + off) * 4 + 4)
                        act.activation(wo, zo, ACT.Exp).then_inc(ov2_weight, 1)
                        act.wait_ge(ov2_weight, g + off + 1)
                        act.wait_ge(aggregated, s.T + 1)
                        act.wait_ge(ov2_agg, g + off + 1)
                        for h in range(HEADS):
                            cols = slice(h * C, (h + 1) * C)
                            act.activation(GS[0][:, 0, cols], GO[:, cols], ACT.Identity,
                                           scale=wo[:, h:h + 1]).then_inc(ov2_hi, 1)

                def relu(s):
                    for half in range(2):
                        act.wait_ge(mixedT, 2 * s.T + 1 + half)
                        act.activation(hT[0][:, 4 * half:4 * half + 4, :].rearrange("p k n -> p (k n)"),
                                       bank[3 + half][:, :], ACT.Relu).then_inc(relu_hi, 1)

                def prepare(s):
                    spread(s)
                    weigh(s)
                    scale_high(s)
                    weigh_overflow(s)
                    relu(s)

                prepare(phase_tile(first(0, 0), 0))

                def b_body(s, more):
                    n = phase_tile(after(s), 0)
                    if more:
                        spread(n)
                        weigh(n)
                        scale_high(n)
                        weigh_overflow(n)
                    act.wait_ge(dense_done, s.t + 1)
                    wait(act, stored2[s.u], 16 * s.h)
                    for i in range(2):
                        act.copy(rowb[s.u][:, i * W3:(i + 1) * W3], bank[5 + i][:, 0:W3]).then_inc(h2_act, 1)
                    if more:
                        relu(n)

                over_tiles(act, b_body)
                act.wait_ge(wc_in, WC_LOADS)
                act.wait_ge(dense_done, TILES)
                for hi, raw in ((wfc_hi, wfc_raw), (f1_hi, f1_raw), (f2_hi, f2_raw)):
                    act.copy(hi[:, :, :].rearrange("p k n -> p (k n)"),
                             raw[:, :, :].rearrange("p k n -> p (k n)")).then_inc(wc_hi_done, 1)
                prepare(phase_tile(first(0, 0), 1))

                def turned_gelu(s):
                    act.wait_ge(c_gT, s.t + 1)
                    high_part(gT[0][:, :, :], bank[7][:, :]).then_inc(gT_hi, 1)

                def c_body(s, more):
                    n = phase_tile(after(s), 1)
                    if more:
                        spread(n)
                        weigh(n)
                        scale_high(n)
                    if not is_zero(s.t):
                        turned_gelu(before(s))
                    if more:
                        weigh_overflow(n)
                    act.wait_ge(c_xT, s.t + 1)
                    high_part(xT2[0][:, :, :], bank[5][:, :]).then_inc(xT2_hi, 1)
                    if more:
                        relu(n)
                    act.wait_ge(c_top, 2 * s.t + 2)
                    act.activation(e8, m8, ACT.Exp, bias=nmax, accum_out=esum).then_inc(c_exp, 1)
                    act.wait_ge(ffn_in, 4 * s.t + 4)
                    flat = ffn_v[:, :, :].rearrange("p i f -> p (i f)")
                    act.activation(flat, flat, ACT.Gelu).then_inc(gelu_done, 1)

                over_tiles(act, c_body)
                turned_gelu(first(HALF - 1, 1))


_INS = ['x', 'src', 'dst', 'L0_gnn_W1', 'L0_gnn_a_src1', 'L0_gnn_a_dst1', 'L0_gnn_b1', 'L0_gnn_W2', 'L0_gnn_a_src2',
        'L0_gnn_a_dst2', 'L0_gnn_b2', 'L0_gnn_Wfc', 'L0_gnn_bfc', 'L0_ffn_Wg', 'L0_ffn_W1', 'L0_ffn_b1', 'L0_ffn_W2',
        'L0_ffn_b2']


def kernel(**inputs):
    import numpy as np
    import concourse.bacc as bacc
    from concourse.bass_utils import run_bass_kernel_spmd

    nc = bacc.Bacc("TRN2", target_bir_lowering=False, num_devices=1)
    arrays, args = {}, []
    for name in _INS:
        a = np.ascontiguousarray(inputs[name])
        arrays[f"in_{name}"] = a
        args.append(nc.dram_tensor(f"in_{name}", a.shape, mybir.dt.from_np(a.dtype), kind="ExternalInput").ap())
    args.append(nc.dram_tensor("out", arrays["in_x"].shape, F32, kind="ExternalOutput").ap())
    gnn_ffn_kernel(nc, *args)
    r = run_bass_kernel_spmd(nc, [arrays], core_ids=[0])
    return r.results[0]["out"]
```

```python
from contextlib import ExitStack, contextmanager

import concourse.bass as bass
from concourse import mybir

F32 = mybir.dt.float32
F32R = mybir.dt.float32r
BF16 = mybir.dt.bfloat16
I32 = mybir.dt.int32
ALU = mybir.AluOpType
ACT = mybir.ActivationFunctionType
AX = mybir.AxisListType
ds = bass.ds

P = 128
EPS = 1e-5
SLOPE = 0.2
BIG = 1e30
NODES = 125
HEADS = 4
OVMUL = 16384
GUESS = float(0x5f3759df - (1 << 22) - (1 << 31))


class Tile:

    def __init__(self, t, h, u, T=None, TH=None, phase=0):
        self.t, self.h, self.u, self.T, self.TH, self.phase = t, h, u, T, TH, phase


class Count:
    n = 0


class Space:

    def __init__(self, nc, start):
        self.nc, self.end = nc, (start + 31) // 32 * 32

    def take(self, name, shape, dt=F32):
        tensor = self.nc.alloc_sbuf_tensor_at(name, shape, dt, offset=self.end)
        size = 2 if dt == BF16 else 4
        for n in shape[1:]:
            size *= n
        self.end += (size + 31) // 32 * 32
        return tensor

    def pair(self, name, shape):
        return [self.take(f"{name}_{part}", shape, F32R) for part in ("hi", "lo")]


def first(tile_half, u):
    return Tile(t=tile_half * 2 + u, h=tile_half, u=u)


def is_zero(t):
    return isinstance(t, int) and t == 0


def wait(eng, sem, value):
    if not isinstance(value, int) or value > 0:
        eng.wait_ge(sem, value)


def gnn_ffn_kernel(nc, x, src, dst, w1, as1, ad1, b1, w2, as2, ad2, b2, wfc, bfc, wg, f1, fb1, f2, fb2, out):
    N, D = x.shape
    E = src.shape[0]
    HC = w1.shape[1]
    C = HC // HEADS
    EX, _, DFF = f1.shape
    FF = EX * DFF
    TILES = N // NODES
    HALF = TILES // 2
    EC = E // NODES
    KD, KH, KF = D // P, HC // P, FF // P
    ROW = HC + 2 * HEADS
    MAIN = 2 * TILES
    SLOTS = MAIN + (E // P + 2)
    ROWS = TILES * P
    DUMMY = 1 << 20
    FG = FF + EX
    W3, F2W = ROW // 3, FG // 2
    WC_LOADS = 16 * (EX + 3)
    assert N % NODES == 0 and E % NODES == 0 and TILES % 2 == 0 and SLOTS % 2 == 0

    table1 = nc.dram_tensor("table1", (ROWS, ROW), F32, kind="Internal").ap()
    table2 = nc.dram_tensor("table2", (ROWS, ROW), F32, kind="Internal").ap()
    slots_dram = nc.dram_tensor("slots", (P * SLOTS, 2), I32, kind="Internal").ap()

    ctx = ExitStack()
    with ctx:
        def sem(name):
            return ctx.enter_context(nc.semaphore(name))

        banks01 = ctx.enter_context(nc.psum_tensor("banks01", [P, 2, 512], F32))
        bank = [banks01[:, 0, :], banks01[:, 1, :]]
        bank += [ctx.enter_context(nc.psum_tensor(f"bank{i}", [P, 512], F32)) for i in range(2, 8)]

        base = Space(nc, nc.sbuf_base)
        b1_bc = base.take("b1_bc", [P, ROW])
        b2_bc = base.take("b2_bc", [P, ROW])
        bfc_bc = base.take("bfc_bc", [P, D])
        fb1_bc = base.take("fb1_bc", [P, FF])
        fb2_sb = base.take("fb2_sb", [EX, D])
        ones_ex = base.take("ones_ex", [EX, P])
        fb2_twice = base.take("fb2_twice", [P, D])
        ident = base.take("ident", [P, P])
        iota_node = base.take("iota_node", [P, P])
        slot_loc = base.take("slot_loc", [P, SLOTS])
        slot_meta = base.take("slot_meta", [P, SLOTS, 2], I32)
        ov_start = base.take("ov_start", [1, TILES + 8], I32)

        weights_b = Space(nc, base.end)
        w2_hi = weights_b.take("w2_hi", [P, KH, ROW], F32R)
        w2_raw = Space(nc, weights_b.end).take("w2_raw", [P, KH, ROW])
        w2_lo = weights_b.take("w2_lo", [P, KH, ROW], F32R)
        weights_c = Space(nc, base.end)
        wfc_hi, wfc_lo = weights_c.pair("wfc", [P, KH, D])
        f1_hi, f1_lo = weights_c.pair("f1", [P, KD, FG])
        f2_hi, f2_lo = weights_c.pair("f2", [P, KF, D])
        assert weights_c.end <= weights_b.end

        onehot_t = Space(nc, weights_b.end).take("onehot_t", [P, EC, TILES], BF16)
        same = Space(nc, base.end).take("same", [P, EC, EC], BF16)
        lookup = Space(nc, base.end).take("lookup", [P, EC, TILES])
        assert EC * TILES * 4 <= KH * ROW * 4 and EC * TILES * 2 <= KD * ROW * 4

        phase_a = Space(nc, weights_b.end)
        w1_hi = phase_a.take("w1_hi", [P, KD, ROW], F32R)
        w1_raw = Space(nc, phase_a.end).take("w1_raw", [P, KD, ROW])
        w1_lo = phase_a.take("w1_lo", [P, KD, ROW], F32R)
        a_bc = phase_a.take("a_bc", [P, 4, HC])
        fold_out = phase_a.take("fold_out", [P, C])
        xa = [phase_a.take(f"xa{u}", [P, D]) for u in range(2)]
        xna = [phase_a.take(f"xna{u}", [P, D]) for u in range(2)]
        xTa = [phase_a.pair(f"xTa{u}", [P, KD, P]) for u in range(2)]
        stat_a = phase_a.take("stat_a", [P, 10])
        rowa = [phase_a.take(f"rowa{u}", [P, ROW]) for u in range(2)]
        pairs = phase_a.take("pairs", [P, EC, 2], I32)
        slot_idx = phase_a.take("slot_idx", [P, EC], I32)
        pair_st = phase_a.take("pair_st", [P, 4, 2], I32)
        idx_st = phase_a.take("idx_st", [P, 4], I32)
        fill = phase_a.take("fill", [P, SLOTS, 2], I32)
        dst_i = phase_a.take("dst_i", [P, EC], I32)
        src_i = phase_a.take("src_i", [P, EC], I32)
        ef = phase_a.take("ef", [P, 10, EC])
        ei = phase_a.take("ei", [P, 4, EC], I32)
        earlier = phase_a.take("earlier", [P, EC, EC], BF16)
        iota_tile = phase_a.take("iota_tile", [P, TILES])
        tri = phase_a.take("tri", [P, P])
        ones = phase_a.take("ones", [P, P])
        count_pt = phase_a.take("count_pt", [P, TILES])
        scan = phase_a.take("scan", [P, 2, TILES])
        ov_i = phase_a.take("ov_i", [P, 2, TILES], I32)
        base_t = phase_a.take("base_t", [P, 3, TILES])

        raw_c = Space(nc, weights_b.end)
        wfc_raw = raw_c.take("wfc_raw", [P, KH, D])
        f1_raw = raw_c.take("f1_raw", [P, KD, FG])
        f2_raw = raw_c.take("f2_raw", [P, KF, D])
        phase_c = Space(nc, weights_b.end)
        xc = [phase_c.take(f"xc{u}", [P, D]) for u in range(2)]
        x2 = [phase_c.take(f"x2_{u}", [P, D]) for u in range(2)]
        xn2 = phase_c.take("xn2", [P, D])
        xT2 = phase_c.pair("xT2", [P, KD, P])
        ffn_v = phase_c.take("ffn_v", [P, 2, FF])
        gsum = phase_c.take("gsum", [P, FF])
        gT = phase_c.pair("gT", [P, KF, P])
        outb = [phase_c.take(f"outb{u}", [P, D]) for u in range(2)]

        agg = Space(nc, max(raw_c.end, phase_c.end))
        G = [agg.take(f"G{u}", [P, 2, ROW]) for u in range(2)]
        H = [agg.take(f"H{u}", [P, ROW]) for u in range(2)]
        GS = agg.pair("GS", [P, 2, HC])
        weighted = agg.take("weighted", [P, HC])
        GO = agg.take("GO", [P, ROW])
        gidx = [agg.take(f"gidx{u}", [P, 2], I32) for u in range(2)]
        goidx = agg.take("goidx", [P, 1], I32)
        OH = [agg.take(f"OH{u}", [P, 2, P], F32R) for u in range(2)]
        NM = agg.take("NM", [P, 2, P])
        AM = agg.take("AM", [P, 2, HEADS, P])
        OHo = agg.take("OHo", [P, P], F32R)
        NMo = agg.take("NMo", [P, P])
        AMo = agg.take("AMo", [P, HEADS, P])
        ohTo = agg.take("ohTo", [P, P])
        ohT = agg.take("ohT", [P, 2, P])
        small_f = agg.take("small_f", [P, 106])
        mixed = agg.take("mixed", [P, HC])
        hT = [agg.pair(f"hT{u}", [P, KH, P]) for u in range(2)]
        rowb = [agg.take(f"rowb{u}", [P, ROW]) for u in range(2)]

        mx, mxo = small_f[:, 0:4], small_f[:, 4:8]
        lsum, rhs8 = small_f[:, 8:12], small_f[:, 12:20]
        selfz, wself = small_f[:, 20:24], small_f[:, 24:28]
        z = small_f[:, 28:36].rearrange("p (c h) -> p c h", c=2)
        w = small_f[:, 36:44].rearrange("p (c h) -> p c h", c=2)
        zo, wo = small_f[:, 44:48], small_f[:, 48:52]
        dsum, rden, wsn = small_f[:, 52:56], small_f[:, 56:60], small_f[:, 60:64]
        stat_c = small_f[:, 96:106]
        m8, nmax, e8, esum = small_f[:, 73:81], small_f[:, 81:82], small_f[:, 82:90], small_f[:, 90:91]
        rsum, s2, p2 = small_f[:, 91:92], small_f[:, 92:93], small_f[:, 94:96]

        small = bank[2]
        ohT_ps = small[:, 0:256].rearrange("p (c e) -> p c e", c=2)
        edge_ps = small[:, 256:272].rearrange("p (c k) -> p c k", c=2)
        den_ps, den_o_ps, edge_o_ps = small[:, 272:276], small[:, 280:284], small[:, 288:296]
        ohT_o_ps = small[:, 384:512]
        gate_ps = bank[7][:, F2W - EX:F2W]

        w1_in, edges_in, w2_in, wc_in = sem("w1_in"), sem("edges_in"), sem("w2_in"), sem("wc_in")
        bias_in = sem("bias_in")
        consts = sem("consts")
        fold1, fold2 = sem("fold1"), sem("fold2")
        w1_hi_done, w1_lo_done, w2_hi_done, w2_lo_done = (sem(n) for n in (
            "w1_hi_done", "w1_lo_done", "w2_hi_done", "w2_lo_done"))
        wc_hi_done, wc_lo_done, xc_cleared = sem("wc_hi_done"), sem("wc_lo_done"), sem("xc_cleared")
        fb2_sum = sem("fb2_sum")
        placing, count_done, pl_base, filled, staged, scattered, meta_in, meta_ready = (
            sem("placing"), sem("count_done"), sem("pl_base"), sem("filled"), sem("staged"),
            [sem(f"scattered{i}") for i in range(4)], sem("meta_in"), sem("meta_ready"))
        placed, ov_ready, c_const = sem("placed"), sem("ov_ready"), sem("c_const")
        xa_in = [sem(f"xa_in{u}") for u in range(2)]
        stored1 = [sem(f"stored1_{u}") for u in range(2)]
        a_stats, xna_ready, xa_turned, xTa_hi, xTa_lo, h1_done, h1_biased = (
            sem(n) for n in ("a_stats", "xna_ready", "xa_turned", "xTa_hi", "xTa_lo", "h1_done", "h1_biased"))
        self_in = [sem(f"self_in{u}") for u in range(2)]
        gathered = [[sem(f"gathered{u}{c}") for c in range(2)] for u in range(2)]
        cleared = sem("cleared")
        (index_staged, onehot, nomatch, masked, maskedT, onehotT, onehotT_copied, edge_max, node_max, lgt_sum,
         shift_ready, self_logit, self_weight, edge_rhs, edge_logit, edge_weight, scaled_hi, scaled_lo0, scaled_lo1, aggregated, den_done,
         den_total, den_inv, self_scale, self_scaled, mix_done, mixedT, relu_hi, relu_lo) = (sem(n) for n in (
             "index_staged", "onehot", "nomatch", "masked", "maskedT", "onehotT", "onehotT_copied", "edge_max",
             "node_max", "lgt_sum", "shift_ready", "self_logit", "self_weight", "edge_rhs", "edge_logit",
             "edge_weight", "scaled_hi", "scaled_lo0", "scaled_lo1", "aggregated", "den_done", "den_total", "den_inv", "self_scale",
             "self_scaled", "mix_done", "mixedT", "relu_hi", "relu_lo"))
        (ov_staged, ov_in, ov1_masked, ov1_dve, ov1_T, ov1_max, ov2_onehot, ov2_T, ov2_copied, ov2_rhs, ov2_logit,
         ov2_weight, ov2_hi, ov2_lo, ov2_agg, ov2_den) = (sem(n) for n in (
             "ov_staged", "ov_in", "ov1_masked", "ov1_dve", "ov1_T", "ov1_max", "ov2_onehot", "ov2_T", "ov2_copied",
             "ov2_rhs", "ov2_logit", "ov2_weight", "ov2_hi", "ov2_lo", "ov2_agg", "ov2_den"))
        dense_done, h2_act, h2_dve, h2_biased = sem("dense_done"), sem("h2_act"), sem("h2_dve"), sem("h2_biased")
        stored2 = [sem(f"stored2_{u}") for u in range(2)]
        chunk_weighted = sem("chunk_weighted")
        xc_in = [sem(f"xc_in{u}") for u in range(2)]
        out_stored = [sem(f"out_stored{u}") for u in range(2)]
        (x_biased, fc_done, c_x2, x2_biased, c_stats, c_root, c_xn, c_xT, xT2_hi, xT2_lo, f1_done, c_top, c_exp, c_prob,
         ffn_in, gelu_done, gsum_done, c_gT, gT_hi, gT_lo, f2_done, out_sum) = (sem(n) for n in (
             "x_biased", "fc_done", "c_x2", "x2_biased", "c_stats", "c_root", "c_xn", "c_xT", "xT2_hi", "xT2_lo", "f1_done",
             "c_top", "c_exp", "c_prob", "ffn_in", "gelu_done", "gsum_done", "c_gT", "gT_hi", "gT_lo", "f2_done",
             "out_sum"))

        def phase_tile(s, phase):
            if s is None:
                return None
            return Tile(t=s.t, h=s.h, u=s.u, T=s.t + TILES * phase, TH=s.h + HALF * phase, phase=phase)

        def ahead(s, by):
            n = first(s.h + (s.u + by) // 2, (s.u + by) % 2)
            return None if isinstance(n.t, int) and n.t >= TILES else n

        thirds = [(i * W3, (i + 1) * W3) for i in range(3)]

        def early(eng, value):
            return value if isinstance(value, int) else eng.snap(eng.to_reg(value))

        def alone(eng, sem, value):
            eng.wait_ge(consts, 1)
            eng.wait_ge(sem, value)

        @contextmanager
        def overflow(eng, s, total):
            with eng.If(0 < total):
                a = eng.value_load(ov_start[0:1, ds(s.t, 1)], min_val=0, max_val=SLOTS - MAIN)
                b = eng.value_load(ov_start[0:1, ds(s.t + 1, 1)], min_val=0, max_val=SLOTS - MAIN)
                with eng.If(a < b):
                    with eng.Fori(a, b) as g:
                        yield g, a, b, (total if s.phase else 0)

        def separate(eng, sem_, value):
            if eng is nc.gpsimd:
                alone(eng, sem_, early(eng, value))
            else:
                eng.wait_ge(sem_, value)

        def root_steps(eng, stat, sem_, n):
            a, y, t = stat[:, 7:8], stat[:, 8:9], stat[:, 9:10]
            ops = [lambda: eng.tensor_scalar(a, a, EPS, 0.5, ALU.add, ALU.mult),
                   lambda: eng.tensor_scalar(y.bitcast(I32), a.bitcast(I32), -0.5, GUESS, ALU.mult, ALU.add)]
            ops += [lambda: eng.tensor_scalar(t, y, a, y, ALU.mult, ALU.mult),
                    lambda: eng.tensor_scalar(y, t, -1.5, y, ALU.add, ALU.mult)] * 3
            for i, op in enumerate(ops):
                if i:
                    separate(eng, sem_, n + i)
                op().then_inc(sem_, 1)

        def over_tiles(eng, body):
            body(first(0, 0))
            body(first(0, 1))
            with eng.Fori(1, HALF - 2) as it:
                body(first(it, 0))
                body(first(it, 1))
            for h in (HALF - 2, HALF - 1):
                body(first(h, 0))
                body(first(h, 1))

        with nc.Block() as block:
            @block.sync
            def _(sp):
                sp.dma_start(dst_i[0:NODES, :], dst.rearrange("(p c) -> p c", c=EC)).then_inc(edges_in, 16)
                sp.dma_start(src_i[0:NODES, :], src.rearrange("(p c) -> p c", c=EC)).then_inc(edges_in, 16)
                sp.wait_ge(consts, 1)
                for u in range(2):
                    sp.dma_start(xa[u][0:NODES, :], x[u * NODES:(u + 1) * NODES, :]).then_inc(xa_in[u], 16)
                sp.dma_start(w1_raw[:, :, 0:HC], w1.rearrange("(k p) n -> p k n", p=P)).then_inc(w1_in, 16)
                for i, a in enumerate((as1, ad1, as2, ad2)):
                    sp.dma_start(a_bc[:, i, :], a.rearrange("h c -> (h c)").partition_broadcast(P)).then_inc(w1_in, 16)
                sp.dma_start(w2_raw[:, :, 0:HC], w2.rearrange("(k p) n -> p k n", p=P)).then_inc(w2_in, 16)
                for to, of in ((b1_bc, b1), (b2_bc, b2)):
                    sp.dma_start(to[:, 0:HC], of.partition_broadcast(P)).then_inc(w2_in, 16)
                sp.dma_start(fb2_sb[:, :], fb2).then_inc(bias_in, 16)
                sp.dma_start(bfc_bc[:, :], bfc.partition_broadcast(P)).then_inc(bias_in, 16)
                sp.dma_start(fb1_bc[:, :], fb1.rearrange("e f -> (e f)").partition_broadcast(P)).then_inc(bias_in, 16)

                def xa_load(s):
                    start = early(sp, s.t * NODES)
                    sp.wait_ge(xna_ready, s.t - 1)
                    sp.dma_start(xa[s.u][0:NODES, :], x[ds(start, NODES), :]).then_inc(xa_in[s.u], 16)

                def a_io(s):
                    if ahead(s, 3):
                        xa_load(ahead(s, 3))
                    sp.wait_ge(h1_biased, 3 * s.t + 3)
                    sp.dma_start(table1[ds(s.t * P, P), :], rowa[s.u][:, :]).then_inc(stored1[s.u], 16)

                xa_load(first(1, 0))
                over_tiles(sp, a_io)

                for i in range(4):
                    sp.wait_ge(scattered[i], 16 * (EC // 4))
                sp.dma_start(slot_meta[:, :, :], slots_dram.rearrange("(p c) k -> p c k", p=P)).then_inc(meta_in, 16)
                sp.wait_ge(cleared, 1)
                for u in range(2):
                    sp.wait_ge(stored1[u], 16 * HALF)

                sp.dma_start(wfc_raw[:, :, :], wfc.rearrange("(k p) n -> p k n", p=P)).then_inc(wc_in, 16)
                for e in range(EX):
                    sp.dma_start(f1_raw[:, :, e * DFF:(e + 1) * DFF],
                                 f1[e].rearrange("(k p) f -> p k f", p=P)).then_inc(wc_in, 16)
                sp.dma_start(f1_raw[:, :, FF:FG], wg.rearrange("(k p) e -> p k e", p=P)).then_inc(wc_in, 16)
                sp.dma_start(f2_raw[:, :, :],
                             f2.rearrange("e f d -> (e f) d").rearrange("(k p) d -> p k d", p=P)).then_inc(wc_in, 16)

                def self_load(s, table):
                    sp.dma_start(H[s.u][:, :], table[ds(s.t * P, P), :]).then_inc(self_in[s.u], 16)

                def b_io(s):
                    if ahead(s, 2):
                        sp.wait_ge(self_scaled, 4 * (s.t + 1))
                        self_load(ahead(s, 2), table1)
                    sp.wait_ge(h2_dve, s.t + 1)
                    sp.wait_ge(h2_biased, s.t + 1)
                    sp.dma_start(table2[ds(s.t * P, P), :], rowb[s.u][:, :]).then_inc(stored2[s.u], 16)

                self_load(first(0, 0), table1)
                self_load(first(0, 1), table1)
                over_tiles(sp, b_io)

                sp.wait_ge(self_scaled, 4 * TILES)
                for u in range(2):
                    sp.wait_ge(stored2[u], 16 * HALF)

                def x_load(s):
                    sp.dma_start(xc[s.u][0:NODES, :], x[ds(s.t * NODES, NODES), :]).then_inc(xc_in[s.u], 16)

                def out_store(s):
                    start = early(sp, s.t * NODES)
                    sp.wait_ge(out_sum, s.t + 1)
                    sp.dma_start(out[ds(start, NODES), :], outb[s.u][0:NODES, :]).then_inc(out_stored[s.u], 16)

                def c_io(s):
                    n = ahead(s, 2)
                    if n:
                        sp.wait_ge(self_scaled, 4 * (s.t + TILES + 1))
                        self_load(n, table2)
                        sp.wait_ge(c_x2, s.t + 1)
                        x_load(n)
                    if not is_zero(s.t):
                        out_store(ahead(s, -1))

                for u in range(2):
                    self_load(first(0, u), table2)
                sp.wait_ge(xc_cleared, 1)
                for u in range(2):
                    x_load(first(0, u))
                over_tiles(sp, c_io)
                out_store(first(HALF - 1, 1))
                for u in range(2):
                    sp.wait_ge(out_stored[u], 16 * HALF)

            @block.gpsimd
            def _(pool):
                for u in range(2):
                    pool.memset(xa[u][:, :], 0.0)
                pool.memset(b1_bc[:, HC:ROW], 0.0)
                pool.memset(b2_bc[:, HC:ROW], 0.0)
                pool.memset(ones_ex[:, :], 1.0)
                pool.memset(fill[:, :, 0:1], DUMMY)
                pool.memset(fill[:, :, 1:2], -1).then_inc(consts, 1)
                pool.iota(iota_node[:, :], [[1, P]], base=0, channel_multiplier=0,
                          allow_small_or_imprecise_dtypes=True)
                pool.iota(iota_tile[:, :], [[1, TILES]], base=0, channel_multiplier=0,
                          allow_small_or_imprecise_dtypes=True)
                pool.memset(ident[:, :], 0.0)
                pool.memset(tri[:, :], 1.0)
                pool.memset(earlier[:, :, :], 1.0)
                pool.memset(ones[:, :], 1.0).then_inc(consts, 1)
                pool.wait_ge(consts, 2)
                pool.affine_select(out=ident[:, :], in_=ident[:, :], pattern=[[-1, P]], compare_op=ALU.not_equal,
                                   fill=1.0, base=0, channel_multiplier=1)
                pool.affine_select(out=tri[:, :], in_=tri[:, :], pattern=[[1, P]], compare_op=ALU.is_gt,
                                   fill=0.0, base=0, channel_multiplier=-1)
                pool.affine_select(out=earlier[:, :, :], in_=earlier[:, :, :], pattern=[[1, EC], [-1, EC]],
                                   compare_op=ALU.is_gt, fill=0.0, base=0, channel_multiplier=0).then_inc(consts, 1)
                pool.dma_start(slots_dram.rearrange("(p c) k -> p c k", p=P), fill[:, :, :]).then_inc(filled, 16)

                pool.wait_ge(placed, 2)
                pool.wait_ge(filled, 16)
                def scatter(it):
                    for i in range(4):
                        wait(pool, scattered[i], 16 * it)
                    counted = early(pool, 2 * it + 2)
                    pool.tensor_copy(pair_st[0:NODES, :, :], pairs[0:NODES, ds(4 * it, 4), :]).then_inc(staged, 1)
                    pool.tensor_copy(idx_st[0:NODES, :], slot_idx[0:NODES, ds(4 * it, 4)]).then_inc(staged, 1)
                    alone(pool, staged, counted)
                    for i in range(4):
                        pool.indirect_dma_start(
                            out=slots_dram, out_offset=bass.IndirectOffsetOnAxis(ap=idx_st[0:NODES, i:i + 1], axis=0),
                            in_=pair_st[0:NODES, i, :], in_offset=None).then_inc(scattered[i], 16)

                scatter(0)
                with pool.Fori(1, EC // 4) as it:
                    scatter(it)

                pool.wait_ge(fold2, KH * 8)
                for k in range(KH):
                    pool.tensor_copy(w2_hi[:, k, :], w2_raw[:, k, :]).then_inc(w2_hi_done, 1)
                pool.wait_ge(w2_hi_done, KH)
                pool.tensor_tensor(w2_lo[:, :, :], w2_raw[:, :, :], w2_hi[:, :, :].bitcast(F32),
                                   ALU.subtract).then_inc(w2_lo_done, 1)

                for i in range(4):
                    pool.wait_ge(scattered[i], 16 * (EC // 4))
                pool.wait_ge(w2_lo_done, 1)
                pool.wait_ge(h1_done, TILES)
                for u in range(2):
                    pool.wait_ge(stored1[u], 16 * HALF)
                for u in range(2):
                    pool.memset(G[u][:, :, :], 0.0)
                pool.memset(GO[:, :], 0.0).then_inc(cleared, 1)
                pool.wait_ge(cleared, 1)
                pool.wait_ge(ov_ready, 1)
                pool.wait_ge(meta_in, 16)
                total = pool.snap(pool.value_load(ov_start[0:1, TILES:TILES + 1], min_val=0, max_val=SLOTS - MAIN))

                pool.sem_inc(ov1_masked, 1)
                pool.sem_inc(ov2_agg, 1)

                def gather(s, table):
                    counted = early(pool, s.T + 1)
                    pool.tensor_copy(gidx[s.u][:, :], slot_meta[:, ds(2 * s.t, 2), 0]).then_inc(index_staged, 1)
                    alone(pool, index_staged, counted)
                    for c in range(2):
                        pool.indirect_dma_start(
                            out=G[s.u][:, c, :], out_offset=None, in_=table,
                            in_offset=bass.IndirectOffsetOnAxis(ap=gidx[s.u][:, c:c + 1], axis=0),
                            bounds_check=ROWS - 1, oob_is_err=False).then_inc(gathered[s.u][c], 16)

                def gather_one(g, nth, table):
                    counted = early(pool, nth + 1)
                    pool.tensor_copy(goidx[:, :], slot_meta[:, ds(g + MAIN, 1), 0]).then_inc(ov_staged, 1)
                    alone(pool, ov_staged, counted)
                    pool.indirect_dma_start(
                        out=GO[:, :], out_offset=None, in_=table,
                        in_offset=bass.IndirectOffsetOnAxis(ap=goidx[:, 0:1], axis=0),
                        bounds_check=ROWS - 1, oob_is_err=False).then_inc(ov_in, 16)

                def gather_for_maximum(s, table):
                    with overflow(pool, s, total) as (g, a, b, off):
                        alone(pool, ov2_agg, a + off + 1)
                        pool.wait_ge(ov1_masked, g + off + 1)
                        gather_one(g, a + g + off * 2, table)

                def gather_for_sum(s, table):
                    with overflow(pool, s, total) as (g, a, b, off):
                        alone(pool, ov1_masked, b + off + 1)
                        pool.wait_ge(ov2_agg, g + off + 1)
                        gather_one(g, b + g + off * 2, table)

                def mask(s):
                    for c in range(2):
                        pool.wait_ge(gathered[s.u][c], 16 * s.TH + 16)
                    wait(pool, maskedT, s.T)
                    pool.wait_ge(nomatch, s.T + 1)
                    full = [P, 2, HEADS, P]
                    pool.tensor_tensor(AM[:, :, :, :], NM[:, :, :].unsqueeze(2).to_broadcast(full),
                                       G[s.u][:, :, HC:HC + HEADS].unsqueeze(3).to_broadcast(full),
                                       ALU.add).then_inc(masked, 1)

                def bias_row(s):
                    pool.wait_ge(h2_act, 2 * s.t + 2)
                    pool.tensor_tensor(rowb[s.u][:, 0:2 * W3], rowb[s.u][:, 0:2 * W3], b2_bc[:, 0:2 * W3],
                                       ALU.add).then_inc(h2_biased, 1)

                def bias_x(s):
                    pool.wait_ge(xc_in[s.u], 16 * s.h + 16)
                    pool.tensor_tensor(xc[s.u][:, :], xc[s.u][:, :], bfc_bc[:, :], ALU.add).then_inc(x_biased, 1)

                def bias_x2(s):
                    pool.wait_ge(c_xn, s.t + 1)
                    pool.tensor_tensor(x2[s.u][:, :], x2[s.u][:, :], fb2_twice[:, :], ALU.add).then_inc(x2_biased, 1)

                def scale_low(s):
                    pool.wait_ge(edge_weight, s.T + 1)
                    pool.tensor_tensor(weighted[:, :].rearrange("p (h c) -> p h c", h=HEADS),
                                       G[s.u][:, 1, 0:HC].rearrange("p (h c) -> p h c", h=HEADS),
                                       w[:, 1, :].unsqueeze(2).to_broadcast([P, HEADS, C]),
                                       ALU.mult).then_inc(chunk_weighted, 1)
                    pool.wait_ge(chunk_weighted, s.t - 1)
                    pool.wait_ge(scaled_hi, 8 * s.T + 8)
                    pool.wait_ge(aggregated, s.T)
                    pool.tensor_tensor(GS[1][:, 1, :], weighted[:, :], GS[0][:, 1, :].bitcast(F32),
                                       ALU.subtract).then_inc(scaled_lo1, 4)

                def regather(s, table):
                    n = ahead(s, 2)
                    if n:
                        pool.wait_ge(scaled_lo0, 4 * s.T + 4)
                        pool.wait_ge(scaled_lo1, 4 * s.T + 4)
                        gather(phase_tile(n, s.phase), table)

                def aggregation(table, stored, phase):
                    for u in range(2):
                        pool.wait_ge(stored[u], 16 * HALF)
                    s0, s1 = phase_tile(first(0, 0), phase), phase_tile(first(0, 1), phase)
                    gather(s0, table)
                    gather(s1, table)
                    mask(s0)
                    gather_for_maximum(s0, table)
                    if phase:
                        pool.wait_ge(wc_lo_done, 3)
                        pool.memset(xc[0][:, :], 0.0)
                        pool.memset(xc[1][:, :], 0.0).then_inc(xc_cleared, 1)
                    mask(s1)
                    gather_for_sum(s0, table)
                    regather(s0, table)
                    gather_for_maximum(s1, table)
                    mask(phase_tile(first(1, 0), phase))
                    if phase:
                        bias_x(s0)
                        pool.wait_ge(c_const, 1)

                    def body(t):
                        n, m, l = (phase_tile(ahead(t, i), phase) for i in (1, 2, 3))
                        if n:
                            regather(n, table)
                            gather_for_sum(n, table)
                        if phase:
                            separate(pool, c_stats, 2 * t.t + 2)
                            root_steps(pool, stat_c, c_root, 8 * t.t)
                        if m:
                            gather_for_maximum(m, table)
                        if phase and n:
                            bias_x(n)
                        if phase and m:
                            scale_low(m)
                        if l:
                            mask(l)
                        if phase:
                            bias_x2(t)
                        else:
                            bias_row(t)

                    over_tiles(pool, body)

                aggregation(table1, stored1, 0)
                aggregation(table2, stored2, 1)

            @block.tensor
            def _(pe):
                pe.wait_ge(consts, 3)
                pe.wait_ge(count_done, 1)
                pe.matmul(bank[7][:, 0:TILES], tri[0:NODES, :], count_pt[0:NODES, :], start=True, stop=True)
                pe.matmul(bank[7][:, 128:128 + TILES], ones[0:NODES, :], count_pt[0:NODES, :],
                          start=True, stop=True).then_inc(pl_base, 1)
                pe.wait_ge(w1_hi_done, 1)
                pe.wait_ge(w1_lo_done, 1)

                def three(out, lhs, rhs, k, last, cols):
                    (l_hi, l_lo), (r_hi, r_lo) = lhs, rhs
                    for i, (l, r) in enumerate(((l_hi, r_hi), (l_hi, r_lo), (l_lo, r_hi))):
                        for o, (a, b) in zip(out, cols):
                            ins = pe.matmul(o, l[:, k, :], r[:, k, a:b], start=(k == 0 and i == 0),
                                            stop=(k == last and i == 2), skip_group_check=True)
                    return ins

                def turn(s):
                    pe.wait_ge(xna_ready, s.t + 1)
                    wait(pe, xTa_hi, s.t - 1)
                    wait(pe, xTa_lo, s.t - 1)
                    for k in range(KD):
                        ins = pe.transpose(bank[s.u][:, k * P:(k + 1) * P], xna[s.u][:, k * P:(k + 1) * P], ident[:, :])
                    ins.then_inc(xa_turned, 1)

                def product(s):
                    pe.wait_ge(xTa_hi, s.t + 1)
                    pe.wait_ge(xTa_lo, s.t + 1)
                    wait(pe, h1_biased, 3 * s.t - 3)
                    for k in range(KD):
                        ins = three([bank[2 + 3 * s.u + i][:, 0:W3] for i in range(3)], xTa[s.u], (w1_hi, w1_lo), k,
                                    KD - 1, thirds)
                    ins.then_inc(h1_done, 1)

                pe.wait_ge(placed, 1)
                turn(first(0, 0))

                def a_body(s):
                    if ahead(s, 1):
                        turn(ahead(s, 1))
                    product(s)

                over_tiles(pe, a_body)

                def turn_masked(s):
                    pe.wait_ge(masked, s.T + 1)
                    for c in range(2):
                        for h in range(HEADS):
                            ins = pe.transpose(bank[c][:, h * P:(h + 1) * P], AM[:, c, h, :], ident[:, :])
                    ins.then_inc(maskedT, 1)
                    wait(pe, den_inv, s.T)
                    for c in range(2):
                        ins = pe.transpose(ohT_ps[:, c, :], OH[s.u][:, c, :].bitcast(F32), ident[:, :])
                    ins.then_inc(onehotT, 1)

                def turn_overflow(s):
                    with overflow(pe, s, total) as (g, a, b, off):
                        pe.wait_ge(ov1_masked, g + off + 2)
                        for h in range(HEADS):
                            ins = pe.transpose(bank[0][:, h * P:(h + 1) * P], AMo[:, h, :], ident[:, :])
                        ins.then_inc(ov1_T, 1)

                def target_values(s):
                    pe.wait_ge(shift_ready, 2 * s.T + 2)
                    pe.wait_ge(onehotT_copied, s.T + 1)
                    for c in range(2):
                        ins = pe.matmul(edge_ps[:, c, :], ohT[:, c, :], rhs8, start=True, stop=True)
                    ins.then_inc(edge_rhs, 1)

                def sum_weights(s):
                    pe.wait_ge(edge_weight, s.T + 1)
                    for c in range(2):
                        ins = pe.matmul(den_ps, OH[s.u][:, c, :].bitcast(F32), w[:, c, :], start=(c == 0), stop=(c == 1))
                    ins.then_inc(den_done, 1)

                def aggregate(s):
                    for c in range(2):
                        pe.wait_ge((scaled_lo0, scaled_lo1)[c], 4 * s.T + 4)
                        for i, part in enumerate(GS):
                            for half in range(2):
                                ins = pe.matmul(bank[3 + half][:, :], OH[s.u][:, c, :], part[:, c, half * 512:half * 512 + 512],
                                                start=(c == 0 and i == 0), stop=True, skip_group_check=True)
                    ins.then_inc(aggregated, 1)
                    with overflow(pe, s, total) as (g, a, b, off):
                        pe.wait_ge(ov2_onehot, g + off + 1)
                        pe.transpose(ohT_o_ps, OHo[:, :].bitcast(F32), ident[:, :]).then_inc(ov2_T, 1)
                        pe.wait_ge(ov2_copied, g + off + 1)
                        pe.matmul(edge_o_ps, ohTo[:, :], rhs8, start=True, stop=True).then_inc(ov2_rhs, 1)
                        pe.wait_ge(ov2_lo, (g + off) * 4 + 4)
                        for part in GS:
                            for half in range(2):
                                pe.matmul(bank[3 + half][:, :], OHo[:, :], part[:, 0, half * 512:half * 512 + 512],
                                          start=False, stop=True, skip_group_check=True)
                        pe.matmul(den_o_ps, OHo[:, :].bitcast(F32), wo, start=True, stop=True).then_inc(ov2_agg, 1)

                def turn_mixed(s):
                    for half in range(2):
                        pe.wait_ge(mix_done, 4 * s.T + 2 + 2 * half)
                        for k in range(4):
                            c = 4 * half + k
                            ins = pe.transpose(bank[3 + half][:, k * P:(k + 1) * P], mixed[:, c * P:(c + 1) * P], ident[:, :])
                        ins.then_inc(mixedT, 1)

                def dense(s, ks):
                    for k in ks:
                        if k % 4 == 0:
                            pe.wait_ge(relu_hi, 2 * s.T + 1 + k // 4)
                            pe.wait_ge(relu_lo, 2 * s.T + 1 + k // 4)
                        if 0 < k < KH - 1:
                            three([bank[5 + i][:, 0:W3] for i in range(3)], hT[s.u], (w2_hi, w2_lo), k, KH - 1, thirds)
                            continue
                        for i in range(3):
                            if k == 0:
                                wait(pe, *((h2_act, 2 * s.T - 1), (h2_act, 2 * s.T), (h2_dve, s.T))[i])
                            ins = three([bank[5 + i][:, 0:W3]], hT[s.u], (w2_hi, w2_lo), k, KH - 1, [thirds[i]])
                            if k == KH - 1:
                                ins.then_inc(dense_done, 1)

                def prepare(phase):
                    s0, s1 = phase_tile(first(0, 0), phase), phase_tile(first(0, 1), phase)
                    turn_masked(s0)
                    turn_overflow(s0)
                    target_values(s0)
                    sum_weights(s0)
                    aggregate(s0)
                    turn_masked(s1)
                    turn_overflow(s1)
                    turn_mixed(s0)
                    target_values(s1)

                pe.wait_ge(h1_biased, 3 * TILES)
                pe.wait_ge(ov_ready, 1)
                pe.wait_ge(w2_hi_done, KH)
                pe.wait_ge(w2_lo_done, 1)
                total = pe.snap(pe.value_load(ov_start[0:1, TILES:TILES + 1], min_val=0, max_val=SLOTS - MAIN))
                prepare(0)

                def b_body(t):
                    s, n, m = (phase_tile(x, 0) for x in (t, ahead(t, 1), ahead(t, 2)))
                    dense(s, range(0, 2))
                    if n:
                        sum_weights(n)
                    dense(s, range(2, 4))
                    if n:
                        aggregate(n)
                    if m:
                        turn_masked(m)
                        turn_overflow(m)
                    dense(s, range(4, 6))
                    if n:
                        turn_mixed(n)
                    dense(s, range(6, KH))
                    if m:
                        target_values(m)

                over_tiles(pe, b_body)

                pe.wait_ge(h2_act, 2 * TILES)
                pe.wait_ge(h2_dve, TILES)
                pe.wait_ge(bias_in, 16 * 3)
                pe.matmul(bank[7][:, :], ones_ex[:, :], fb2_sb[:, :], start=True, stop=True).then_inc(fb2_sum, 1)
                prepare(1)
                pe.wait_ge(wc_hi_done, 3)
                pe.wait_ge(wc_lo_done, 3)
                pe.wait_ge(c_const, 1)

                def connect(s, ks):
                    for k in ks:
                        if k % 4 == 0:
                            pe.wait_ge(relu_hi, 2 * s.T + 1 + k // 4)
                            pe.wait_ge(relu_lo, 2 * s.T + 1 + k // 4)
                        ins = three([bank[5][:, :]], hT[s.u], (wfc_hi, wfc_lo), k, KH - 1, [(0, D)])
                    if ks[-1] == KH - 1:
                        ins.then_inc(fc_done, 1)

                def turn_gelu(s):
                    pe.wait_ge(gsum_done, s.t + 1)
                    for k in range(KF):
                        ins = pe.transpose(bank[7][:, k * P:(k + 1) * P], gsum[:, k * P:(k + 1) * P], ident[:, :])
                    ins.then_inc(c_gT, 1)

                def ffn_out(s):
                    pe.wait_ge(gT_hi, s.t + 1)
                    pe.wait_ge(gT_lo, s.t + 1)
                    for k in range(KF):
                        ins = three([bank[6][:, :]], gT, (f2_hi, f2_lo), k, KF - 1, [(0, D)])
                    ins.then_inc(f2_done, 1)

                def turn_x2(s):
                    pe.wait_ge(c_xn, s.t + 1)
                    for k in range(KD):
                        ins = pe.transpose(bank[5][:, k * P:(k + 1) * P], xn2[:, k * P:(k + 1) * P], ident[:, :])
                    ins.then_inc(c_xT, 1)

                def ffn_in_gate(s):
                    pe.wait_ge(xT2_hi, s.t + 1)
                    pe.wait_ge(xT2_lo, s.t + 1)
                    wait(pe, out_sum, s.t)
                    for k in range(KD):
                        ins = three([bank[6][:, 0:F2W], bank[7][:, 0:F2W]], xT2, (f1_hi, f1_lo), k, KD - 1,
                                    [(0, F2W), (F2W, FG)])
                    ins.then_inc(f1_done, 1)

                def c_body(t):
                    s, n, m = (phase_tile(x, 1) for x in (t, ahead(t, 1), ahead(t, 2)))
                    connect(s, range(0, 4))
                    if n:
                        sum_weights(n)
                    connect(s, range(4, KH))
                    if n:
                        aggregate(n)
                    if not is_zero(t.t):
                        turn_gelu(ahead(t, -1))
                    if m:
                        turn_masked(m)
                        turn_overflow(m)
                    if not is_zero(t.t):
                        ffn_out(ahead(t, -1))
                    turn_x2(s)
                    if n:
                        turn_mixed(n)
                    if m:
                        target_values(m)
                    ffn_in_gate(s)

                over_tiles(pe, c_body)
                turn_gelu(first(HALF - 1, 1))
                ffn_out(first(HALF - 1, 1))

            @block.vector
            def _(v):
                pl = Count()

                def step(ins):
                    ins.then_inc(placing, 1)
                    pl.n += 1

                def settle():
                    v.wait_ge(placing, pl.n)

                e = lambda i: ef[0:NODES, i, :]
                n_ = NODES
                v.wait_ge(consts, 3)
                v.wait_ge(edges_in, 32)
                step(v.tensor_copy(e(0), dst_i[0:n_, :]))
                step(v.tensor_copy(e(1), src_i[0:n_, :]))
                settle()

                def split(node, tile, rest, tmp_i):
                    step(v.tensor_scalar(tmp_i, node, 1.0 / NODES, None, ALU.mult))
                    settle()
                    step(v.tensor_copy(tile, tmp_i))
                    settle()
                    step(v.scalar_tensor_tensor(rest, tile, -float(NODES), node, ALU.mult, ALU.add))
                    settle()
                    step(v.tensor_scalar(e(9), rest, 0.0, None, ALU.is_lt))
                    step(v.tensor_scalar(e(8), rest, float(NODES), None, ALU.is_ge))
                    settle()
                    step(v.tensor_tensor(tile, tile, e(9), ALU.subtract))
                    settle()
                    step(v.tensor_tensor(tile, tile, e(8), ALU.add))
                    settle()
                    step(v.scalar_tensor_tensor(rest, tile, -float(NODES), node, ALU.mult, ALU.add))
                    settle()

                split(e(0), e(2), e(3), ei[0:n_, 0, :])
                split(e(1), e(4), e(5), ei[0:n_, 1, :])
                step(v.scalar_tensor_tensor(pairs[0:n_, :, 0], e(4), float(P), e(5), ALU.mult, ALU.add))
                step(v.tensor_copy(pairs[0:n_, :, 1], e(3)))
                full = [n_, EC, TILES]
                step(v.tensor_tensor(onehot_t[0:n_, :, :], e(2).unsqueeze(2).to_broadcast(full),
                                     iota_tile[0:n_, :].unsqueeze(1).to_broadcast(full), ALU.is_equal))
                settle()
                v.tensor_reduce(count_pt[0:n_, :], onehot_t[0:n_, :, :].rearrange("p c t -> p t c"), AX.X,
                                ALU.add).then_inc(count_done, 1)
                full = [n_, EC, EC]
                step(v.tensor_tensor(same[0:n_, :, :], e(2).unsqueeze(2).to_broadcast(full),
                                     e(2).unsqueeze(1).to_broadcast(full), ALU.is_equal))
                settle()
                step(v.tensor_tensor(same[0:n_, :, :], same[0:n_, :, :], earlier[0:n_, :, :], ALU.mult))
                settle()
                step(v.tensor_reduce(e(6), same[0:n_, :, :], AX.X, ALU.add))
                v.wait_ge(pl_base, 1)
                step(v.tensor_scalar(base_t[:, 0, :], bank[7][:, 128:128 + TILES], -float(P + 1), 0.0, ALU.add, ALU.max))
                settle()
                step(v.tensor_copy(ov_i[:, 0, :], base_t[:, 0, :]))
                settle()
                step(v.tensor_scalar(ov_i[:, 1, :], ov_i[:, 0, :], 7, None, ALU.arith_shift_right))
                settle()
                step(v.tensor_copy(base_t[:, 1, :], ov_i[:, 1, :]))
                settle()
                step(v.tensor_copy(scan[:, 0, :], base_t[:, 1, :]))
                settle()
                cur, d = 0, 1
                while d < TILES:
                    step(v.tensor_copy(scan[:, 1 - cur, 0:d], scan[:, cur, 0:d]))
                    step(v.tensor_tensor(scan[:, 1 - cur, d:TILES], scan[:, cur, d:TILES],
                                         scan[:, cur, 0:TILES - d], ALU.add))
                    settle()
                    cur, d = 1 - cur, 2 * d
                step(v.memset(ov_start[0:1, :], 0))
                settle()
                v.tensor_copy(ov_start[0:1, 1:TILES + 1], scan[0:1, cur, :]).then_inc(ov_ready, 1)
                step(v.tensor_tensor(base_t[:, 2, :], scan[:, cur, :], base_t[:, 1, :], ALU.subtract))
                assert E < OVMUL and SLOTS * OVMUL < 1 << 24
                settle()
                full = [n_, EC, TILES]
                step(v.scalar_tensor_tensor(base_t[0:n_, 0, :], base_t[0:n_, 2, :], float(OVMUL), bank[7][0:n_, 0:TILES],
                                            ALU.mult, ALU.add))
                settle()
                step(v.tensor_tensor(lookup[0:n_, :, :], onehot_t[0:n_, :, :],
                                     base_t[0:n_, 0, :].unsqueeze(1).to_broadcast(full), ALU.mult))
                settle()
                step(v.tensor_reduce(e(9), lookup[0:n_, :, :], AX.X, ALU.add))
                settle()
                step(v.tensor_copy(ei[0:n_, 0, :], e(9)))
                settle()
                step(v.tensor_scalar(ei[0:n_, 1, :], ei[0:n_, 0, :], OVMUL.bit_length() - 1, None,
                                     ALU.arith_shift_right))
                step(v.tensor_scalar(ei[0:n_, 2, :], ei[0:n_, 0, :], OVMUL - 1, None, ALU.bitwise_and))
                settle()
                step(v.tensor_copy(e(8), ei[0:n_, 1, :]))
                step(v.tensor_copy(e(7), ei[0:n_, 2, :]))
                settle()
                step(v.tensor_tensor(e(6), e(6), e(7), ALU.add))
                settle()
                step(v.tensor_copy(ei[0:n_, 0, :], e(6)))
                settle()
                step(v.tensor_scalar(ei[0:n_, 1, :], ei[0:n_, 0, :], 7, None, ALU.arith_shift_right))
                step(v.tensor_scalar(ei[0:n_, 2, :], ei[0:n_, 0, :], P - 1, None, ALU.bitwise_and))
                settle()
                step(v.tensor_copy(e(0), ei[0:n_, 1, :]))
                step(v.tensor_copy(e(1), ei[0:n_, 2, :]))
                settle()
                step(v.scalar_tensor_tensor(e(7), e(2), -2.0, e(8), ALU.mult, ALU.add))
                step(v.tensor_scalar(e(5), e(0), 2.0, None, ALU.is_ge))
                step(v.scalar_tensor_tensor(e(4), e(2), 2.0, e(0), ALU.mult, ALU.add))
                settle()
                step(v.tensor_scalar(e(7), e(7), float(MAIN - 2), None, ALU.add))
                settle()
                step(v.tensor_tensor(e(7), e(7), e(5), ALU.mult))
                settle()
                step(v.tensor_tensor(e(4), e(4), e(7), ALU.add))
                settle()
                v.scalar_tensor_tensor(slot_idx[0:n_, :], e(1), float(SLOTS), e(4), ALU.mult,
                                       ALU.add).then_inc(placed, 1)
                v.wait_ge(placed, 1)
                v.tensor_copy(e(0), e(1)).then_inc(placed, 1)

                def fold(w_sb, k_all, which, done):
                    for k in range(k_all):
                        for j in range(2):
                            for h in range(HEADS):
                                i = (k * 2 + j) * HEADS + h
                                wait(v, done, i)
                                v.tensor_tensor_reduce(
                                    fold_out[:, :], w_sb[:, k, h * C:(h + 1) * C],
                                    a_bc[:, which + j, h * C:(h + 1) * C], 1.0, 0.0, ALU.mult, ALU.add,
                                    w_sb[:, k, HC + j * HEADS + h:HC + j * HEADS + h + 1]).then_inc(done, 1)

                v.wait_ge(w1_in, 16 * 5)
                fold(w1_raw, KD, 0, fold1)
                v.wait_ge(w2_in, 16 * 3)
                v.wait_ge(fold1, KD * 8)
                fold(w2_raw, KH, 2, fold2)
                v.wait_ge(w1_hi_done, 1)
                v.tensor_tensor(w1_lo[:, :, :], w1_raw[:, :, :], w1_hi[:, :, :].bitcast(F32),
                                ALU.subtract).then_inc(w1_lo_done, 1)

                def statistics(xt, stat, sem_, n):
                    counted = early(v, n + 1)
                    v.bn_stats(stat[:, 0:6], xt).then_inc(sem_, 1)
                    alone(v, sem_, counted)
                    v.bn_aggr(stat[:, 6:8], stat[:, 0:6]).then_inc(sem_, 1)

                def normalised(xt, xn, stat, done):
                    v.tensor_scalar(xn, xt, stat[:, 6:7], stat[:, 8:9], ALU.subtract, ALU.mult).then_inc(done, 1)

                def a_norm(s):
                    v.wait_ge(xa_in[s.u], 16 * s.h + 16)
                    wait(v, xa_turned, s.t - 1)
                    wait(v, xna_ready, s.t)
                    statistics(xa[s.u][:, :], stat_a, a_stats, 10 * s.t)
                    v.wait_ge(a_stats, 10 * s.t + 2)
                    root_steps(v, stat_a, a_stats, 10 * s.t + 2)
                    v.wait_ge(a_stats, 10 * s.t + 10)
                    normalised(xa[s.u][:, :], xna[s.u][:, :], stat_a, xna_ready)

                def low_part(out, turned, high):
                    return v.tensor_tensor(out.rearrange("p k n -> p (k n)"), turned,
                                           high.rearrange("p k n -> p (k n)").bitcast(F32), ALU.subtract)

                def a_low(s):
                    v.wait_ge(xTa_hi, s.t + 1)
                    wait(v, h1_done, s.t - 1)
                    low_part(xTa[s.u][1][:, :, :], bank[s.u][:, :], xTa[s.u][0][:, :, :]).then_inc(xTa_lo, 1)

                def a_evict(s):
                    v.wait_ge(h1_done, s.t + 1)
                    wait(v, stored1[s.u], 16 * s.h)
                    for i, (a, b) in enumerate(thirds):
                        v.tensor_tensor(rowa[s.u][:, a:b], bank[2 + 3 * s.u + i][:, 0:W3], b1_bc[:, a:b],
                                        ALU.add).then_inc(h1_biased, 1)

                a_norm(first(0, 0))
                a_norm(first(0, 1))
                a_low(first(0, 0))

                def a_body(s):
                    if ahead(s, 2):
                        a_norm(ahead(s, 2))
                    if ahead(s, 1):
                        a_low(ahead(s, 1))
                    a_evict(s)

                over_tiles(v, a_body)
                v.wait_ge(meta_in, 16)
                v.tensor_copy(slot_loc[:, :], slot_meta[:, :, 1]).then_inc(meta_ready, 1)
                v.wait_ge(meta_ready, 1)
                total = v.snap(v.value_load(ov_start[0:1, TILES:TILES + 1], min_val=0, max_val=SLOTS - MAIN))

                def al_src(row):
                    return row[:, HC:HC + HEADS]

                def al_dst(row):
                    return row[:, HC + HEADS:ROW]

                def match(s):
                    wait(v, aggregated, s.T - 1)
                    full = [P, 2, P]
                    v.tensor_tensor(OH[s.u][:, :, :], iota_node[:, :].unsqueeze(1).to_broadcast(full),
                                    slot_loc[:, ds(2 * s.t, 2)].unsqueeze(2).to_broadcast(full),
                                    ALU.is_equal).then_inc(onehot, 1)
                    v.wait_ge(onehot, s.T + 1)
                    wait(v, masked, s.T)
                    v.tensor_scalar(NM[:, :, :], OH[s.u][:, :, :].bitcast(F32), BIG, -BIG, ALU.mult,
                                    ALU.add).then_inc(nomatch, 1)

                def maximum(s):
                    counted = early(v, s.T + 1)
                    v.wait_ge(maskedT, s.T + 1)
                    v.tensor_reduce(mx, banks01[:, :, :].rearrange("p c (h e) -> p h c e", h=HEADS), AX.XY,
                                    ALU.max).then_inc(edge_max, 1)
                    alone(v, edge_max, counted)
                    with overflow(v, s, total) as (g, a, b, off):
                        v.wait_ge(ov_in, (a + g + off * 2 + 1) * 16)
                        mask_overflow(g, off, 1)
                        v.wait_ge(ov1_T, g + off + 1)
                        v.tensor_reduce(mxo, bank[0][:, :].rearrange("p (h e) -> p h e", h=HEADS), AX.X,
                                        ALU.max).then_inc(ov1_max, 1)
                        v.wait_ge(ov1_max, (g + off) * 2 + 1)
                        v.tensor_tensor(mx, mx, mxo, ALU.max).then_inc(ov1_max, 1)
                        v.wait_ge(ov1_max, (g + off) * 2 + 2)
                    v.wait_ge(self_in[s.u], 16 * s.TH + 16)
                    als, ald = al_src(H[s.u]), al_dst(H[s.u])
                    v.tensor_tensor(mx, mx, als, ALU.max).then_inc(node_max, 1)
                    v.wait_ge(node_max, s.T + 1)
                    v.tensor_tensor(lsum, mx, ald, ALU.add).then_inc(lgt_sum, 1)
                    v.wait_ge(lgt_sum, s.T + 1)
                    v.tensor_copy(rhs8[:, 0:4], ald).then_inc(shift_ready, 1)
                    v.scalar_tensor_tensor(rhs8[:, 4:8], lsum, SLOPE, lsum, ALU.mult, ALU.max).then_inc(shift_ready, 1)
                    v.tensor_tensor(selfz, als, ald, ALU.add).then_inc(self_logit, 1)
                    v.wait_ge(self_logit, 3 * s.T + 1)
                    v.scalar_tensor_tensor(selfz, selfz, SLOPE, selfz, ALU.mult, ALU.max).then_inc(self_logit, 1)
                    v.wait_ge(self_logit, 3 * s.T + 2)
                    v.wait_ge(shift_ready, 2 * s.T + 2)
                    v.tensor_tensor(selfz, selfz, rhs8[:, 4:8], ALU.subtract).then_inc(self_logit, 1)

                def mask_overflow(g, off, which):
                    v.tensor_tensor(OHo[:, :], iota_node[:, :],
                                    slot_loc[:, ds(g + MAIN, 1)].to_broadcast([P, P]),
                                    ALU.is_equal).then_inc(ov1_dve if which == 1 else ov2_onehot, 1)
                    if which == 1:
                        v.wait_ge(ov1_dve, (g + off) * 2 + 1)
                        v.tensor_scalar(NMo[:, :], OHo[:, :].bitcast(F32), BIG, -BIG, ALU.mult, ALU.add).then_inc(ov1_dve, 1)
                        v.wait_ge(ov1_dve, (g + off) * 2 + 2)
                        full = [P, HEADS, P]
                        v.tensor_tensor(AMo[:, :, :], NMo[:, :].unsqueeze(1).to_broadcast(full),
                                        al_src(GO).unsqueeze(2).to_broadcast(full), ALU.add).then_inc(ov1_masked, 1)

                def logits(zt, als, per_target, sem_, n):
                    v.tensor_tensor(zt, als, per_target[0], ALU.add).then_inc(sem_, 1)
                    v.wait_ge(sem_, n + 1)
                    v.scalar_tensor_tensor(zt, zt, SLOPE, zt, ALU.mult, ALU.max).then_inc(sem_, 1)
                    v.wait_ge(sem_, n + 2)
                    v.tensor_tensor(zt, zt, per_target[1], ALU.subtract).then_inc(sem_, 1)
                    v.wait_ge(sem_, n + 3)
                    v.tensor_scalar(zt, zt, 0.0, None, ALU.min).then_inc(sem_, 1)

                def edge_logits(s):
                    v.wait_ge(edge_rhs, s.T + 1)
                    logits(z, G[s.u][:, :, HC:HC + HEADS], (edge_ps[:, :, 0:4], edge_ps[:, :, 4:8]), edge_logit, 4 * s.T)

                def scale_low(s, chunks=range(2)):
                    v.wait_ge(edge_weight, s.T + 1)
                    wait(v, aggregated, s.T)
                    for c in chunks:
                        for h in range(HEADS):
                            cols = slice(h * C, (h + 1) * C)
                            v.wait_ge(scaled_hi, 8 * s.T + 4 * c + h + 1)
                            v.scalar_tensor_tensor(GS[1][:, c, cols], G[s.u][:, c, cols], w[:, c, h:h + 1],
                                                   GS[0][:, c, cols].bitcast(F32), ALU.mult,
                                                   ALU.subtract).then_inc((scaled_lo0, scaled_lo1)[c], 1)

                def mean_weights(s):
                    counted = early(v, s.T + 1)
                    v.wait_ge(den_done, s.T + 1)
                    v.wait_ge(self_weight, s.T + 1)
                    v.tensor_tensor(dsum, den_ps, wself, ALU.add).then_inc(den_total, 1)
                    alone(v, den_total, counted)
                    with overflow(v, s, total) as (g, a, b, off):
                        v.wait_ge(ov_in, (b + g + off * 2 + 1) * 16)
                        mask_overflow(g, off, 2)
                        v.wait_ge(ov2_T, g + off + 1)
                        v.tensor_copy(ohTo[:, :], ohT_o_ps).then_inc(ov2_copied, 1)
                        v.wait_ge(ov2_rhs, g + off + 1)
                        logits(zo, al_src(GO), (edge_o_ps[:, 0:4], edge_o_ps[:, 4:8]), ov2_logit, (g + off) * 4)
                        v.wait_ge(ov2_weight, g + off + 1)
                        v.wait_ge(aggregated, s.T + 1)
                        for h in range(HEADS):
                            cols = slice(h * C, (h + 1) * C)
                            v.wait_ge(ov2_hi, (g + off) * 4 + h + 1)
                            v.scalar_tensor_tensor(GS[1][:, 0, cols], GO[:, cols], wo[:, h:h + 1],
                                                   GS[0][:, 0, cols].bitcast(F32), ALU.mult,
                                                   ALU.subtract).then_inc(ov2_lo, 1)
                        v.wait_ge(ov2_agg, g + off + 2)
                        v.tensor_tensor(dsum, dsum, den_o_ps, ALU.add).then_inc(ov2_den, 1)
                        v.wait_ge(ov2_den, g + off + 1)
                    v.reciprocal(rden, dsum).then_inc(den_inv, 1)
                    v.wait_ge(den_inv, s.T + 1)
                    wait(v, self_scaled, 4 * s.T)
                    v.tensor_tensor(wsn, wself, rden, ALU.mult).then_inc(self_scale, 1)

                def mix(s):
                    v.wait_ge(aggregated, s.T + 1)
                    for h in range(HEADS):
                        cols = slice(h * C, (h + 1) * C)
                        v.wait_ge(self_scaled, 4 * s.T + h + 1)
                        v.scalar_tensor_tensor(mixed[:, cols], bank[3 + h // 2][:, (h % 2) * C:(h % 2 + 1) * C],
                                               rden[:, h:h + 1], mixed[:, cols], ALU.mult, ALU.add).then_inc(mix_done, 1)

                def relu_low(s):
                    for half in range(2):
                        v.wait_ge(relu_hi, 2 * s.T + 1 + half)
                        ks = slice(4 * half, 4 * half + 4)
                        v.scalar_tensor_tensor(hT[s.u][1][:, ks, :].rearrange("p k n -> p (k n)"), bank[3 + half][:, :], 0.0,
                                               hT[s.u][0][:, ks, :].rearrange("p k n -> p (k n)").bitcast(F32), ALU.max,
                                               ALU.subtract).then_inc(relu_lo, 1)

                def prepare(phase):
                    s0, s1 = phase_tile(first(0, 0), phase), phase_tile(first(0, 1), phase)
                    match(s0)
                    maximum(s0)
                    edge_logits(s0)
                    match(s1)
                    scale_low(s0)
                    mean_weights(s0)
                    mix(s0)
                    match(phase_tile(first(1, 0), phase))
                    maximum(s1)
                    relu_low(s0)
                    edge_logits(s1)
                    scale_low(s1)

                prepare(0)

                def b_body(t):
                    s, n, m, l = (phase_tile(x, 0) for x in (t, ahead(t, 1), ahead(t, 2), ahead(t, 3)))
                    if n:
                        mean_weights(n)
                        mix(n)
                    if m:
                        maximum(m)
                    if n:
                        relu_low(n)
                    v.wait_ge(dense_done, 3 * s.t + 3)
                    wait(v, stored2[s.u], 16 * s.h)
                    v.tensor_tensor(rowb[s.u][:, 2 * W3:ROW], bank[7][:, 0:W3], b2_bc[:, 2 * W3:ROW],
                                    ALU.add).then_inc(h2_dve, 1)
                    if m:
                        edge_logits(m)
                    if l:
                        match(l)
                    if m:
                        scale_low(m)

                over_tiles(v, b_body)

                for i, (lo, raw, hi) in enumerate(((wfc_lo, wfc_raw, wfc_hi), (f1_lo, f1_raw, f1_hi),
                                                   (f2_lo, f2_raw, f2_hi))):
                    v.wait_ge(wc_hi_done, i + 1)
                    v.tensor_tensor(lo[:, :, :], raw[:, :, :], hi[:, :, :].bitcast(F32),
                                    ALU.subtract).then_inc(wc_lo_done, 1)
                v.wait_ge(fb2_sum, 1)
                v.tensor_scalar(fb2_twice[:, :], bank[7][:, :], 2.0, None, ALU.mult).then_inc(c_const, 1)
                v.wait_ge(c_const, 1)
                prepare(1)

                def gelu_sum(s):
                    v.wait_ge(gelu_done, s.t + 1)
                    v.tensor_tensor(gsum[:, :], ffn_v[:, 0, :], ffn_v[:, 1, :], ALU.add).then_inc(gsum_done, 1)

                def gelu_low(s):
                    v.wait_ge(gT_hi, s.t + 1)
                    low_part(gT[1][:, :, :], bank[7][:, :], gT[0][:, :, :]).then_inc(gT_lo, 1)

                def finish_tile(s):
                    v.wait_ge(f2_done, s.t + 1)
                    v.wait_ge(x2_biased, s.t + 1)
                    wait(v, out_stored[s.u], 16 * s.h)
                    v.tensor_tensor(outb[s.u][:, :], bank[6][:, :], x2[s.u][:, :], ALU.add).then_inc(out_sum, 1)

                def gate(s):
                    alone(v, f1_done, s.t + 1)
                    v.max(m8, gate_ps).then_inc(c_top, 1)
                    v.wait_ge(c_top, 2 * s.t + 1)
                    v.tensor_scalar(nmax, m8[:, 0:1], -1.0, None, ALU.mult).then_inc(c_top, 1)
                    v.wait_ge(c_exp, s.t + 1)
                    v.reciprocal(rsum, esum).then_inc(c_prob, 1)
                    v.wait_ge(c_prob, 5 * s.t + 1)
                    v.tensor_scalar(e8, e8, rsum, None, ALU.mult).then_inc(c_prob, 1)
                    v.wait_ge(c_prob, 5 * s.t + 2)
                    v.tensor_tensor(s2, e8[:, 0:1], e8[:, 1:2], ALU.add).then_inc(c_prob, 1)
                    v.wait_ge(c_prob, 5 * s.t + 3)
                    v.reciprocal(s2, s2).then_inc(c_prob, 1)
                    v.wait_ge(c_prob, 5 * s.t + 4)
                    v.tensor_scalar(p2, e8[:, 0:2], s2, None, ALU.mult).then_inc(c_prob, 1)
                    v.wait_ge(c_prob, 5 * s.t + 5)

                def ffn_inner(s):
                    for i in range(2):
                        for b, a, z_ in ((6, 0, F2W), (7, F2W, FF)):
                            v.scalar_tensor_tensor(ffn_v[:, i, a:z_], bank[b][:, 0:z_ - a], p2[:, i:i + 1],
                                                   fb1_bc[:, a:z_], ALU.mult, ALU.add).then_inc(ffn_in, 1)

                def c_body(t):
                    s, n, m, l = (phase_tile(x, 1) for x in (t, ahead(t, 1), ahead(t, 2), ahead(t, 3)))
                    if n:
                        mean_weights(n)
                    if not is_zero(t.t):
                        gelu_sum(ahead(t, -1))
                    v.wait_ge(fc_done, s.t + 1)
                    v.wait_ge(x_biased, s.t + 1)
                    v.tensor_tensor(x2[s.u][:, :], bank[5][:, :], xc[s.u][:, :], ALU.add).then_inc(c_x2, 1)
                    v.wait_ge(c_x2, s.t + 1)
                    statistics(x2[s.u][:, :], stat_c, c_stats, 2 * s.t)
                    if not is_zero(t.t):
                        gelu_low(ahead(t, -1))
                    if n:
                        mix(n)
                    if m:
                        maximum(m)
                    v.wait_ge(c_root, 8 * s.t + 8)
                    normalised(x2[s.u][:, :], xn2[:, :], stat_c, c_xn)
                    if not is_zero(t.t):
                        finish_tile(ahead(t, -1))
                    v.wait_ge(xT2_hi, s.t + 1)
                    low_part(xT2[1][:, :, :], bank[5][:, :], xT2[0][:, :, :]).then_inc(xT2_lo, 1)
                    if m:
                        edge_logits(m)
                    if n:
                        relu_low(n)
                    if m:
                        scale_low(m, range(1))
                    gate(s)
                    ffn_inner(s)
                    if l:
                        match(l)

                over_tiles(v, c_body)
                gelu_sum(first(HALF - 1, 1))
                gelu_low(first(HALF - 1, 1))
                finish_tile(first(HALF - 1, 1))

            @block.scalar
            def _(act):
                def high_part(out, turned):
                    return act.copy(out.rearrange("p k n -> p (k n)"), turned)

                def turned(s):
                    act.wait_ge(xa_turned, s.t + 1)
                    wait(act, h1_done, s.t - 1)
                    high_part(xTa[s.u][0][:, :, :], bank[s.u][:, :]).then_inc(xTa_hi, 1)

                def a_body(s):
                    if ahead(s, 1):
                        turned(ahead(s, 1))

                act.wait_ge(fold1, KD * 8)
                act.copy(w1_hi[:, :, :].rearrange("p k n -> p (k n)"),
                         w1_raw[:, :, :].rearrange("p k n -> p (k n)")).then_inc(w1_hi_done, 1)
                turned(first(0, 0))
                over_tiles(act, a_body)
                act.wait_ge(ov_ready, 1)
                act.wait_ge(cleared, 1)
                total = act.snap(act.value_load(ov_start[0:1, TILES:TILES + 1], min_val=0, max_val=SLOTS - MAIN))

                def spread(s):
                    act.wait_ge(onehotT, s.T + 1)
                    act.copy(ohT[:, :, :].rearrange("p c e -> p (c e)"), small[:, 0:256]).then_inc(onehotT_copied, 1)

                def weigh_self(s):
                    act.wait_ge(self_logit, 3 * s.T + 3)
                    act.activation(wself, selfz, ACT.Exp).then_inc(self_weight, 1)

                def weigh(s):
                    act.wait_ge(edge_logit, 4 * s.T + 4)
                    act.activation(w, z, ACT.Exp).then_inc(edge_weight, 1)

                def scale_high(s):
                    act.wait_ge(edge_weight, s.T + 1)
                    wait(act, aggregated, s.T)
                    for c in range(2):
                        for h in range(HEADS):
                            cols = slice(h * C, (h + 1) * C)
                            act.activation(GS[0][:, c, cols], G[s.u][:, c, cols], ACT.Copy,
                                           scale=w[:, c, h:h + 1]).then_inc(scaled_hi, 1)

                def weigh_overflow(s):
                    with overflow(act, s, total) as (g, a, b, off):
                        act.wait_ge(ov2_logit, (g + off) * 4 + 4)
                        act.activation(wo, zo, ACT.Exp).then_inc(ov2_weight, 1)
                        act.wait_ge(ov2_weight, g + off + 1)
                        act.wait_ge(aggregated, s.T + 1)
                        act.wait_ge(ov2_agg, g + off + 1)
                        for h in range(HEADS):
                            cols = slice(h * C, (h + 1) * C)
                            act.activation(GS[0][:, 0, cols], GO[:, cols], ACT.Copy,
                                           scale=wo[:, h:h + 1]).then_inc(ov2_hi, 1)

                def scale_self(s, heads=range(HEADS)):
                    if heads[0] == 0:
                        wait(act, mixedT, 2 * s.T)
                        act.wait_ge(self_scale, s.T + 1)
                    for h in heads:
                        cols = slice(h * C, (h + 1) * C)
                        act.activation(mixed[:, cols], H[s.u][:, cols], ACT.Copy,
                                       scale=wsn[:, h:h + 1]).then_inc(self_scaled, 1)

                def relu(s):
                    for half in range(2):
                        act.wait_ge(mixedT, 2 * s.T + 1 + half)
                        act.activation(hT[s.u][0][:, 4 * half:4 * half + 4, :].rearrange("p k n -> p (k n)"),
                                       bank[3 + half][:, :], ACT.Relu).then_inc(relu_hi, 1)

                def prepare(phase):
                    s0, s1 = phase_tile(first(0, 0), phase), phase_tile(first(0, 1), phase)
                    spread(s0)
                    weigh_self(s0)
                    weigh(s0)
                    scale_high(s0)
                    weigh_overflow(s0)
                    scale_self(s0)
                    spread(s1)
                    weigh_self(s1)
                    relu(s0)
                    weigh(s1)
                    scale_high(s1)

                prepare(0)

                def b_body(t):
                    s, n, m = (phase_tile(x, 0) for x in (t, ahead(t, 1), ahead(t, 2)))
                    if n:
                        weigh_overflow(n)
                        scale_self(n)
                    if m:
                        spread(m)
                    if n:
                        relu(n)
                    if m:
                        weigh_self(m)
                    wait(act, stored2[s.u], 16 * s.h)
                    for i in range(2):
                        act.wait_ge(dense_done, 3 * s.t + i + 1)
                        act.copy(rowb[s.u][:, i * W3:(i + 1) * W3], bank[5 + i][:, 0:W3]).then_inc(h2_act, 1)
                    if m:
                        weigh(m)
                        scale_high(m)

                over_tiles(act, b_body)

                act.wait_ge(wc_in, WC_LOADS)
                act.wait_ge(dense_done, 3 * TILES)
                for hi, raw in ((wfc_hi, wfc_raw), (f1_hi, f1_raw), (f2_hi, f2_raw)):
                    act.copy(hi[:, :, :].rearrange("p k n -> p (k n)"),
                             raw[:, :, :].rearrange("p k n -> p (k n)")).then_inc(wc_hi_done, 1)
                prepare(1)

                def turned_gelu(s):
                    act.wait_ge(c_gT, s.t + 1)
                    high_part(gT[0][:, :, :], bank[7][:, :]).then_inc(gT_hi, 1)

                def c_body(t):
                    s, n, m = (phase_tile(x, 1) for x in (t, ahead(t, 1), ahead(t, 2)))
                    if n:
                        weigh_overflow(n)
                        scale_self(n, range(0, 1))
                    if not is_zero(t.t):
                        turned_gelu(ahead(t, -1))
                    if n:
                        scale_self(n, range(1, HEADS))
                    if m:
                        spread(m)
                        weigh_self(m)
                    act.wait_ge(c_xT, s.t + 1)
                    high_part(xT2[0][:, :, :], bank[5][:, :]).then_inc(xT2_hi, 1)
                    if n:
                        relu(n)
                    if m:
                        weigh(m)
                        scale_high(m)
                    act.wait_ge(c_top, 2 * s.t + 2)
                    act.activation(e8, m8, ACT.Exp, bias=nmax, accum_out=esum).then_inc(c_exp, 1)
                    act.wait_ge(ffn_in, 4 * s.t + 4)
                    flat = ffn_v[:, :, :].rearrange("p i f -> p (i f)")
                    act.activation(flat, flat, ACT.Gelu).then_inc(gelu_done, 1)

                over_tiles(act, c_body)
                turned_gelu(first(HALF - 1, 1))


_INS = ['x', 'src', 'dst', 'L0_gnn_W1', 'L0_gnn_a_src1', 'L0_gnn_a_dst1', 'L0_gnn_b1', 'L0_gnn_W2', 'L0_gnn_a_src2',
        'L0_gnn_a_dst2', 'L0_gnn_b2', 'L0_gnn_Wfc', 'L0_gnn_bfc', 'L0_ffn_Wg', 'L0_ffn_W1', 'L0_ffn_b1', 'L0_ffn_W2',
        'L0_ffn_b2']


def kernel(**inputs):
    import numpy as np
    import concourse.bacc as bacc
    from concourse.bass_utils import run_bass_kernel_spmd

    nc = bacc.Bacc("TRN2", target_bir_lowering=False, num_devices=1)
    arrays, args = {}, []
    for name in _INS:
        a = np.ascontiguousarray(inputs[name])
        arrays[f"in_{name}"] = a
        args.append(nc.dram_tensor(f"in_{name}", a.shape, mybir.dt.from_np(a.dtype), kind="ExternalInput").ap())
    args.append(nc.dram_tensor("out", arrays["in_x"].shape, F32, kind="ExternalOutput").ap())
    gnn_ffn_kernel(nc, *args)
    r = run_bass_kernel_spmd(nc, [arrays], core_ids=[0])
    return r.results[0]["out"]
```
